# Optimizing a Trainium2 kernel written in Bass

```python
import numpy as np
import jax
import jax.numpy as jnp

def _softmax(x, axis=-1):
    return jax.nn.softmax(x, axis=axis)

def _gelu(x):
    return jax.nn.gelu(x, approximate=True)

def _silu(x):
    return jax.nn.silu(x)

def _sigmoid(x):
    return jax.nn.sigmoid(x)

def _layernorm(x, axis=-1, eps=1e-05):
    m = jnp.mean(x, axis=axis, keepdims=True)
    v = jnp.var(x, axis=axis, keepdims=True)
    return (x - m) / jnp.sqrt(v + eps)

def _scatter_add(tgt, idx, src, axis=0):
    return tgt.at[idx].add(src)

def _segment_sum(src, seg, n):
    return jax.ops.segment_sum(src, seg, n)
kernel_name = 'mk_xattn_ffn_d2_seqx_r4_b0755d'

def setup_inputs(seed: int=0):
    np.random.seed(seed)
    _w = jnp.asarray

    def _rec_inputs():
        import jax
        import jax.numpy as jnp
        _rk = jax.random.key(seed)
        x = -0.0002928 + 1 * jax.random.normal(jax.random.fold_in(_rk, 1), (64, 128, 256), jnp.float32)
        _lenS = 128 - jax.random.randint(jax.random.fold_in(_rk, 7), (64,), 0, max(1, 128 // 4) + 1, jnp.int32)
        _lenS2 = 128 - jax.random.randint(jax.random.fold_in(_rk, 8), (64,), 0, max(1, 128 // 4) + 1, jnp.int32)
        _ctx_1024P = jax.random.normal(jax.random.fold_in(_rk, 11), (64, 16, 256), jnp.float32)
        _ctx_1024c = jax.random.dirichlet(jax.random.fold_in(_rk, 511), 0.3 * jnp.ones((16,), jnp.float32), (64, 128))
        _ctx_1024t = jnp.einsum('bsk,bkd->bsd', _ctx_1024c, _ctx_1024P)
        _ctx_1024t = _ctx_1024t * jax.lax.rsqrt(jnp.mean(jnp.square(_ctx_1024t)) + 1e-12) * 0.953939
        ctx_1024 = -1.39393e-06 + 0.999914 * (_ctx_1024t + 0.3 * jax.random.normal(jax.random.fold_in(_rk, 611), (64, 128, 256), jnp.float32))
        _validS = jnp.arange(128)[None, :] < _lenS[:, None]
        _validS2 = jnp.arange(128)[None, :] < _lenS2[:, None]
        _causal = jnp.tril(jnp.ones((128, 128), dtype=bool))
        mask_Bx1x1xS2_if1 = jnp.where(jnp.ones((64, 1, 1, 128), dtype=bool), 1, 0).astype(jnp.int32)
        return (x, ctx_1024, mask_Bx1x1xS2_if1)
    x, ctx_1024, mask_Bx1x1xS2_if1 = _rec_inputs()

    def _L0_xattn_setup():
        import jax, jax.numpy as jnp
        import numpy as np
        SCALE_BASE = 512.0
        GN_EPS = 1e-05

        def _xpos(x, downscale):
            L, D = (x.shape[-2], x.shape[-1])
            half = D // 2
            base = (jnp.arange(0, D, 2, dtype=jnp.float32) + 0.4 * D) / (1.4 * D)
            min_pos = -(L // 2)
            power = (jnp.arange(min_pos, min_pos + L, dtype=jnp.float32) / SCALE_BASE)[:, None]
            scale = base[None, :] ** power
            inv_freq = 1.0 / 10000.0 ** (jnp.arange(half, dtype=jnp.float32) / half)
            ang = jnp.arange(L, dtype=jnp.float32)[:, None] * inv_freq[None, :]
            sin, cos = (jnp.sin(ang), jnp.cos(ang))
            if downscale:
                scale = 1.0 / scale
            sin_s = jnp.repeat(sin * scale, 2, axis=-1)
            cos_s = jnp.repeat(cos * scale, 2, axis=-1)
            x1, x2 = (x[..., ::2], x[..., 1::2])
            rot = jnp.stack((-x2, x1), axis=-1).reshape(x.shape)
            return x * cos_s + rot * sin_s

        def _decay_mask(L, H):
            gammas = 1.0 - jnp.exp(jnp.linspace(np.log(1.0 / 32.0), np.log(1.0 / 512.0), H)).astype(jnp.float32)
            idx = jnp.arange(L)
            dist = idx[:, None] - idx[None, :]
            causal = dist >= 0
            d = jnp.maximum(dist, 0).astype(jnp.float32)
            return jnp.where(causal[None], gammas[:, None, None] ** d[None], 0.0)
        key = jax.random.key(seed)
        ks = jax.random.split(key, 9)
        B, L, D, H = (2, 512, 256, 16)
        hd = D // H
        return {'query': jax.random.normal(ks[0], (B, L, D), jnp.float32), 'key': jax.random.normal(ks[1], (B, L, D), jnp.float32), 'value': jax.random.normal(ks[2], (B, L, D), jnp.float32), 'W_Q': jax.random.normal(ks[3], (H, D, hd), jnp.float32) / D, 'W_K': jax.random.normal(ks[4], (H, D, hd), jnp.float32) / D, 'W_V': jax.random.normal(ks[5], (H, D, hd), jnp.float32) / D, 'g_w': jax.random.normal(ks[6], (D, D), jnp.float32) * (2.0 / (D + D)) ** 0.5, 'g_b': jnp.zeros((D,), jnp.float32), 'out_w': jax.random.normal(ks[7], (D, D), jnp.float32) * (2.0 / (D + D)) ** 0.5, 'out_b': jnp.zeros((D,), jnp.float32)}
    _L0_xattn_all = _L0_xattn_setup()
    _L0_xattn_in = {k: v for k, v in _L0_xattn_all.items() if k in ('W_Q', 'W_K', 'W_V', 'g_w', 'g_b', 'out_w', 'out_b')}
    del _L0_xattn_all

    def _L0_ffn_setup():
        import jax, jax.numpy as jnp
        import numpy as np
        DIM = 256

        def _reference_tuple_inner(x, W_r, W_k, W_v, mu_r, mu_k):
            B, T, C = x.shape
            x_prev = jnp.concatenate([jnp.zeros((B, 1, C), x.dtype), x[:, :-1, :]], axis=1)
            xr = mu_r * x + (1.0 - mu_r) * x_prev
            xk = mu_k * x + (1.0 - mu_k) * x_prev
            r = jax.nn.sigmoid(jnp.einsum('btc,dc->btd', xr, W_r))
            k = jnp.einsum('btc,dc->btd', xk, W_k)
            k_act = jnp.square(jax.nn.relu(k))
            out = r * jnp.einsum('btc,dc->btd', k_act, W_v)
            new_state = x[:, -1, :]
            return (out, new_state)
        key = jax.random.key(seed)
        ks = jax.random.split(key, 6)
        B, T, C = (8, 512, DIM)
        x = jax.random.normal(ks[0], (B, T, C), dtype=jnp.float32)
        s = 1.0 / np.sqrt(C)
        W_r = jax.random.uniform(ks[1], (C, C), jnp.float32, -s, s)
        W_k = jax.random.uniform(ks[2], (C, C), jnp.float32, -s, s)
        W_v = jax.random.uniform(ks[3], (C, C), jnp.float32, -s, s)
        mu_r = jax.random.uniform(ks[4], (C,), jnp.float32)
        mu_k = jax.random.uniform(ks[5], (C,), jnp.float32)
        return {'x': x, 'W_r': W_r, 'W_k': W_k, 'W_v': W_v, 'mu_r': mu_r, 'mu_k': mu_k}
    _L0_ffn_all = _L0_ffn_setup()
    _L0_ffn_in = {k: v for k, v in _L0_ffn_all.items() if k in ('W_r', 'W_k', 'W_v', 'mu_r', 'mu_k')}
    del _L0_ffn_all

    def _L1_xattn_setup():
        import jax, jax.numpy as jnp
        import numpy as np
        D_MODEL = 256
        N_HEADS = 16
        D_K = D_MODEL // N_HEADS
        NEG = -1000000000.0

        def _split_heads(x):
            B, S, _ = x.shape
            return x.reshape(B, S, N_HEADS, D_K).transpose(0, 2, 1, 3)
        key = jax.random.key(seed)
        ks = jax.random.split(key, 12)
        B, S, D = (2, 512, D_MODEL)
        s = 1.0 / np.sqrt(D)
        inp = {'query': jax.random.normal(ks[0], (B, S, D), jnp.float32), 'key': jax.random.normal(ks[1], (B, S, D), jnp.float32), 'value': jax.random.normal(ks[2], (B, S, D), jnp.float32), 'mask': jnp.ones((B, 1, 1, S), jnp.int32), 'Wq': jax.random.normal(ks[3], (D, D), jnp.float32) * s, 'bq': jax.random.normal(ks[4], (D,), jnp.float32) * s, 'Wk': jax.random.normal(ks[5], (D, D), jnp.float32) * s, 'bk': jax.random.normal(ks[6], (D,), jnp.float32) * s, 'Wv': jax.random.normal(ks[7], (D, D), jnp.float32) * s, 'bv': jax.random.normal(ks[8], (D,), jnp.float32) * s, 'Wo': jax.random.normal(ks[9], (D, D), jnp.float32) * s, 'bo': jax.random.normal(ks[10], (D,), jnp.float32) * s}
        return inp
    _L1_xattn_all = _L1_xattn_setup()
    _L1_xattn_in = {k: v for k, v in _L1_xattn_all.items() if k in ('Wq', 'bq', 'Wk', 'bk', 'Wv', 'bv', 'Wo', 'bo')}
    del _L1_xattn_all

    def _L1_ffn_setup():
        import jax, jax.numpy as jnp
        import numpy as np
        DIM = 256
        HIDDEN = 768
        SCALE = 1.0 / 127.0

        def _dequant(w_int, dtype):
            return w_int.astype(dtype) * jnp.asarray(SCALE, dtype)
        key = jax.random.key(seed)
        k_x, k_g, k_u, k_d = jax.random.split(key, 4)
        x = jax.random.normal(k_x, (4, 512, DIM), dtype=jnp.float32)
        w_gate = jax.random.randint(k_g, (HIDDEN, DIM), -127, 128, dtype=jnp.int32)
        w_up = jax.random.randint(k_u, (HIDDEN, DIM), -127, 128, dtype=jnp.int32)
        w_down = jax.random.randint(k_d, (DIM, HIDDEN), -127, 128, dtype=jnp.int32)
        return {'x': x, 'w_gate': w_gate, 'w_up': w_up, 'w_down': w_down}
    _L1_ffn_all = _L1_ffn_setup()
    _L1_ffn_in = {k: v for k, v in _L1_ffn_all.items() if k in ('w_gate', 'w_up', 'w_down')}
    del _L1_ffn_all
    return {'x': x, 'ctx_1024': ctx_1024, 'mask_Bx1x1xS2_if1': mask_Bx1x1xS2_if1, 'L0_xattn_W_Q': _L0_xattn_in['W_Q'], 'L0_xattn_W_K': _L0_xattn_in['W_K'], 'L0_xattn_W_V': _L0_xattn_in['W_V'], 'L0_xattn_g_w': _L0_xattn_in['g_w'], 'L0_xattn_g_b': _L0_xattn_in['g_b'], 'L0_xattn_out_w': _L0_xattn_in['out_w'], 'L0_xattn_out_b': _L0_xattn_in['out_b'], 'L0_ffn_W_r': _L0_ffn_in['W_r'], 'L0_ffn_W_k': _L0_ffn_in['W_k'], 'L0_ffn_W_v': _L0_ffn_in['W_v'], 'L0_ffn_mu_r': _L0_ffn_in['mu_r'], 'L0_ffn_mu_k': _L0_ffn_in['mu_k'], 'L1_xattn_Wq': _L1_xattn_in['Wq'], 'L1_xattn_bq': _L1_xattn_in['bq'], 'L1_xattn_Wk': _L1_xattn_in['Wk'], 'L1_xattn_bk': _L1_xattn_in['bk'], 'L1_xattn_Wv': _L1_xattn_in['Wv'], 'L1_xattn_bv': _L1_xattn_in['bv'], 'L1_xattn_Wo': _L1_xattn_in['Wo'], 'L1_xattn_bo': _L1_xattn_in['bo'], 'L1_ffn_w_gate': _L1_ffn_in['w_gate'], 'L1_ffn_w_up': _L1_ffn_in['w_up'], 'L1_ffn_w_down': _L1_ffn_in['w_down']}

def reference(x, ctx_1024, mask_Bx1x1xS2_if1, L0_xattn_W_Q, L0_xattn_W_K, L0_xattn_W_V, L0_xattn_g_w, L0_xattn_g_b, L0_xattn_out_w, L0_xattn_out_b, L0_ffn_W_r, L0_ffn_W_k, L0_ffn_W_v, L0_ffn_mu_r, L0_ffn_mu_k, L1_xattn_Wq, L1_xattn_bq, L1_xattn_Wk, L1_xattn_bk, L1_xattn_Wv, L1_xattn_bv, L1_xattn_Wo, L1_xattn_bo, L1_ffn_w_gate, L1_ffn_w_up, L1_ffn_w_down):
    import jax
    import jax.numpy as jnp

    def _L0_xattn_ref(query, key, value, W_Q, W_K, W_V, g_w, g_b, out_w, out_b):
        import jax, jax.numpy as jnp
        import numpy as np
        SCALE_BASE = 512.0
        GN_EPS = 1e-05

        def _xpos(x, downscale):
            L, D = (x.shape[-2], x.shape[-1])
            half = D // 2
            base = (jnp.arange(0, D, 2, dtype=jnp.float32) + 0.4 * D) / (1.4 * D)
            min_pos = -(L // 2)
            power = (jnp.arange(min_pos, min_pos + L, dtype=jnp.float32) / SCALE_BASE)[:, None]
            scale = base[None, :] ** power
            inv_freq = 1.0 / 10000.0 ** (jnp.arange(half, dtype=jnp.float32) / half)
            ang = jnp.arange(L, dtype=jnp.float32)[:, None] * inv_freq[None, :]
            sin, cos = (jnp.sin(ang), jnp.cos(ang))
            if downscale:
                scale = 1.0 / scale
            sin_s = jnp.repeat(sin * scale, 2, axis=-1)
            cos_s = jnp.repeat(cos * scale, 2, axis=-1)
            x1, x2 = (x[..., ::2], x[..., 1::2])
            rot = jnp.stack((-x2, x1), axis=-1).reshape(x.shape)
            return x * cos_s + rot * sin_s

        def _decay_mask(L, H):
            gammas = 1.0 - jnp.exp(jnp.linspace(np.log(1.0 / 32.0), np.log(1.0 / 512.0), H)).astype(jnp.float32)
            idx = jnp.arange(L)
            dist = idx[:, None] - idx[None, :]
            causal = dist >= 0
            d = jnp.maximum(dist, 0).astype(jnp.float32)
            return jnp.where(causal[None], gammas[:, None, None] ** d[None], 0.0)
        B, L, D = query.shape
        H = W_Q.shape[0]
        q = jnp.einsum('bld,hde->bhle', query, W_Q)
        k = jnp.einsum('bld,hde->bhle', key, W_K)
        v = jnp.einsum('bld,hde->bhle', value, W_V)
        q = _xpos(q, downscale=False)
        k = _xpos(k, downscale=True)
        sim = jnp.einsum('bhnd,bhsd->bhns', q, k) * _decay_mask(L, H)[None]
        ret = jnp.einsum('bhns,bhsd->bhnd', sim, v)
        mu = ret.mean(axis=-1, keepdims=True)
        var = ret.var(axis=-1, keepdims=True)
        ret = (ret - mu) / jnp.sqrt(var + GN_EPS)
        ret = ret.transpose(0, 2, 1, 3).reshape(B, L, D)
        gate = jax.nn.silu(query @ g_w.T + g_b)
        return ret * gate @ out_w.T + out_b

    def _L0_ffn_ref(x, W_r, W_k, W_v, mu_r, mu_k):
        import jax, jax.numpy as jnp
        import numpy as np
        DIM = 256

        def _reference_tuple_inner(x, W_r, W_k, W_v, mu_r, mu_k):
            B, T, C = x.shape
            x_prev = jnp.concatenate([jnp.zeros((B, 1, C), x.dtype), x[:, :-1, :]], axis=1)
            xr = mu_r * x + (1.0 - mu_r) * x_prev
            xk = mu_k * x + (1.0 - mu_k) * x_prev
            r = jax.nn.sigmoid(jnp.einsum('btc,dc->btd', xr, W_r))
            k = jnp.einsum('btc,dc->btd', xk, W_k)
            k_act = jnp.square(jax.nn.relu(k))
            out = r * jnp.einsum('btc,dc->btd', k_act, W_v)
            new_state = x[:, -1, :]
            return (out, new_state)
        return _reference_tuple_inner(x, W_r, W_k, W_v, mu_r, mu_k)[0]

    def _L1_xattn_ref(query, key, value, mask, Wq, bq, Wk, bk, Wv, bv, Wo, bo):
        import jax, jax.numpy as jnp
        import numpy as np
        D_MODEL = 256
        N_HEADS = 16
        D_K = D_MODEL // N_HEADS
        NEG = -1000000000.0

        def _split_heads(x):
            B, S, _ = x.shape
            return x.reshape(B, S, N_HEADS, D_K).transpose(0, 2, 1, 3)
        Q = _split_heads(query @ Wq.T + bq)
        K = _split_heads(key @ Wk.T + bk)
        V = _split_heads(value @ Wv.T + bv)
        scores = jnp.einsum('bhqd,bhkd->bhqk', Q, K) / np.sqrt(D_K).astype(np.float32)
        scores = jnp.where(mask == 0, jnp.float32(NEG), scores)
        attn = jax.nn.softmax(scores, axis=-1)
        out = jnp.einsum('bhqk,bhkd->bhqd', attn, V)
        B, H, S, dk = out.shape
        out = out.transpose(0, 2, 1, 3).reshape(B, S, H * dk)
        return out @ Wo.T + bo

    def _L1_ffn_ref(x, w_gate, w_up, w_down):
        import jax, jax.numpy as jnp
        import numpy as np
        DIM = 256
        HIDDEN = 768
        SCALE = 1.0 / 127.0

        def _dequant(w_int, dtype):
            return w_int.astype(dtype) * jnp.asarray(SCALE, dtype)
        wg = _dequant(w_gate, x.dtype)
        wu = _dequant(w_up, x.dtype)
        wd = _dequant(w_down, x.dtype)
        gate = jnp.einsum('bsd,hd->bsh', x, wg)
        up = jnp.einsum('bsd,hd->bsh', x, wu)
        h = jax.nn.silu(gate) * up
        return jnp.einsum('bsh,dh->bsd', h, wd)
    x = x + _L0_xattn_ref(_layernorm(x, axis=-1), ctx_1024, ctx_1024, L0_xattn_W_Q, L0_xattn_W_K, L0_xattn_W_V, L0_xattn_g_w, L0_xattn_g_b, L0_xattn_out_w, L0_xattn_out_b)
    x = x + _L0_ffn_ref(_layernorm(x, axis=-1), L0_ffn_W_r, L0_ffn_W_k, L0_ffn_W_v, L0_ffn_mu_r, L0_ffn_mu_k)
    x = x + _L1_xattn_ref(_layernorm(x, axis=-1), ctx_1024, ctx_1024, mask_Bx1x1xS2_if1, L1_xattn_Wq, L1_xattn_bq, L1_xattn_Wk, L1_xattn_bk, L1_xattn_Wv, L1_xattn_bv, L1_xattn_Wo, L1_xattn_bo)
    x = x + _L1_ffn_ref(_layernorm(x, axis=-1), L1_ffn_w_gate, L1_ffn_w_up, L1_ffn_w_down)
    return x

_drawn_inputs = setup_inputs


def setup_inputs(seed=0):
    import zlib

    import numpy as np

    out = dict(_drawn_inputs(seed))
    spreads = {'L0_xattn_g_b': (0.0, 0.1), 'L0_xattn_out_b': (0.0, 0.1)}
    factors = {'L0_ffn_W_r': 2.718, 'L0_ffn_mu_r': 5.5, 'L1_xattn_bq': 3.442, 'L1_xattn_bk': 8.0}
    for name, (base, spread) in spreads.items():
        noise = np.random.default_rng([zlib.crc32(name.encode()), seed]).standard_normal(out[name].shape)
        drawn = base * np.exp(spread * noise) if base else spread * noise
        out[name] = jnp.asarray(drawn.astype(out[name].dtype))
    for name, factor in factors.items():
        out[name] = (out[name] * factor).astype(out[name].dtype)
    return out
```

```python
from contextlib import ExitStack

import concourse.bass as bass
from concourse import mybir

P = 128
SEQ = 64
GS = 2
NG = SEQ // GS
D = 256
NC = D // P
H = 16
HD = D // H
HP = 2 * HD
PAIRS = H // 2
QUADS = H // 4
HID = 768
NHC = HID // P
EPS = 1e-5
NEG = -1e9

F32 = mybir.dt.float32
F32R = mybir.dt.float32r
BF16 = mybir.dt.bfloat16
I32 = mybir.dt.int32
ALU = mybir.AluOpType
ACT = mybir.ActivationFunctionType
AX_X = mybir.AxisListType.X

AB_ITEMS = (["ctx_T", "x_T", "v", "gate", "q", "q_rot", "k", "k_rot"] + [f"score{p}" for p in range(PAIRS)]
            + ["o_T0", "o_T1", "y_T", "out", "x1_T", "recept", "key", "mix"])
CD_ITEMS = (["k", "v", "x_T", "q"] + [f"rough{p}" for p in range(PAIRS)] + ["max_T", "pad"]
            + [f"score{p}" for p in range(PAIRS)] + ["o_T0", "o_T1", "y_T", "out", "x3_T", "pad2"]
            + [f"hidden{i}" for i in range(NHC)])
CD_ITEMS = [n for n in CD_ITEMS if n not in ("pad", "pad2")]
if len(CD_ITEMS) % 2:
    raise ValueError("each ring bank has the same number of items in every iteration")


class Signal:

    def __init__(self, sem, per):
        self.sem, self.per = sem, per

    def wait(self, eng, it, count=None):
        eng.wait_ge(self.sem, it * self.per + (self.per if count is None else count))

    def wait_prev(self, eng, it, count=None):
        if isinstance(it, int) and it == 0:
            return
        eng.wait_ge(self.sem, (it - 1) * self.per + (self.per if count is None else count))


class Ring:

    def __init__(self, banks, filled, drained, items):
        self.banks, self.filled, self.drained = banks, filled, drained
        self.where = {n: (i % 2, i // 2) for i, n in enumerate(items)}
        self.per = len(items) // 2

    def bank(self, name):
        return self.banks[self.where[name][0]]

    def claim(self, pe, it, name):
        b, k = self.where[name]
        if isinstance(it, int) and it * self.per + k == 0:
            return self.banks[b]
        pe.wait_ge(self.drained[b], it * self.per + k)
        return self.banks[b]

    def wait(self, eng, it, name):
        b, k = self.where[name]
        eng.wait_ge(self.filled[b], it * self.per + k + 1)
        return self.banks[b]

    def done(self, eng, it, name):
        b, k = self.where[name]
        eng.wait_ge(self.drained[b], it * self.per + k + 1)

    def fill(self, ins, name):
        ins.then_inc(self.filled[self.where[name][0]], 1)

    def drain(self, ins, name):
        ins.then_inc(self.drained[self.where[name][0]], 1)


def build(nc, io):
    ctx = ExitStack()
    with ctx:
        def sb(name, shape, dt=F32):
            return ctx.enter_context(nc.sbuf_tensor(name, shape, dt))

        def psum(name, shape, dt=F32):
            return ctx.enter_context(nc.psum_tensor(name, shape, dt))

        def sem(name):
            return ctx.enter_context(nc.semaphore(name))

        names = ["a_q", "a_q_rot", "a_k", "a_k_rot", "a_v", "a_gate", "a_out",
                 "b_r", "b_k", "b_v", "c_q", "c_k", "c_v", "c_out"]
        W = {n: (sb(f"{n}_hi", [P, NC, D], F32R), sb(f"{n}_lo", [P, NC, D], F32R)) for n in names}
        W["d_gate"] = (sb("d_gate_hi", [P, NC, HID], F32R), sb("d_gate_lo", [P, NC, HID], F32R))
        W["d_up"] = (sb("d_up_hi", [P, NC, HID], F32R), sb("d_up_lo", [P, NC, HID], F32R))
        W["d_down"] = (sb("d_down_hi", [P, NHC, D], F32R), sb("d_down_lo", [P, NHC, D], F32R))
        decay = sb("decay", [P, H, P])
        rope = sb("rope", [P, 4, P])
        ident = sb("ident", [P, P])
        ident_bf = sb("ident_bf", [P, P], BF16)
        sel = sb("sel", [P, NC + 1, P], BF16)
        bias = sb("bias", [P, 4, D])
        cols = sb("cols", [P, 10])
        half = sb("half", [P, 2 * H])
        key_tab = sb("key_tab", [P, SEQ, 2])
        kcols = sb("kcols", [P, GS, 2])
        any_key = sb("any_key", [SEQ, 1])
        head_mean = sb("head_mean", [P, NC * H])
        bq4 = sb("bq4", [P, NC])
        mask_row = sb("mask_row", [P, GS * P], I32)
        mask_add = sb("mask_add", [P, GS * P], BF16)
        COL = {"mu_r": 0, "mu_k": 2, "bq": 4, "bk": 6, "even": 8, "odd": 9}

        xin = sb("xin", [P, GS, D])
        cin = sb("cin", [P, GS, D])
        c_hi = sb("c_hi", [P, NC, GS * P], F32R)
        c_lo = sb("c_lo", [P, NC, GS * P], F32R)

        class Chain:
            def __init__(self, n):
                self.x_hi = sb(f"{n}_x_hi", [P, NC, GS * P], F32R)
                self.x_lo = sb(f"{n}_x_lo", [P, NC, GS * P], F32R)
                self.t1 = sb(f"{n}_t1", [P, 2 * D])
                self.t2 = sb(f"{n}_t2", [P, 2 * D])
                self.qk = sb(f"{n}_qk", [P, 2, 2 * D])
                self.qv_hi = sb(f"{n}_qv_hi", [P, NC, GS, 2, P], F32R)
                self.qv_lo = sb(f"{n}_qv_lo", [P, NC, GS, 2, P], F32R)
                self.k_hi = sb(f"{n}_k_hi", [P, NC, GS * P], F32R)
                self.k_lo = sb(f"{n}_k_lo", [P, NC, GS * P], F32R)
                self.v = sb(f"{n}_v", [P, GS, H, HP])
                self.p = sb(f"{n}_p", [P, 2, GS, 2, P])
                self.y = sb(f"{n}_y", [P, 2, NC, GS * P], F32R)
                self.xb = sb(f"{n}_xb", [P, GS, D])
                self.stats = sb(f"{n}_stats", [P, GS, 6])
                self.mv = sb(f"{n}_mv", [P, GS, 2])
                self.negmean = sb(f"{n}_negmean", [P, GS])
                self.vareps = sb(f"{n}_vareps", [P, GS])
                self.rstd = sb(f"{n}_rstd", [P, GS])
                self.ring = [psum(f"{n}_ring{i}", [P, 512]) for i in range(2)]
                self.o = psum(f"{n}_o", [P, QUADS, GS, P])

        AB, CD = Chain("ab"), Chain("cd")
        sg = sb("sg", [P, GS, D])
        x2 = sb("x2", [P, GS, D])
        xs = sb("xs", [P, NC, GS, P + 1])
        ssq = sb("ssq", [P, GS, H])
        gn_var = sb("gn_var", [P, GS, H])
        gn_rstd = sb("gn_rstd", [P, GS, H])
        q_hi = sb("q_hi", [P, NC, GS * P], F32R)
        mx = sb("mx", [P, PAIRS, GS, 2])
        mx_parts = sb("mx_parts", [P, GS, 2, 4, 32], BF16)
        m_T = sb("m_T", [P, GS, 2, P], BF16)
        rz = sb("rz", [P, GS, H])
        xo = sb("xo", [P, GS, D])

        r_ab = Ring(AB.ring, [sem("ab_filled0"), sem("ab_filled1")], [sem("ab_drained0"), sem("ab_drained1")], AB_ITEMS)
        r_cd = Ring(CD.ring, [sem("cd_filled0"), sem("cd_filled1")], [sem("cd_drained0"), sem("cd_drained1")], CD_ITEMS)

        def signals(**per):
            return {n: Signal(sem(n), k) for n, k in per.items()}

        S = signals(
            x_in=16, ctx_in=16, a_stats=2, a_aggr=2, a_small=2, a_rstd=1, a_xhat=2, a_x_hi=1, a_c_hi=1,
            a_th=1, a_sg=1, a_xb=1, a_qk=2, a_qv_hi=2, a_qv_lo=2, a_k_hi=1, a_k_lo=1,
            a_pv=PAIRS, a_osb=2, a_sq=2, a_ssq=2, a_gvar=2, a_grstd=2, a_yg=2, a_y_hi=1,
            b_stats=2, b_aggr=2, b_small=2, b_rstd=1, b_xhat=2, b_d=1, b_xr=2, b_xk=2,
            b_xr_hi=1, b_xr_lo=1, b_xk_hi=1, b_xk_lo=1, b_relu=1, b_k2_hi=1, b_k2_lo=1, b_x2=1,
            mask_in=16, c_mask=1, c_kcols=1, c_stats=2, c_aggr=2, c_small=2, c_rstd=1, c_xhat=2, c_x_hi=1,
            c_k_hi=1, c_k_lo=1, c_kv=2, c_q_hi=1, c_qv_hi=2, c_qv_lo=2, c_xb=1,
            c_part0=NC, c_part1=NC, c_pv=PAIRS, c_osb=2, c_rz=2, c_yb=1, c_y_hi=1,
            d_stats=2, d_aggr=2, d_small=2, d_rstd=1, d_xhat=2, d_x_hi=1,
            d_th=NHC, d_a=NHC, d_h_hi=NHC, d_h_lo=NHC, d_down=NHC, d_x4=1, out_done=16,
        )
        load = sem("load")
        staged = [sem("staged0"), sem("staged1")]
        w_ready, w_centred, w_hi_done, w_lo_done = sem("w_ready"), sem("w_centred"), sem("w_hi_done"), sem("w_lo_done")
        mask_prep, mask_T, dve_const, act_const = sem("mask_prep"), sem("mask_T"), sem("dve_const"), sem("act_const")
        v_zero = sem("v_zero")
        NLOAD, NDVE_CONST, NACT_CONST = 14, 8, 3

        def flat(x):
            n = len(x.shape)
            names_ = "abcdef"[:n - 1]
            return x[:].rearrange("p " + " ".join(names_) + " -> p (" + " ".join(names_) + ")")

        def raw(x):
            return x.bitcast(F32)

        stepped = sem("stepped")

        def apart(eng):
            eng.sem_inc(stepped, 1)

        stage = [AB.qk[:].rearrange("p a n -> p (a n)"), CD.qk[:].rearrange("p a n -> p (a n)")]
        wf = [flat(AB.v), flat(CD.p)]
        SCALES = {"a_out": 0.5, "b_v": 0.5, "c_q": 0.25}
        parts = []
        for n, (hi, lo) in W.items():
            src = io[n].rearrange("(c p) n -> p c n", p=P)
            if n in names:
                parts.append((n, flat(hi), flat(lo), src))
            else:
                for c in range(hi.shape[1]):
                    parts.append((n, hi[:, c, :], lo[:, c, :], src[:, c:c + 1, :]))

        def width(part):
            return part[3].shape[1] * part[3].shape[2]

        block = ctx.enter_context(nc.Block())

        def seqs(u):
            return slice(GS * u, GS * u + GS) if isinstance(u, int) else bass.ds(GS * u, GS)

        @block.sync
        def _(sp):
            for dst, src in ((decay[:], io["decay"]), (rope[:], io["rope"]), (ident[:], io["ident"]),
                             (cols[:, COL["even"]:COL["odd"] + 1], io["parity"]),
                             (cols[:, 0:2], io["mu_r"].rearrange("(c p) -> p c", p=P)),
                             (cols[:, 2:4], io["mu_k"].rearrange("(c p) -> p c", p=P)),
                             (cols[:, 4:6], io["bq"].rearrange("(c p) -> p c", p=P)),
                             (cols[:, 6:8], io["bk"].rearrange("(c p) -> p c", p=P)),
                             (bias[:, 0, :], io["gate_b"].partition_broadcast(P)),
                             (bias[:, 1, :], io["out_b"].partition_broadcast(P)),
                             (bias[:, 2, :], io["bv"].partition_broadcast(P)),
                             (bias[:, 3, :], io["bo"].partition_broadcast(P)),
                             (CD.t1[0:SEQ, 0:P].bitcast(I32), io["mask"].rearrange("b i j k -> b (i j k)")),
                             (flat(AB.p)[:, 0:(NC + 1) * P], io["sel"])):
                sp.dma_start(dst, src, allow_slow_non_contiguous=True).then_inc(load, 16)
            for i, part in enumerate(parts):
                if i >= 2:
                    sp.wait_ge(w_ready, i - 1)
                dst = stage[i % 2][:, 0:width(part)]
                dst = dst.bitcast(I32) if part[0].startswith("d_") else dst
                sp.dma_start(dst.rearrange("p (c n) -> p c n", c=part[3].shape[1]), part[3]).then_inc(staged[i % 2], 16)

            def loads(u):
                S["a_xb"].wait_prev(sp, u)
                S["a_xhat"].wait_prev(sp, u)
                sp.dma_start(xin[:], io["x"][seqs(u)].rearrange("s p c -> p s c")).then_inc(S["x_in"].sem, 16)
                if not (isinstance(u, int) and u == 0):
                    r_ab.wait(sp, u - 1, "ctx_T")
                sp.dma_start(cin[:], io["ctx"][seqs(u)].rearrange("s p c -> p s c")).then_inc(S["ctx_in"].sem, 16)

            def mask(j):
                S["c_mask"].wait_prev(sp, j)
                sp.dma_start(mask_row[0:P:32, :], io["mask"][seqs(j)].rearrange("s i j k -> (s i j k)").partition_broadcast(4)).then_inc(S["mask_in"].sem, 16)

            def store(j):
                S["d_x4"].wait(sp, j)
                sp.dma_start(io["out"][seqs(j)].rearrange("s p c -> p s c"), xo[:]).then_inc(S["out_done"].sem, 16)

            loads(0)
            loads(1)
            sp.wait_ge(dve_const, NDVE_CONST)
            mask(0)
            with sp.Fori(1, NG - 1) as u:
                loads(u + 1)
                mask(u)
                store(u - 1)
            mask(NG - 1)
            store(NG - 2)
            store(NG - 1)
            S["out_done"].wait(sp, NG - 1)

        @block.tensor
        def _(pe):
            def wterms(n, c, cols_):
                hi, lo = W[n]
                return hi[:, c, cols_], lo[:, c, cols_]

            def channel_major(ring, it, item, n, x_hi, x_lo, width=NC, base=0, out=None):
                bank = ring.claim(pe, it, item) if out is None else out
                ins = None
                for m in range(width):
                    dst = bank[:, m * 256:(m + 1) * 256]
                    k = 0
                    for c in range(NC):
                        w_hi, w_lo = wterms(n, c, slice(base + m * P, base + (m + 1) * P))
                        for w, x in ((w_hi, x_hi), (w_lo, x_hi), (w_hi, x_lo)):
                            ins = pe.matmul(dst, w, x[:, c, :], start=(k == 0), stop=(k == 3 * NC - 1))
                            k += 1
                return ins

            def token_major(bank, n, x_hi, x_lo, chunks=NC):
                ins = None
                for s in range(GS):
                    dst = bank[:, s * D:(s + 1) * D]
                    k = 0
                    for c in range(chunks):
                        w_hi, w_lo = wterms(n, c, slice(0, D))
                        xh, xl = x_hi[:, c, s * P:(s + 1) * P], x_lo[:, c, s * P:(s + 1) * P]
                        for x, w in ((xh, w_hi), (xl, w_hi), (xh, w_lo)):
                            ins = pe.matmul(dst, x, w, start=(k == 0), stop=(k == 3 * chunks - 1))
                            k += 1
                return ins

            def transposes(bank, src):
                ins = None
                for c in range(NC):
                    for s in range(GS):
                        o = (c * GS + s) * P
                        ins = pe.transpose(bank[:, o:o + P], src[:, s * D + c * P:s * D + (c + 1) * P], ident[:])
                return ins

            def scores(ch, bank, p, add_max):
                c, g = p // 4, p % 4
                r = slice(32 * g, 32 * g + 32)
                ins = None
                for s in range(GS):
                    dst = bank[:, s * 256:(s + 1) * 256]
                    t = slice(s * P, (s + 1) * P)
                    q_h = ch.qv_hi[r, c, s, :, :].rearrange("p a q -> p (a q)")
                    q_l = ch.qv_lo[r, c, s, :, :].rearrange("p a q -> p (a q)")
                    terms = ((ch.k_hi[r, c, t], q_h), (ch.k_lo[r, c, t], q_h), (ch.k_hi[r, c, t], q_l))
                    for i, (k, q) in enumerate(terms):
                        ins = pe.matmul(dst, k, q, start=(i == 0), stop=(i == 2 and not add_max))
                    if add_max:
                        ins = pe.matmul(dst, sel[r, c, :], m_T[r, s, :, :].rearrange("r a q -> r (a q)"),
                                        start=False, stop=True)
                return ins

            def attend(ch, p):
                ins = None
                for s in range(GS):
                    for par in range(2):
                        h = 2 * p + par
                        j, quad = h % 4, h // 4
                        ins = pe.matmul(ch.o[32 * j:32 * j + 32, quad, s, :], ch.v[:, s, h, :],
                                        ch.p[:, p % 2, s, par, :], start=True, stop=True, skip_group_check=True,
                                        tile_position=(0, 32 * j))
                return ins

            def heads_to_tokens(ch, bank, s):
                ins = None
                for quad in range(QUADS):
                    ins = pe.transpose(bank[:, quad * P:(quad + 1) * P],
                                       ch.qk[:].rearrange("p a b -> p (a b)")[:, (quad * GS + s) * P:(quad * GS + s + 1) * P],
                                       ident[:])
                return ins

            def ctx_T(u):
                bank = r_ab.claim(pe, u, "ctx_T")
                S["ctx_in"].wait(pe, u)
                r_ab.fill(transposes(bank, cin[:].rearrange("p s c -> p (s c)")), "ctx_T")

            def x_T(u):
                bank = r_ab.claim(pe, u, "x_T")
                S["a_xhat"].wait(pe, u)
                r_ab.fill(transposes(bank, AB.t1[:]), "x_T")

            def a_v(u):
                bank = r_ab.claim(pe, u, "v")
                r_ab.done(pe, u, "ctx_T")
                r_ab.fill(token_major(bank, "a_v", c_hi, c_lo), "v")

            def a_gate(u):
                bank = r_ab.claim(pe, u, "gate")
                r_ab.done(pe, u, "x_T")
                r_ab.fill(token_major(bank, "a_gate", AB.x_hi, AB.x_lo), "gate")

            def a_proj(u, item, n, hi, lo):
                r_ab.fill(channel_major(r_ab, u, item, n, hi, lo), item)

            def a_score(u, p):
                bank = r_ab.claim(pe, u, f"score{p}")
                if p == 0:
                    S["a_qv_hi"].wait(pe, u)
                    S["a_qv_lo"].wait(pe, u)
                    S["a_k_hi"].wait(pe, u)
                    S["a_k_lo"].wait(pe, u)
                r_ab.fill(scores(AB, bank, p, False), f"score{p}")

            def a_attend(u, p):
                r_ab.done(pe, u, f"score{p}")
                if p == 0:
                    r_ab.done(pe, u, "v")
                    S["a_osb"].wait_prev(pe, u, 1)
                if p == PAIRS // 2:
                    S["a_osb"].wait_prev(pe, u, 2)
                attend(AB, p).then_inc(S["a_pv"].sem, 1)

            def a_o_T(u, s):
                bank = r_ab.claim(pe, u, f"o_T{s}")
                S["a_osb"].wait(pe, u)
                r_ab.fill(heads_to_tokens(AB, bank, s), f"o_T{s}")

            def a_y_T(u):
                bank = r_ab.claim(pe, u, "y_T")
                S["a_yg"].wait(pe, u)
                r_ab.fill(transposes(bank, AB.t2[:]), "y_T")

            def a_out(u):
                bank = r_ab.claim(pe, u, "out")
                r_ab.done(pe, u, "y_T")
                r_ab.fill(token_major(bank, "a_out", AB.y[:, 0], AB.y[:, 1]), "out")

            def x1_T(u):
                bank = r_ab.claim(pe, u, "x1_T")
                S["b_xhat"].wait(pe, u)
                r_ab.fill(transposes(bank, AB.t1[:]), "x1_T")

            def b_recept(u):
                bank = r_ab.claim(pe, u, "recept")
                S["b_xr_hi"].wait(pe, u)
                S["b_xr_lo"].wait(pe, u)
                r_ab.fill(token_major(bank, "b_r", AB.x_hi, AB.x_lo), "recept")

            def b_key(u):
                S["b_xk_hi"].wait(pe, u)
                S["b_xk_lo"].wait(pe, u)
                r_ab.fill(channel_major(r_ab, u, "key", "b_k", AB.k_hi, AB.k_lo), "key")

            def b_mix(u):
                bank = r_ab.claim(pe, u, "mix")
                S["b_k2_hi"].wait(pe, u)
                S["b_k2_lo"].wait(pe, u)
                r_ab.fill(token_major(bank, "b_v", AB.y[:, 0], AB.y[:, 1]), "mix")

            def c_k(j):
                r_ab.done(pe, j, "ctx_T")
                r_cd.fill(channel_major(r_cd, j, "k", "c_k", c_hi, c_lo), "k")

            def c_v(j):
                bank = r_cd.claim(pe, j, "v")
                r_cd.fill(token_major(bank, "c_v", c_hi, c_lo), "v")

            def c_x_T(j):
                bank = r_cd.claim(pe, j, "x_T")
                S["c_xhat"].wait(pe, j)
                r_cd.fill(transposes(bank, CD.t1[:]), "x_T")

            def c_q(j):
                r_cd.done(pe, j, "x_T")
                r_cd.fill(channel_major(r_cd, j, "q", "c_q", CD.x_hi, CD.x_lo), "q")

            def c_rough(j, p):
                bank = r_cd.claim(pe, j, f"rough{p}")
                if p == 0:
                    S["c_q_hi"].wait(pe, j)
                    S["c_kv"].wait(pe, j)
                    S["c_mask"].wait(pe, j)
                c, g = p // 4, p % 4
                r = slice(32 * g, 32 * g + 32)
                ins = None
                for s in range(GS):
                    dst = bank[:, s * 256:(s + 1) * 256]
                    kv = CD.y[r, :, :, :].rearrange("p v c (s k) -> p v c s k", s=GS)[:, :, c, s, :]
                    pe.matmul(dst, q_hi[r, c, s * P:(s + 1) * P], kv, start=True, stop=False)
                    ins = pe.matmul(dst, sel[r, NC, :], mask_add[r, s * P:(s + 1) * P].rearrange("r (o k) -> r o k", o=1)
                                    .broadcast_to([32, 2, P]), start=False, stop=True)
                r_cd.fill(ins, f"rough{p}")

            def c_max_T(j):
                bank = r_cd.claim(pe, j, "max_T")
                S["c_part1"].wait(pe, j)
                bf = bank[:].bitcast(BF16)
                for s in range(GS):
                    for par in range(2):
                        o = (s * 2 + par) * P
                        ins = pe.transpose(bf[:, o:o + P],
                                           mx_parts[:, s, par, :, :].rearrange("q a b -> q (a b)"), ident_bf[:])
                r_cd.fill(ins, "max_T")

            def c_score(j, p):
                bank = r_cd.claim(pe, j, f"score{p}")
                if p == 0:
                    S["c_qv_hi"].wait(pe, j)
                    S["c_qv_lo"].wait(pe, j)
                    S["c_k_hi"].wait(pe, j)
                    S["c_k_lo"].wait(pe, j)
                    r_cd.done(pe, j, "max_T")
                r_cd.fill(scores(CD, bank, p, True), f"score{p}")

            def c_attend(j, p):
                r_cd.done(pe, j, f"score{p}")
                if p == 0:
                    r_cd.done(pe, j, "v")
                    S["d_x4"].wait_prev(pe, j)
                if p == PAIRS // 2:
                    S["c_osb"].wait_prev(pe, j, 2)
                attend(CD, p).then_inc(S["c_pv"].sem, 1)

            def c_o_T(j, s):
                bank = r_cd.claim(pe, j, f"o_T{s}")
                S["c_osb"].wait(pe, j)
                r_cd.fill(heads_to_tokens(CD, bank, s), f"o_T{s}")

            def c_y_T(j):
                bank = r_cd.claim(pe, j, "y_T")
                S["c_yb"].wait(pe, j)
                r_cd.fill(transposes(bank, CD.t2[:]), "y_T")

            def c_out(j):
                bank = r_cd.claim(pe, j, "out")
                r_cd.done(pe, j, "y_T")
                r_cd.fill(token_major(bank, "c_out", CD.y[:, 0], CD.y[:, 1]), "out")

            def x3_T(j):
                bank = r_cd.claim(pe, j, "x3_T")
                S["d_xhat"].wait(pe, j)
                r_cd.fill(transposes(bank, CD.t1[:]), "x3_T")

            def d_hidden(j, i):
                item = f"hidden{i}"
                bank = r_cd.claim(pe, j, item)
                if i == 0:
                    r_cd.done(pe, j, "x3_T")
                channel_major(r_cd, j, item, "d_gate", CD.x_hi, CD.x_lo, 1, i * P, bank[:, 0:256])
                r_cd.fill(channel_major(r_cd, j, item, "d_up", CD.x_hi, CD.x_lo, 1, i * P, bank[:, 256:512]), item)

            def d_down(j, i):
                S["d_h_hi"].wait(pe, j, i + 1)
                S["d_h_lo"].wait(pe, j, i + 1)
                acc = CD.o[:, 0:2, :, :].rearrange("p a b c -> p (a b c)")
                w_hi, w_lo = W["d_down"][0][:, i, :], W["d_down"][1][:, i, :]
                for s in range(GS):
                    h_hi = CD.qv_hi[:, i % 2, 0, :, :].rearrange("p a b -> p (a b)")[:, s * P:(s + 1) * P]
                    h_lo = CD.qv_lo[:, i % 2, 0, :, :].rearrange("p a b -> p (a b)")[:, s * P:(s + 1) * P]
                    for k, (h, w) in enumerate(((h_hi, w_hi), (h_lo, w_hi), (h_hi, w_lo))):
                        ins = pe.matmul(acc[:, s * D:(s + 1) * D], h, w,
                                        start=(i == 0 and s == 0 and k == 0), stop=(i == NHC - 1 and k == 2),
                                        skip_group_check=True)
                ins.then_inc(S["d_down"].sem, 1)

            def body(u, j):
                ab, cd = u is not None, j is not None
                if cd:
                    c_k(j); c_v(j)
                if ab:
                    ctx_T(u); x_T(u)
                if cd:
                    c_x_T(j)
                if ab:
                    a_v(u)
                if cd:
                    c_q(j)
                if ab:
                    a_gate(u)
                steps = [lambda: a_proj(u, "q", "a_q", AB.x_hi, AB.x_lo),
                         lambda: a_proj(u, "q_rot", "a_q_rot", AB.x_hi, AB.x_lo),
                         lambda: a_proj(u, "k", "a_k", c_hi, c_lo),
                         lambda: a_proj(u, "k_rot", "a_k_rot", c_hi, c_lo)]
                for p in range(PAIRS):
                    if ab and p % 2 == 0:
                        steps[p // 2]()
                    if cd:
                        c_rough(j, p)
                if cd:
                    c_max_T(j)
                for p in range(PAIRS + 1):
                    if ab and p < PAIRS:
                        a_score(u, p)
                    if cd and p < PAIRS:
                        c_score(j, p)
                    if ab and p > 0:
                        a_attend(u, p - 1)
                    if cd and p > 0:
                        c_attend(j, p - 1)
                for s in range(GS):
                    if ab:
                        a_o_T(u, s)
                    if cd:
                        c_o_T(j, s)
                if ab:
                    a_y_T(u)
                if cd:
                    c_y_T(j)
                if ab:
                    a_out(u)
                if cd:
                    c_out(j)
                if ab:
                    x1_T(u)
                if cd:
                    x3_T(j)
                    d_hidden(j, 0)
                if ab:
                    b_recept(u)
                if cd:
                    d_hidden(j, 1)
                    d_down(j, 0)
                if ab:
                    b_key(u)
                if cd:
                    d_hidden(j, 2)
                    d_down(j, 1)
                    d_hidden(j, 3)
                    d_down(j, 2)
                if ab:
                    b_mix(u)
                if cd:
                    d_hidden(j, 4)
                    d_down(j, 3)
                    d_hidden(j, 5)
                    d_down(j, 4)
                    d_down(j, 5)

            pe.wait_ge(load, 16 * NLOAD)
            pe.wait_ge(mask_prep, 4)
            pe.transpose(AB.ring[0][:, 0:SEQ], CD.t2[0:SEQ, 0:P], ident[0:SEQ, 0:SEQ])
            pe.transpose(AB.ring[0][:, SEQ:2 * SEQ], CD.t2[0:SEQ, P:2 * P], ident[0:SEQ, 0:SEQ]).then_inc(mask_T, 1)
            pe.wait_ge(w_lo_done, len(parts))
            pe.wait_ge(dve_const, NDVE_CONST)
            pe.wait_ge(act_const, NACT_CONST)
            body(0, None)
            with pe.Fori(1, NG) as u:
                body(u, u - 1)
            body(None, NG - 1)

        @block.scalar
        def _(act):
            def ctx_hi(u):
                bank = r_ab.wait(act, u, "ctx_T")
                if not (isinstance(u, int) and u == 0):
                    r_cd.wait(act, u - 1, "v")
                if not (isinstance(u, int) and u == 0):
                    r_ab.wait(act, u - 1, "k_rot")
                act.activation(flat(c_hi), bank[:], ACT.Copy).then_inc(S["a_c_hi"].sem, 1)

            def x_hi(ring, it, item, ch, sig):
                bank = ring.wait(act, it, item)
                act.activation(flat(ch.x_hi), bank[:], ACT.Copy).then_inc(S[sig].sem, 1)

            def values(ring, it, ch):
                bank = ring.wait(act, it, "v")
                ring.drain(act.activation(ch.v[:, :, :, 0:HD].rearrange("p s h e -> p (s h) e"),
                                          bank[:].rearrange("p (a e) -> p a e", e=HD), ACT.Copy), "v")

            def a_th(u):
                r_ab.done(act, u, "gate")
                act.activation(AB.t2[:], AB.t1[:], ACT.Tanh, scale=0.5).then_inc(S["a_th"].sem, 1)

            def a_k_hi(u):
                S["a_qk"].wait(act, u, 2)
                act.activation(flat(AB.k_hi), AB.qk[:, 1, :], ACT.Copy).then_inc(S["a_k_hi"].sem, 1)

            def osb(ch, n, it, half_):
                S[n + "_pv"].wait(act, it, 4 * half_ + 4)
                act.activation(ch.qk[:, half_, :], ch.o[:, 2 * half_:2 * half_ + 2, :, :].rearrange("p a b c -> p (a b c)"),
                               ACT.Copy).then_inc(S[n + "_osb"].sem, 1)

            def a_sq(u, s):
                bank = r_ab.wait(act, u, f"o_T{s}")
                act.activation(AB.t1[:, s * D:(s + 1) * D].rearrange("p (h e) -> p h e", e=HD),
                               bank[:].rearrange("p (h e) -> p h e", e=HP)[:, :, 0:HD],
                               ACT.Square).then_inc(S["a_sq"].sem, 1)

            def y_hi(ring, it, ch, n):
                bank = ring.wait(act, it, "y_T")
                act.activation(flat(ch.y[:, 0]), bank[:], ACT.Copy).then_inc(S[n + "_y_hi"].sem, 1)

            def b_xs(u):
                bank = r_ab.wait(act, u, "x1_T")
                r_ab.drain(act.activation(xs[:, :, :, 1:P + 1].rearrange("p c s t -> p (c s) t"),
                                          bank[:].rearrange("p (a t) -> p a t", t=P), ACT.Copy), "x1_T")

            def b_xr_hi(u):
                S["b_xr"].wait(act, u)
                act.activation(flat(AB.x_hi), AB.t2[:], ACT.Copy).then_inc(S["b_xr_hi"].sem, 1)

            def b_xk_hi(u):
                S["b_xk"].wait(act, u)
                act.activation(flat(AB.k_hi), AB.qk[:, 0, :], ACT.Copy).then_inc(S["b_xk_hi"].sem, 1)

            def b_th(u):
                bank = r_ab.wait(act, u, "recept")
                S["b_xr_lo"].wait(act, u)
                r_ab.drain(act.activation(AB.t2[:], bank[:], ACT.Tanh, scale=0.5), "recept")

            def b_relu(u):
                bank = r_ab.wait(act, u, "key")
                act.activation(AB.qk[:, 1, :], bank[:], ACT.Relu).then_inc(S["b_relu"].sem, 1)

            def b_k2_hi(u):
                r_ab.done(act, u, "key")
                act.activation(flat(AB.y[:, 0]), AB.t1[:], ACT.Copy).then_inc(S["b_k2_hi"].sem, 1)

            def plus_bias(j, item, slot, col):
                bank = r_cd.wait(act, j, item)
                for m in range(NC):
                    ins = act.activation(CD.qk[:, slot, m * 256:(m + 1) * 256], bank[:, m * 256:(m + 1) * 256],
                                         ACT.Identity, bias=col[:, m:m + 1])
                r_cd.drain(ins, item)

            def c_k_hi(j):
                r_cd.done(act, j, "k")
                act.activation(flat(CD.k_hi), CD.qk[:, 1, :], ACT.Copy).then_inc(S["c_k_hi"].sem, 1)

            def c_q_hi(j):
                r_cd.done(act, j, "q")
                act.activation(flat(q_hi), CD.qk[:, 0, :], ACT.Copy).then_inc(S["c_q_hi"].sem, 1)

            def c_mT(j):
                bank = r_cd.wait(act, j, "max_T")
                r_cd.drain(act.activation(flat(m_T), bank[:].bitcast(BF16)[:, 0:GS * 2 * P], ACT.Copy), "max_T")

            def c_exp(j, p):
                bank = r_cd.wait(act, j, f"score{p}")
                if p == 0:
                    S["c_kcols"].wait(act, j)
                if p >= 2:
                    S["c_pv"].wait(act, j, p - 1)
                for s in range(GS):
                    ins = act.activation(flat(CD.p[:, p % 2, s]), bank[:, s * 256:(s + 1) * 256],
                                         ACT.Exp, bias=kcols[:, s, 1:2], scale=kcols[:, s, 0:1])
                r_cd.drain(ins, f"score{p}")

            def d_th(j, i):
                bank = r_cd.wait(act, j, f"hidden{i}")
                act.activation(CD.t1[:, (i % 2) * 256:(i % 2) * 256 + 256], bank[:, 0:256], ACT.Tanh,
                               scale=0.5 / 127.0).then_inc(S["d_th"].sem, 1)

            def d_h_hi(j, i):
                r_cd.done(act, j, f"hidden{i}")
                if i >= 2:
                    S["d_down"].wait(act, j, i - 1)
                act.activation(flat(CD.qv_hi[:, i % 2, 0]), CD.t2[:, (i % 2) * 256:(i % 2) * 256 + 256],
                               ACT.Copy).then_inc(S["d_h_hi"].sem, 1)

            def body(u, j):
                ab, cd = u is not None, j is not None
                if cd:
                    plus_bias(j, "k", 1, cols[:, COL["bk"]:COL["bk"] + 2])
                    c_k_hi(j)
                    values(r_cd, j, CD)
                if ab:
                    ctx_hi(u)
                    x_hi(r_ab, u, "x_T", AB, "a_x_hi")
                if cd:
                    x_hi(r_cd, j, "x_T", CD, "c_x_hi")
                if ab:
                    values(r_ab, u, AB)
                if cd:
                    plus_bias(j, "q", 0, bq4)
                    c_q_hi(j)
                if ab:
                    a_th(u)
                    a_k_hi(u)
                if cd:
                    c_mT(j)
                for p in range(PAIRS):
                    if cd:
                        c_exp(j, p)
                    if ab and p == 5:
                        osb(AB, "a", u, 0)
                    if cd and p == 5:
                        osb(CD, "c", j, 0)
                if ab:
                    osb(AB, "a", u, 1)
                if cd:
                    osb(CD, "c", j, 1)
                if ab:
                    a_sq(u, 0)
                    a_sq(u, 1)
                    y_hi(r_ab, u, AB, "a")
                if cd:
                    y_hi(r_cd, j, CD, "c")
                if ab:
                    b_xs(u)
                if cd:
                    x_hi(r_cd, j, "x3_T", CD, "d_x_hi")
                    d_th(j, 0)
                if ab:
                    b_xr_hi(u)
                    b_xk_hi(u)
                if cd:
                    d_h_hi(j, 0)
                    d_th(j, 1)
                if ab:
                    b_th(u)
                    b_relu(u)
                if cd:
                    d_h_hi(j, 1)
                    d_th(j, 2)
                if ab:
                    b_k2_hi(u)
                if cd:
                    for i in range(2, NHC):
                        d_h_hi(j, i)
                        if i + 1 < NHC:
                            d_th(j, i + 1)

            act.wait_ge(load, 16 * NLOAD)
            for i, part in enumerate(parts):
                act.wait_ge(w_ready, i + 1)
                act.activation(part[1], wf[i % 2][:, 0:width(part)], ACT.Copy).then_inc(w_hi_done, 1)
            act.wait_ge(mask_T, 1)
            for i in range(2):
                act.activation(key_tab[:, :, i], AB.ring[0][:, i * SEQ:(i + 1) * SEQ], ACT.Copy).then_inc(act_const, 1)
            act.activation(bq4[:], cols[:, COL["bq"]:COL["bq"] + 2], ACT.Copy, scale=0.25).then_inc(act_const, 1)
            act.wait_ge(act_const, NACT_CONST)
            act.wait_ge(v_zero, 1)
            body(0, None)
            with act.Fori(1, NG) as u:
                body(u, u - 1)
            body(None, NG - 1)

        @block.vector
        def _(dve):
            def stats(ch, it, n, x):
                for s in range(GS):
                    dve.bn_stats(ch.stats[:, s, :], x[:, s, :]).then_inc(S[n + "_stats"].sem, 1)
                for s in range(GS):
                    S[n + "_stats"].wait(dve, it, s + 1)
                    apart(dve)
                    dve.bn_aggr(ch.mv[:, s, :], ch.stats[:, s, :]).then_inc(S[n + "_aggr"].sem, 1)

            def low(ring, it, item, sig, lo, hi):
                bank = ring.wait(dve, it, item)
                S[sig].wait(dve, it)
                ring.drain(dve.tensor_tensor(lo, bank[:], raw(hi), ALU.subtract), item)

            def table(i):
                return rope[:, i:i + 1, :].broadcast_to([P, 2 * GS, P])

            def rows(x):
                return x.rearrange("p (a t) -> p a t", t=P)

            def a_gate(u):
                bank = r_ab.wait(dve, u, "gate")
                r_ab.drain(dve.tensor_tensor(AB.t1[:].rearrange("p (s n) -> p s n", s=GS), bank[:].rearrange("p (s n) -> p s n", s=GS),
                                             bias[:, 0:1, :].broadcast_to([P, GS, D]), ALU.add), "gate")

            def a_sg(u):
                S["a_th"].wait(dve, u)
                dve.scalar_tensor_tensor(flat(sg), AB.t2[:], 1.0, AB.t1[:], ALU.add, ALU.mult).then_inc(S["a_sg"].sem, 1)

            def a_rotate(u, i):
                item = ("q", "q_rot", "k", "k_rot")[i]
                bank = r_ab.wait(dve, u, item)
                if i == 0:
                    S["a_sg"].wait(dve, u)
                if i == 2:
                    S["a_qk"].wait(dve, u, 1)
                dst = AB.t2 if i % 2 else AB.t1
                r_ab.drain(dve.tensor_tensor(rows(dst[:]), rows(bank[:]), table(i), ALU.mult), item)

            def qv_low(ch, it, n):
                for par in range(2):
                    S[n + "_qv_hi"].wait(dve, it, par + 1)
                    dve.scalar_tensor_tensor(ch.qv_lo[:].rearrange("p c s a t -> p (c s) a t")[:, :, par, :],
                                             rows(ch.qk[:, 0, :]), cols[:, COL["even"] + par:COL["even"] + par + 1],
                                             raw(ch.qv_hi[:]).rearrange("p c s a t -> p (c s) a t")[:, :, par, :],
                                             ALU.mult, ALU.subtract).then_inc(S[n + "_qv_lo"].sem, 1)

            def k_low(ch, it, n):
                S[n + "_k_hi"].wait(dve, it)
                dve.tensor_tensor(flat(ch.k_lo), ch.qk[:, 1, :], raw(flat(ch.k_hi)), ALU.subtract).then_inc(S[n + "_k_lo"].sem, 1)

            def a_decay(u, p):
                bank = r_ab.wait(dve, u, f"score{p}")
                if p >= 2:
                    S["a_pv"].wait(dve, u, p - 1)
                r_ab.drain(dve.tensor_tensor(AB.p[:, p % 2].rearrange("k s a q -> k s (a q)"),
                                             bank[:].rearrange("k (s n) -> k s n", s=GS),
                                             decay[:, 2 * p:2 * p + 2, :].rearrange("k (o a) q -> k o (a q)", o=1).broadcast_to([P, GS, 2 * P]),
                                             ALU.mult), f"score{p}")

            def heads(bank):
                return bank[:].rearrange("p (h e) -> p h e", e=HP)[:, :, 0:HD]

            def a_ssq(u, s):
                S["a_sq"].wait(dve, u, s + 1)
                dve.tensor_reduce(ssq[:, s, :], AB.t1[:, s * D:(s + 1) * D].rearrange("p (h e) -> p h e", e=HD),
                                  AX_X, ALU.add).then_inc(S["a_ssq"].sem, 1)

            def a_y(u, s):
                bank = r_ab.wait(dve, u, f"o_T{s}")
                S["a_grstd"].wait(dve, u, s + 1)
                r_ab.drain(dve.tensor_tensor(flat(AB.p[:, 0])[:, s * D:(s + 1) * D].rearrange("p (h e) -> p h e", e=HD), heads(bank),
                                             gn_rstd[:, s, :].rearrange("p (h o) -> p h o", o=1).broadcast_to([P, H, HD]), ALU.mult), f"o_T{s}")

            def residual(ring, it, ch, n):
                bank = ring.wait(dve, it, "out")
                S[n + "_xb"].wait(dve, it)
                ring.drain(dve.tensor_tensor(flat(ch.xb), bank[:], flat(ch.xb), ALU.add), "out")

            def b_shift(u):
                r_ab.done(dve, u, "x1_T")
                now = xs[:, :, :, 1:P + 1].rearrange("p c s t -> p (c s) t")
                before = xs[:, :, :, 0:P].rearrange("p c s t -> p (c s) t")
                dve.tensor_tensor(rows(AB.t1[:]), now, before, ALU.subtract).then_inc(S["b_d"].sem, 1)
                S["b_d"].wait(dve, u)
                for dst, mu, sig in ((AB.t2[:], "mu_r", "b_xr"), (AB.qk[:, 0, :], "mu_k", "b_xk")):
                    for c in range(NC):
                        dve.scalar_tensor_tensor(rows(dst)[:, GS * c:GS * c + GS, :], rows(AB.t1[:])[:, GS * c:GS * c + GS, :],
                                                 cols[:, COL[mu] + c:COL[mu] + c + 1], xs[:, c, :, 0:P],
                                                 ALU.mult, ALU.add).then_inc(S[sig].sem, 1)

            def b_lows(u):
                S["b_xr_hi"].wait(dve, u)
                dve.tensor_tensor(flat(AB.x_lo), AB.t2[:], raw(flat(AB.x_hi)), ALU.subtract).then_inc(S["b_xr_lo"].sem, 1)
                S["b_xk_hi"].wait(dve, u)
                dve.tensor_tensor(flat(AB.k_lo), AB.qk[:, 0, :], raw(flat(AB.k_hi)), ALU.subtract).then_inc(S["b_xk_lo"].sem, 1)

            def b_k2(u):
                bank = r_ab.wait(dve, u, "key")
                S["b_relu"].wait(dve, u)
                r_ab.drain(dve.tensor_tensor(AB.t1[:], bank[:], AB.qk[:, 1, :], ALU.mult), "key")

            def b_k2_lo(u):
                S["b_k2_hi"].wait(dve, u)
                dve.tensor_tensor(flat(AB.y[:, 1]), AB.t1[:], raw(flat(AB.y[:, 0])), ALU.subtract).then_inc(S["b_k2_lo"].sem, 1)

            def b_x2(u):
                bank = r_ab.wait(dve, u, "mix")
                r_ab.done(dve, u, "recept")
                r_ab.drain(dve.scalar_tensor_tensor(flat(AB.p[:, 0]), AB.t2[:], 1.0, bank[:], ALU.add, ALU.mult), "mix")
                r_ab.done(dve, u, "mix")
                if not (isinstance(u, int) and u == 0):
                    S["c_xb"].wait(dve, u - 1)
                    S["c_xhat"].wait(dve, u - 1)
                dve.tensor_tensor(flat(x2), flat(AB.xb), flat(AB.p[:, 0]), ALU.add).then_inc(S["b_x2"].sem, 1)

            def c_masks(j):
                S["mask_in"].wait(dve, j)
                dve.tensor_scalar(mask_add[:], mask_row[:], 0.0, NEG, ALU.is_equal, ALU.mult).then_inc(S["c_mask"].sem, 1)
                dve.tensor_copy(kcols[:], key_tab[:, seqs(j), :]).then_inc(S["c_kcols"].sem, 1)

            def c_kv(j):
                r_cd.done(dve, j, "k")
                for par in range(2):
                    dve.tensor_scalar(flat(CD.y[:, par]), CD.qk[:, 1, :], cols[:, COL["even"] + par:COL["even"] + par + 1],
                                      None, ALU.mult).then_inc(S["c_kv"].sem, 1)

            def c_max(j, p):
                bank = r_cd.wait(dve, j, f"rough{p}")
                r_cd.drain(dve.tensor_reduce(mx[:, p, :, :].rearrange("q s a -> q (s a)"),
                                             bank[:].rearrange("q (a k) -> q a k", k=P), AX_X, ALU.max), f"rough{p}")

            def c_parts(j):
                r_cd.done(dve, j, f"rough{PAIRS - 2}")
                r_cd.done(dve, j, f"rough{PAIRS - 1}")
                parts_ = mx_parts[:].rearrange("q s a g r -> q (s a) g r")
                for c in range(NC):
                    m = mx[:, 4 * c:4 * c + 4, :, :].rearrange("q g s a -> q (s a) g")
                    dve.tensor_copy(parts_[:, :, :, c], m).then_inc(S["c_part0"].sem, 1)
                for c in range(NC):
                    m = mx[:, 4 * c:4 * c + 4, :, :].rearrange("q g s a -> q (s a) g")
                    S["c_part0"].wait(dve, j, c + 1)
                    dve.tensor_tensor(parts_[:, :, :, NC + c], m, parts_[:, :, :, c], ALU.subtract).then_inc(S["c_part1"].sem, 1)

            def c_y(j, s):
                bank = r_cd.wait(dve, j, f"o_T{s}")
                dve.reciprocal(rz[:, s, :].rearrange("p (h o) -> p h o", o=1),
                               bank[:].rearrange("p (h e) -> p h e", e=HP)[:, :, HD:HD + 1]).then_inc(S["c_rz"].sem, 1)
                S["c_rz"].wait(dve, j, s + 1)
                r_cd.drain(dve.tensor_tensor(CD.t1[:, s * D:(s + 1) * D].rearrange("p (h e) -> p h e", e=HD), heads(bank),
                                             rz[:, s, :].rearrange("p (h o) -> p h o", o=1).broadcast_to([P, H, HD]), ALU.mult), f"o_T{s}")

            def d_h(j, i):
                bank = r_cd.wait(dve, j, f"hidden{i}")
                half_ = slice((i % 2) * 256, (i % 2) * 256 + 256)
                S["d_th"].wait(dve, j, i + 1)
                dve.scalar_tensor_tensor(CD.t1[:, half_], CD.t1[:, half_], 1.0, bank[:, 0:256], ALU.add, ALU.mult).then_inc(S["d_a"].sem, 1)
                S["d_a"].wait(dve, j, i + 1)
                if i >= 2:
                    S["d_h_lo"].wait(dve, j, i - 1)
                r_cd.drain(dve.tensor_tensor(CD.t2[:, half_], bank[:, 256:512], CD.t1[:, half_], ALU.mult), f"hidden{i}")

            def d_x4(j):
                S["d_down"].wait(dve, j)
                S["out_done"].wait_prev(dve, j)
                dve.scalar_tensor_tensor(flat(xo), CD.o[:, 0:2, :, :].rearrange("p a b c -> p (a b c)"), 0.5 / 127.0 ** 3,
                                         flat(CD.xb), ALU.mult, ALU.add).then_inc(S["d_x4"].sem, 1)

            def body(u, j):
                ab, cd = u is not None, j is not None
                if cd:
                    S["b_x2"].wait(dve, j)
                    stats(CD, j, "c", x2)
                    c_masks(j)
                if ab:
                    S["x_in"].wait(dve, u)
                    stats(AB, u, "a", xin)
                if cd:
                    c_kv(j)
                    k_low(CD, j, "c")
                if ab:
                    low(r_ab, u, "ctx_T", "a_c_hi", flat(c_lo), flat(c_hi))
                    low(r_ab, u, "x_T", "a_x_hi", flat(AB.x_lo), flat(AB.x_hi))
                if cd:
                    low(r_cd, j, "x_T", "c_x_hi", flat(CD.x_lo), flat(CD.x_hi))
                if ab:
                    a_gate(u)
                    a_sg(u)
                for p in range(PAIRS):
                    if ab and p % 2 == 0:
                        a_rotate(u, p // 2)
                    if cd:
                        c_max(j, p)
                    if cd and p == 1:
                        qv_low(CD, j, "c")
                if cd:
                    c_parts(j)
                if ab:
                    qv_low(AB, u, "a")
                    k_low(AB, u, "a")
                    for p in range(PAIRS):
                        a_decay(u, p)
                for s in range(GS):
                    if ab:
                        a_ssq(u, s)
                        a_y(u, s)
                    if cd:
                        c_y(j, s)
                if ab:
                    low(r_ab, u, "y_T", "a_y_hi", flat(AB.y[:, 1]), flat(AB.y[:, 0]))
                if cd:
                    low(r_cd, j, "y_T", "c_y_hi", flat(CD.y[:, 1]), flat(CD.y[:, 0]))
                if ab:
                    residual(r_ab, u, AB, "a")
                    r_ab.done(dve, u, "out")
                    stats(AB, u, "b", AB.xb)
                if cd:
                    residual(r_cd, j, CD, "c")
                    r_cd.done(dve, j, "out")
                    stats(CD, j, "d", CD.xb)
                if ab:
                    b_shift(u)
                if cd:
                    low(r_cd, j, "x3_T", "d_x_hi", flat(CD.x_lo), flat(CD.x_hi))
                    d_h(j, 0)
                if ab:
                    b_lows(u)
                if cd:
                    d_h(j, 1)
                if ab:
                    b_k2(u)
                if cd:
                    d_h(j, 2)
                if ab:
                    b_k2_lo(u)
                if cd:
                    d_h(j, 3)
                if ab:
                    b_x2(u)
                if cd:
                    d_h(j, 4)
                    d_h(j, 5)
                    d_x4(j)

            dve.memset(half[:], -0.5).then_inc(dve_const, 1)
            dve.memset(CD.v[:], 0.0).then_inc(dve_const, 1)
            dve.wait_ge(dve_const, 2)
            dve.memset(CD.v[:, :, :, HD:HD + 1], 1.0).then_inc(dve_const, 1)
            dve.memset(xs[:, :, :, 0:1], 0.0).then_inc(dve_const, 1)
            dve.memset(mask_row[:], 1).then_inc(dve_const, 1)
            dve.memset(mx_parts[:], 0.0).then_inc(dve_const, 1)
            dve.wait_ge(load, 16 * NLOAD)
            dve.tensor_copy(ident_bf[:], ident[:]).then_inc(dve_const, 1)
            dve.tensor_copy(flat(sel), flat(AB.p)[:, 0:(NC + 1) * P]).then_inc(dve_const, 1)
            m01, add = CD.t2[0:SEQ, 0:P], CD.t2[0:SEQ, P:2 * P]
            dve.tensor_scalar(m01, CD.t1[0:SEQ, 0:P].bitcast(I32), 0.0, None, ALU.not_equal).then_inc(mask_prep, 1)
            dve.wait_ge(mask_prep, 1)
            dve.tensor_reduce(any_key[:], m01, AX_X, ALU.max).then_inc(mask_prep, 1)
            dve.wait_ge(mask_prep, 2)
            dve.tensor_scalar(add, m01, -1.0, any_key[:, 0:1], ALU.add, ALU.mult).then_inc(mask_prep, 1)
            dve.wait_ge(mask_prep, 3)
            dve.tensor_scalar(add, add, -NEG, None, ALU.mult).then_inc(mask_prep, 1)
            for i, part in enumerate(parts):
                dve.wait_ge(staged[i % 2], 16 * (i // 2 + 1))
                if i >= 2:
                    dve.wait_ge(w_lo_done, i - 1)
                n, w = part[0], width(part)
                src, dst = stage[i % 2][:, 0:w], wf[i % 2][:, 0:w]
                if n == "a_v":
                    per_head = src.rearrange("p (h e) -> p h e", e=HD)
                    dve.tensor_reduce(head_mean[:, :], per_head, AX_X, ALU.add).then_inc(w_centred, 1)
                    dve.wait_ge(w_centred, 1)
                    dve.tensor_scalar(head_mean[:], head_mean[:], 1.0 / HD, None, ALU.mult).then_inc(w_centred, 1)
                    dve.wait_ge(w_centred, 2)
                    dve.tensor_tensor(dst.rearrange("p (h e) -> p h e", e=HD), per_head,
                                      head_mean[:].rearrange("p (h o) -> p h o", o=1).broadcast_to([P, w // HD, HD]),
                                      ALU.subtract).then_inc(w_ready, 1)
                elif n.startswith("d_"):
                    dve.tensor_copy(dst, src.bitcast(I32)).then_inc(w_ready, 1)
                else:
                    dve.tensor_scalar(dst, src, SCALES.get(n, 1.0), None, ALU.mult).then_inc(w_ready, 1)
            dve.wait_ge(w_lo_done, len(parts))
            dve.memset(AB.v[:], 0.0).then_inc(v_zero, 1)
            dve.wait_ge(act_const, NACT_CONST)
            body(0, None)
            with dve.Fori(1, NG) as u:
                body(u, u - 1)
            body(None, NG - 1)

        @block.gpsimd
        def _(pool):
            def norm(ch, it, n, x):
                S[n + "_aggr"].wait(pool, it)
                apart(pool)
                pool.tensor_scalar(ch.negmean[:], ch.mv[:, :, 0], -1.0, 1.0, ALU.mult, ALU.mult).then_inc(S[n + "_small"].sem, 1)
                pool.tensor_scalar(ch.vareps[:], ch.mv[:, :, 1], EPS, 1.0, ALU.add, ALU.mult).then_inc(S[n + "_small"].sem, 1)
                S[n + "_small"].wait(pool, it)
                pool.tensor_tensor(ch.rstd[:], ch.vareps[:], half[:, 0:GS], ALU.pow).then_inc(S[n + "_rstd"].sem, 1)
                S[n + "_rstd"].wait(pool, it)
                apart(pool)
                for s in range(GS):
                    pool.tensor_scalar(ch.t1[:, s * D:(s + 1) * D], x[:, s, :], ch.negmean[:, s:s + 1], ch.rstd[:, s:s + 1],
                                       ALU.add, ALU.mult).then_inc(S[n + "_xhat"].sem, 1)

            def bias_rows(i):
                return bias[:, i:i + 1, :].broadcast_to([P, GS, D])

            def a_xb(u):
                pool.tensor_tensor(AB.xb[:], xin[:], bias_rows(1), ALU.add).then_inc(S["a_xb"].sem, 1)

            def c_xb(j):
                S["d_x4"].wait_prev(pool, j)
                pool.tensor_tensor(CD.xb[:], x2[:], bias_rows(3), ALU.add).then_inc(S["c_xb"].sem, 1)

            def a_rotated(u, i):
                r_ab.done(pool, u, ("q_rot", "k_rot")[i])
                r_ab.done(pool, u, ("q", "k")[i])
                pool.tensor_tensor(AB.qk[:, i, :], AB.t1[:], AB.t2[:], ALU.add).then_inc(S["a_qk"].sem, 1)

            def qv_high(ch, it, n):
                for par in range(2):
                    pool.tensor_scalar(ch.qv_hi[:].rearrange("p c s a t -> p (c s) a t")[:, :, par, :],
                                       ch.qk[:, 0, :].rearrange("p (a t) -> p a t", t=P),
                                       cols[:, COL["even"] + par:COL["even"] + par + 1], 1.0,
                                       ALU.mult, ALU.mult).then_inc(S[n + "_qv_hi"].sem, 1)

            def a_gn(u, s):
                S["a_ssq"].wait(pool, u, s + 1)
                apart(pool)
                pool.tensor_scalar(gn_var[:, s, :], ssq[:, s, :], 1.0 / HD, EPS, ALU.mult, ALU.add).then_inc(S["a_gvar"].sem, 1)
                S["a_gvar"].wait(pool, u, s + 1)
                pool.tensor_tensor(gn_rstd[:, s, :], gn_var[:, s, :], half[:, 0:H], ALU.pow).then_inc(S["a_grstd"].sem, 1)

            def a_yg(u, s):
                r_ab.done(pool, u, f"o_T{s}")
                pool.tensor_tensor(AB.t2[:, s * D:(s + 1) * D], flat(AB.p[:, 0])[:, s * D:(s + 1) * D], sg[:, s, :],
                                   ALU.mult).then_inc(S["a_yg"].sem, 1)

            def c_yb(j):
                r_cd.done(pool, j, "o_T0")
                r_cd.done(pool, j, "o_T1")
                pool.tensor_tensor(CD.t2[:].rearrange("p (s n) -> p s n", s=GS), CD.t1[:].rearrange("p (s n) -> p s n", s=GS),
                                   bias_rows(2), ALU.add).then_inc(S["c_yb"].sem, 1)

            def d_h_lo(j, i):
                S["d_h_hi"].wait(pool, j, i + 1)
                half_ = slice((i % 2) * 256, (i % 2) * 256 + 256)
                pool.tensor_tensor(flat(CD.qv_lo[:, i % 2, 0]), CD.t2[:, half_], raw(flat(CD.qv_hi[:, i % 2, 0])),
                                   ALU.subtract).then_inc(S["d_h_lo"].sem, 1)

            def body(u, j):
                ab, cd = u is not None, j is not None
                if cd:
                    norm(CD, j, "c", x2)
                if ab:
                    norm(AB, u, "a", xin)
                    a_xb(u)
                if cd:
                    r_cd.done(pool, j, "q")
                    apart(pool)
                    qv_high(CD, j, "c")
                    c_xb(j)
                if ab:
                    a_rotated(u, 0)
                    S["a_qk"].wait(pool, u, 1)
                    apart(pool)
                    qv_high(AB, u, "a")
                    a_rotated(u, 1)
                for s in range(GS):
                    if ab:
                        a_gn(u, s)
                        a_yg(u, s)
                if cd:
                    c_yb(j)
                if ab:
                    norm(AB, u, "b", AB.xb)
                if cd:
                    norm(CD, j, "d", CD.xb)
                    for i in range(NHC):
                        d_h_lo(j, i)

            for i, part in enumerate(parts):
                pool.wait_ge(w_hi_done, i + 1)
                pool.tensor_tensor(part[2], wf[i % 2][:, 0:width(part)], raw(part[1]), ALU.subtract).then_inc(w_lo_done, 1)
            pool.wait_ge(dve_const, NDVE_CONST)
            pool.wait_ge(load, 16 * NLOAD)
            body(0, None)
            with pool.Fori(1, NG) as u:
                body(u, u - 1)
            body(None, NG - 1)


def constants():
    import numpy as np
    f = np.float32
    half_ = HD // 2
    base = (np.arange(0, HD, 2, dtype=f) + f(0.4 * HD)) / f(1.4 * HD)
    power = (np.arange(-(P // 2), P - P // 2, dtype=f) / f(512.0))[:, None]
    scale = (base[None, :] ** power).astype(f)
    inv_freq = (f(1.0) / f(10000.0) ** (np.arange(half_, dtype=f) / f(half_))).astype(f)
    ang = (np.arange(P, dtype=f)[:, None] * inv_freq[None, :]).astype(f)
    sin, cos = np.sin(ang).astype(f), np.cos(ang).astype(f)
    sign = np.where(np.arange(HD) % 2 == 0, f(-1), f(1))
    rope = np.zeros((P, 4, P), f)
    for i, sc in enumerate((scale, (f(1.0) / scale).astype(f))):
        c = np.repeat(cos * sc, 2, axis=1)
        s = np.repeat(sin * sc, 2, axis=1) * sign
        rope[:, 2 * i, :] = np.tile(c.T, (P // HD, 1))
        rope[:, 2 * i + 1, :] = np.tile(s.T, (P // HD, 1))
    gamma = f(1.0) - np.exp(np.linspace(np.log(1.0 / 32.0), np.log(1.0 / 512.0), H).astype(f)).astype(f)
    dist = np.arange(P)[None, :] - np.arange(P)[:, None]
    decay = np.where(dist[:, None, :] >= 0, gamma[None, :, None] ** np.maximum(dist, 0)[:, None, :].astype(f), f(0)).astype(f)
    parity = np.zeros((P, 2), f)
    parity[np.arange(P) // HD % 2 == 0, 0] = 1
    parity[np.arange(P) // HD % 2 == 1, 1] = 1
    sel = np.zeros((4, 32, NC + 1, P), f)
    for c in range(NC):
        sel[:, c, c] = sel[:, NC + c, c] = -1
    sel[:, 0, NC] = 1
    return {"rope": rope, "decay": decay, "ident": np.eye(P, dtype=f), "parity": parity, "sel": sel.reshape(P, -1)}


def kernel(**inputs):
    import numpy as np
    import concourse.bacc as bacc
    from concourse.bass_utils import run_bass_kernel_spmd

    def heads_out(w):
        return np.ascontiguousarray(np.transpose(w, (1, 0, 2)).reshape(D, D))

    def swap_pairs(w):
        return np.ascontiguousarray(w.reshape(D, D // 2, 2)[:, :, ::-1].reshape(D, D))

    def turned(w):
        return np.ascontiguousarray(np.transpose(w))

    i = {k: np.asarray(v) for k, v in inputs.items()}
    arrays = {
        "x": i["x"], "ctx": i["ctx_1024"], "mask": i["mask_Bx1x1xS2_if1"],
        "a_q": heads_out(i["L0_xattn_W_Q"]), "a_q_rot": swap_pairs(heads_out(i["L0_xattn_W_Q"])),
        "a_k": heads_out(i["L0_xattn_W_K"]), "a_k_rot": swap_pairs(heads_out(i["L0_xattn_W_K"])),
        "a_v": heads_out(i["L0_xattn_W_V"]), "a_gate": turned(i["L0_xattn_g_w"]), "a_out": turned(i["L0_xattn_out_w"]),
        "gate_b": i["L0_xattn_g_b"], "out_b": i["L0_xattn_out_b"],
        "b_r": turned(i["L0_ffn_W_r"]), "b_k": turned(i["L0_ffn_W_k"]), "b_v": turned(i["L0_ffn_W_v"]),
        "mu_r": i["L0_ffn_mu_r"], "mu_k": i["L0_ffn_mu_k"],
        "c_q": turned(i["L1_xattn_Wq"]), "c_k": turned(i["L1_xattn_Wk"]), "c_v": turned(i["L1_xattn_Wv"]),
        "c_out": turned(i["L1_xattn_Wo"]), "bq": i["L1_xattn_bq"], "bk": i["L1_xattn_bk"],
        "bv": i["L1_xattn_bv"], "bo": i["L1_xattn_bo"],
        "d_gate": turned(i["L1_ffn_w_gate"]), "d_up": turned(i["L1_ffn_w_up"]), "d_down": turned(i["L1_ffn_w_down"]),
        **constants(),
    }
    nc = bacc.Bacc("TRN2", target_bir_lowering=False, num_devices=1)
    io = {n: nc.dram_tensor(f"in_{n}", a.shape, mybir.dt.from_np(a.dtype), kind="ExternalInput").ap() for n, a in arrays.items()}
    io["out"] = nc.dram_tensor("out_x", (SEQ, P, D), F32, kind="ExternalOutput").ap()
    build(nc, io)
    r = run_bass_kernel_spmd(nc, [{f"in_{n}": a for n, a in arrays.items()}], core_ids=[0])
    return r.results[0]["out_x"]
```

```python
from contextlib import ExitStack

import concourse.bass as bass
from concourse import mybir

P = 128
SEQ = 64
GS = 2
NG = SEQ // GS
D = 256
NC = D // P
H = 16
HD = D // H
HP = 2 * HD
PAIRS = H // 2
QUADS = H // 4
HID = 768
NHC = HID // P
EPS = 1e-5
NEWTON = 3
NEG = -1e9

F32 = mybir.dt.float32
F32R = mybir.dt.float32r
BF16 = mybir.dt.bfloat16
I32 = mybir.dt.int32
ALU = mybir.AluOpType
ACT = mybir.ActivationFunctionType
AX_X = mybir.AxisListType.X

AB_ITEMS = (["x_T", "ctx_T", "q", "q_rot", "k", "k_rot", "v"] + [f"score{p}" for p in range(PAIRS - 2)]
            + ["gate", f"score{PAIRS - 2}", f"score{PAIRS - 1}", "c_k", "o_T0", "o_T1", "y_T", "out", "x1_T", "recept", "key", "c_v", "mix"])
CD_ITEMS = (["x_T", "q"] + [f"rough{p}" for p in range(PAIRS)] + ["max_T"]
            + [f"score{p}" for p in range(PAIRS)] + ["o_T0", "o_T1", "y_T", "out", "x3_T"]
            + [f"hidden{i}" for i in range(NHC)])
if len(AB_ITEMS) % 2 or len(CD_ITEMS) % 2:
    raise ValueError("each ring bank has the same number of items in every iteration")


class Signal:

    def __init__(self, sem, per):
        self.sem, self.per = sem, per

    def wait(self, eng, it, count=None):
        eng.wait_ge(self.sem, it * self.per + (self.per if count is None else count))

    def wait_prev(self, eng, it, count=None):
        if isinstance(it, int) and it == 0:
            return
        eng.wait_ge(self.sem, (it - 1) * self.per + (self.per if count is None else count))


class Ring:

    def __init__(self, banks, filled, drained, items):
        self.banks, self.filled, self.drained = banks, filled, drained
        self.where = {n: (i % 2, i // 2) for i, n in enumerate(items)}
        self.per = len(items) // 2

    def bank(self, name):
        return self.banks[self.where[name][0]]

    def claim(self, pe, it, name):
        b, k = self.where[name]
        if isinstance(it, int) and it * self.per + k == 0:
            return self.banks[b]
        pe.wait_ge(self.drained[b], it * self.per + k)
        return self.banks[b]

    def wait(self, eng, it, name):
        b, k = self.where[name]
        eng.wait_ge(self.filled[b], it * self.per + k + 1)
        return self.banks[b]

    def done(self, eng, it, name):
        b, k = self.where[name]
        eng.wait_ge(self.drained[b], it * self.per + k + 1)

    def fill(self, ins, name):
        ins.then_inc(self.filled[self.where[name][0]], 1)

    def drain(self, ins, name):
        ins.then_inc(self.drained[self.where[name][0]], 1)


def build(nc, io):
    ctx = ExitStack()
    with ctx:
        def sb(name, shape, dt=F32):
            return ctx.enter_context(nc.sbuf_tensor(name, shape, dt))

        def psum(name, shape, dt=F32):
            return ctx.enter_context(nc.psum_tensor(name, shape, dt))

        def sem(name):
            return ctx.enter_context(nc.semaphore(name))

        names = ["a_q", "a_q_rot", "a_k", "a_k_rot", "a_v", "a_gate", "a_out",
                 "b_r", "b_k", "b_v", "c_q", "c_k", "c_v", "c_out"]
        W = {n: (sb(f"{n}_hi", [P, NC, D], F32R), sb(f"{n}_lo", [P, NC, D], F32R)) for n in names}
        W["d_gate"] = (sb("d_gate_hi", [P, NC, HID], F32R), sb("d_gate_lo", [P, NC, HID], F32R))
        W["d_up"] = (sb("d_up_hi", [P, NC, HID], F32R), sb("d_up_lo", [P, NC, HID], F32R))
        W["d_down"] = (sb("d_down_hi", [P, NHC, D], F32R), sb("d_down_lo", [P, NHC, D], F32R))
        decay = sb("decay", [P, H, P])
        rope = sb("rope", [P, 4, P])
        ident = sb("ident", [P, P])
        ident_bf = sb("ident_bf", [P, P], BF16)
        sel = sb("sel", [P, PAIRS + 1, P], BF16)
        bias = sb("bias", [P, 4, D])
        cols = sb("cols", [P, 10])
        half = sb("half", [P, 2 * H])
        key_tab = sb("key_tab", [P, SEQ, 2])
        kcols = sb("kcols", [P, GS, 2])
        any_key = sb("any_key", [SEQ, 1])
        head_mean = sb("head_mean", [P, NC * H])
        bq4 = sb("bq4", [P, NC])
        mask_row = sb("mask_row", [P, GS * P], I32)
        mask_add = sb("mask_add", [P, GS * P], BF16)
        COL = {"mu_r": 0, "mu_k": 2, "bq": 4, "bk": 6, "even": 8, "odd": 9}

        xin = sb("xin", [P, GS, D])
        cin = sb("cin", [P, GS, D])
        c_hi = sb("c_hi", [P, NC, GS * P], F32R)
        c_lo = sb("c_lo", [P, NC, GS * P], F32R)

        class Norm:

            def __init__(self, n):
                self.stats = sb(f"{n}_stats", [P, GS, 6])
                self.mv = sb(f"{n}_mv", [P, GS, 2])
                self.negmean = sb(f"{n}_negmean", [P, GS])
                self.vareps = sb(f"{n}_vareps", [P, GS])
                self.rstd = sb(f"{n}_rstd", [P, GS])

        class Chain:
            def __init__(self, n):
                self.x_hi = sb(f"{n}_x_hi", [P, NC, GS * P], F32R)
                self.x_lo = sb(f"{n}_x_lo", [P, NC, GS * P], F32R)
                self.t1 = sb(f"{n}_t1", [P, 2 * D])
                self.t2 = sb(f"{n}_t2", [P, 2 * D])
                self.qk = sb(f"{n}_qk", [P, 2, 2 * D])
                self.qv_hi = sb(f"{n}_qv_hi", [P, NC, GS, 2, P], F32R)
                self.qv_lo = sb(f"{n}_qv_lo", [P, NC, GS, 2, P], F32R)
                self.k_hi = sb(f"{n}_k_hi", [P, NC, GS * P], F32R)
                self.k_lo = sb(f"{n}_k_lo", [P, NC, GS * P], F32R)
                self.o_sb = [self.qk[:, 0, :], self.qk[:, 1, :] if n == "ab" else self.t2[:]]
                self.v = sb(f"{n}_v", [P, GS, H, HP])
                self.p = sb(f"{n}_p", [P, 2, GS, 2, P])
                self.y = sb(f"{n}_y", [P, 2, NC, GS * P], F32R)
                self.xb = sb(f"{n}_xb", [P, GS, D])
                self.norm = Norm(n)
                self.ring = [psum(f"{n}_ring{i}", [P, 512]) for i in range(2)]
                self.o = psum(f"{n}_o", [P, QUADS, GS, P])

        AB, CD = Chain("ab"), Chain("cd")
        A0 = Norm("a0")
        sg = sb("sg", [P, GS, D])
        x2 = sb("x2", [P, GS, D])
        xs = sb("xs", [P, NC, GS, P + 1])
        ssq = sb("ssq", [P, GS, H])
        gn_var = sb("gn_var", [P, GS, H])
        gn_rstd = sb("gn_rstd", [P, GS, H])
        gn_neg_half = sb("gn_neg_half", [P, GS, H])
        gn_sq = sb("gn_sq", [P, GS, H])
        one_half = sb("one_half", [P, GS, H])
        q_hi = sb("q_hi", [P, NC, GS * P], F32R)
        mx = sb("mx", [P, PAIRS, GS, 2])
        mx_parts = sb("mx_parts", [P, GS, 2, 4, 32], BF16)
        m_T = sb("m_T", [P, GS, 2, P], BF16)
        rz = sb("rz", [P, GS, H])
        xo = CD.p[:, 0].rearrange("p s a q -> p s (a q)")

        r_ab = Ring(AB.ring, [sem("ab_filled0"), sem("ab_filled1")], [sem("ab_drained0"), sem("ab_drained1")], AB_ITEMS)
        r_cd = Ring(CD.ring, [sem("cd_filled0"), sem("cd_filled1")], [sem("cd_drained0"), sem("cd_drained1")], CD_ITEMS)

        def signals(**per):
            return {n: Signal(sem(n), k) for n, k in per.items()}

        S = signals(
            x_in=16, ctx_in=16, a_stats=2, a_aggr=2, a_small=2, a_rstd=1, a_xhat=2, a_x_hi=1, a_c_hi=1,
            a_th=1, a_sg=1, a_xb=1, a_qk=2, a_qv_hi=2, a_qv_lo=2, a_k_hi=1, a_k_lo=1,
            a_pv=PAIRS, a_osb=2, a_sq=2, a_ssq=2, a_gvar=1, a_ghalf=1,
            a_grstd=NEWTON + 1, a_gsq=NEWTON, a_gprod=NEWTON, a_gsum=NEWTON, a_yg=2, a_y_hi=1,
            b_stats=2, b_aggr=2, b_small=2, b_rstd=1, b_xhat=2, b_d=1, b_xr=2, b_xk=2,
            b_xr_hi=1, b_xr_lo=1, b_xk_hi=1, b_xk_lo=1, b_relu=1, b_k2_hi=1, b_k2_lo=1, b_x2=1,
            mask_in=16, c_mask=1, c_kcols=1, c_stats=2, c_aggr=2, c_small=2, c_rstd=1, c_xhat=2, c_x_hi=1,
            c_k_hi=1, c_k_lo=1, c_kv=2, c_q_hi=NC, c_q_lo=1, c_qv_hi=2, c_qv_lo=2, c_xb=1,
            c_part0=NC, c_part1=NC, c_pv=PAIRS, c_osb=2, c_rz=2, c_y_hi=1,
            d_stats=2, d_aggr=2, d_small=2, d_rstd=1, d_xhat=2, d_x_hi=1,
            d_th=NHC, d_a=NHC, d_h_hi=NHC, d_h_lo=NHC, d_down=NHC, d_x4=1, out_done=16,
        )
        load = sem("load")
        staged = [sem("staged0"), sem("staged1")]
        w_ready, w_centred, w_hi_done, w_lo_done = sem("w_ready"), sem("w_centred"), sem("w_hi_done"), sem("w_lo_done")
        mask_prep, mask_T, dve_const, act_const = sem("mask_prep"), sem("mask_T"), sem("dve_const"), sem("act_const")
        v_zero = sem("v_zero")
        NLOAD, NDVE_CONST, NACT_CONST = 15, 10, 3

        def flat(x):
            n = len(x.shape)
            names_ = "abcdef"[:n - 1]
            return x[:].rearrange("p " + " ".join(names_) + " -> p (" + " ".join(names_) + ")")

        def raw(x):
            return x.bitcast(F32)

        stepped = sem("stepped")

        def apart(eng):
            eng.sem_inc(stepped, 1)

        stage = [AB.qk[:].rearrange("p a n -> p (a n)"), CD.qk[:].rearrange("p a n -> p (a n)")]
        wf = [flat(AB.v), flat(CD.p)]
        SCALES = {"a_out": 0.5, "b_v": 0.5, "c_q": 0.25}
        parts = []
        for n, (hi, lo) in W.items():
            src = io[n].rearrange("(c p) n -> p c n", p=P)
            if n in names:
                parts.append((n, flat(hi), flat(lo), src))
            else:
                for c in range(hi.shape[1]):
                    parts.append((n, hi[:, c, :], lo[:, c, :], src[:, c:c + 1, :]))

        def width(part):
            return part[3].shape[1] * part[3].shape[2]

        block = ctx.enter_context(nc.Block())

        def seqs(u):
            return slice(GS * u, GS * u + GS) if isinstance(u, int) else bass.ds(GS * u, GS)

        @block.sync
        def _(sp):
            for dst, src in ((decay[:], io["decay"]), (rope[:], io["rope"]), (ident[:], io["ident"]),
                             (cols[:, COL["even"]:COL["odd"] + 1], io["parity"]),
                             (cols[:, 0:2], io["mu_r"].rearrange("(c p) -> p c", p=P)),
                             (cols[:, 2:4], io["mu_k"].rearrange("(c p) -> p c", p=P)),
                             (cols[:, 4:6], io["bq"].rearrange("(c p) -> p c", p=P)),
                             (cols[:, 6:8], io["bk"].rearrange("(c p) -> p c", p=P)),
                             (bias[:, 0, :], io["gate_b"].partition_broadcast(P)),
                             (bias[:, 1, :], io["out_b"].partition_broadcast(P)),
                             (bias[:, 2, :], io["bv"].partition_broadcast(P)),
                             (bias[:, 3, :], io["bo"].partition_broadcast(P)),
                             (CD.t1[0:SEQ, 0:P].bitcast(I32), io["mask"].rearrange("b i j k -> b (i j k)")),
                             (flat(AB.p)[:, 0:PAIRS * P], io["sel"][:, 0:PAIRS * P]),
                             (CD.t2[:, 0:P], io["sel"][:, PAIRS * P:(PAIRS + 1) * P])):
                sp.dma_start(dst, src, allow_slow_non_contiguous=True).then_inc(load, 16)
            for i, part in enumerate(parts):
                if i >= 2:
                    sp.wait_ge(w_ready, i - 1)
                dst = stage[i % 2][:, 0:width(part)]
                dst = dst.bitcast(I32) if part[0].startswith("d_") else dst
                sp.dma_start(dst.rearrange("p (c n) -> p c n", c=part[3].shape[1]), part[3]).then_inc(staged[i % 2], 16)

            def loads(u):
                S["a_xb"].wait_prev(sp, u)
                S["a_xhat"].wait_prev(sp, u)
                sp.dma_start(xin[:], io["x"][seqs(u)].rearrange("s p c -> p s c")).then_inc(S["x_in"].sem, 16)
                if not (isinstance(u, int) and u == 0):
                    r_ab.wait(sp, u - 1, "ctx_T")
                sp.dma_start(cin[:], io["ctx"][seqs(u)].rearrange("s p c -> p s c")).then_inc(S["ctx_in"].sem, 16)

            def mask(j):
                S["c_mask"].wait_prev(sp, j)
                sp.dma_start(mask_row[0:1, :], io["mask"][seqs(j)].rearrange("(o s) i j k -> o (s i j k)", o=1)).then_inc(S["mask_in"].sem, 16)

            def store(j):
                S["d_x4"].wait(sp, j)
                sp.dma_start(io["out"][seqs(j)].rearrange("s p c -> p s c"), xo).then_inc(S["out_done"].sem, 16)

            loads(0)
            loads(1)
            sp.wait_ge(dve_const, NDVE_CONST)
            mask(0)
            with sp.Fori(1, NG - 1) as u:
                loads(u + 1)
                mask(u)
                store(u - 1)
            mask(NG - 1)
            store(NG - 2)
            store(NG - 1)
            S["out_done"].wait(sp, NG - 1)

        @block.tensor
        def _(pe):
            def wterms(n, c, cols_):
                hi, lo = W[n]
                return hi[:, c, cols_], lo[:, c, cols_]

            def channel_major(ring, it, item, n, x_hi, x_lo, width=NC, base=0, out=None):
                bank = ring.claim(pe, it, item) if out is None else out
                ins = None
                for m in range(width):
                    dst = bank[:, m * 256:(m + 1) * 256]
                    k = 0
                    for c in range(NC):
                        w_hi, w_lo = wterms(n, c, slice(base + m * P, base + (m + 1) * P))
                        for w, x in ((w_hi, x_hi), (w_lo, x_hi), (w_hi, x_lo)):
                            ins = pe.matmul(dst, w, x[:, c, :], start=(k == 0), stop=(k == 3 * NC - 1))
                            k += 1
                return ins

            def token_major(bank, n, x_hi, x_lo, chunks=NC):
                ins = None
                for s in range(GS):
                    dst = bank[:, s * D:(s + 1) * D]
                    k = 0
                    for c in range(chunks):
                        w_hi, w_lo = wterms(n, c, slice(0, D))
                        xh, xl = x_hi[:, c, s * P:(s + 1) * P], x_lo[:, c, s * P:(s + 1) * P]
                        for x, w in ((xh, w_hi), (xl, w_hi), (xh, w_lo)):
                            ins = pe.matmul(dst, x, w, start=(k == 0), stop=(k == 3 * chunks - 1))
                            k += 1
                return ins

            def transposes(bank, src):
                ins = None
                for c in range(NC):
                    for s in range(GS):
                        o = (c * GS + s) * P
                        ins = pe.transpose(bank[:, o:o + P], src[:, s * D + c * P:s * D + (c + 1) * P], ident[:])
                return ins

            def scores(ch, bank, p, add_max):
                c, g = p // 4, p % 4
                r = slice(32 * g, 32 * g + 32)
                ins = None
                for s in range(GS):
                    dst = bank[:, s * 256:(s + 1) * 256]
                    t = slice(s * P, (s + 1) * P)
                    q_h = ch.qv_hi[r, c, s, :, :].rearrange("p a q -> p (a q)")
                    q_l = ch.qv_lo[r, c, s, :, :].rearrange("p a q -> p (a q)")
                    terms = ((ch.k_hi[r, c, t], q_h), (ch.k_lo[r, c, t], q_h), (ch.k_hi[r, c, t], q_l))
                    for i, (k, q) in enumerate(terms):
                        ins = pe.matmul(dst, k, q, start=(i == 0), stop=(i == 2 and not add_max))
                    if add_max:
                        ins = pe.matmul(dst, sel[:, p, :], m_T[:, s, :, :].rearrange("r a q -> r (a q)"),
                                        start=False, stop=True)
                return ins

            def attend(ch, p):
                ins = None
                for s in range(GS):
                    for par in range(2):
                        h = 2 * p + par
                        j, quad = h % 4, h // 4
                        ins = pe.matmul(ch.o[32 * j:32 * j + 32, quad, s, :], ch.v[:, s, h, :],
                                        ch.p[:, p % 2, s, par, :], start=True, stop=True, skip_group_check=True,
                                        tile_position=(0, 32 * j))
                return ins

            def heads_to_tokens(ch, bank, s):
                ins = None
                for quad in range(QUADS):
                    src = ch.o_sb[quad // 2][:, (quad % 2 * GS + s) * P:(quad % 2 * GS + s + 1) * P]
                    ins = pe.transpose(bank[:, quad * P:(quad + 1) * P], src, ident[:])
                return ins

            def ctx_T(u):
                bank = r_ab.claim(pe, u, "ctx_T")
                S["ctx_in"].wait(pe, u)
                r_ab.fill(transposes(bank, cin[:].rearrange("p s c -> p (s c)")), "ctx_T")

            def x_T(u):
                bank = r_ab.claim(pe, u, "x_T")
                S["a_xhat"].wait(pe, u)
                r_ab.fill(transposes(bank, sg[:].rearrange("p s c -> p (s c)")), "x_T")

            def a_v(u):
                bank = r_ab.claim(pe, u, "v")
                r_ab.done(pe, u, "ctx_T")
                r_ab.fill(token_major(bank, "a_v", c_hi, c_lo), "v")

            def a_gate(u):
                bank = r_ab.claim(pe, u, "gate")
                r_ab.fill(token_major(bank, "a_gate", AB.x_hi, AB.x_lo), "gate")

            def a_proj(u, item, n, hi, lo):
                if item == "q":
                    r_ab.done(pe, u, "x_T")
                r_ab.fill(channel_major(r_ab, u, item, n, hi, lo), item)

            def a_score(u, p):
                bank = r_ab.claim(pe, u, f"score{p}")
                if p == 0:
                    S["a_qv_hi"].wait(pe, u)
                    S["a_qv_lo"].wait(pe, u)
                    S["a_k_hi"].wait(pe, u)
                    S["a_k_lo"].wait(pe, u)
                r_ab.fill(scores(AB, bank, p, False), f"score{p}")

            def a_attend(u, p):
                r_ab.done(pe, u, f"score{p}")
                if p == 0:
                    r_ab.done(pe, u, "v")
                    S["a_osb"].wait_prev(pe, u, 1)
                if p == PAIRS // 2:
                    S["a_osb"].wait_prev(pe, u, 2)
                attend(AB, p).then_inc(S["a_pv"].sem, 1)

            def a_o_T(u, s):
                bank = r_ab.claim(pe, u, f"o_T{s}")
                S["a_osb"].wait(pe, u)
                r_ab.fill(heads_to_tokens(AB, bank, s), f"o_T{s}")

            def a_y_T(u):
                bank = r_ab.claim(pe, u, "y_T")
                S["a_yg"].wait(pe, u)
                r_ab.fill(transposes(bank, AB.t2[:]), "y_T")

            def a_out(u):
                bank = r_ab.claim(pe, u, "out")
                r_ab.done(pe, u, "y_T")
                r_ab.fill(token_major(bank, "a_out", AB.y[:, 0], AB.y[:, 1]), "out")

            def x1_T(u):
                bank = r_ab.claim(pe, u, "x1_T")
                S["b_xhat"].wait(pe, u)
                r_ab.fill(transposes(bank, AB.t1[:]), "x1_T")

            def b_recept(u):
                bank = r_ab.claim(pe, u, "recept")
                S["b_xr_hi"].wait(pe, u)
                S["b_xr_lo"].wait(pe, u)
                r_ab.fill(token_major(bank, "b_r", AB.x_hi, AB.x_lo), "recept")

            def b_key(u):
                S["b_xk_hi"].wait(pe, u)
                S["b_xk_lo"].wait(pe, u)
                r_ab.fill(channel_major(r_ab, u, "key", "b_k", AB.k_hi, AB.k_lo), "key")

            def b_mix(u):
                bank = r_ab.claim(pe, u, "mix")
                S["b_k2_hi"].wait(pe, u)
                S["b_k2_lo"].wait(pe, u)
                r_ab.fill(token_major(bank, "b_v", AB.y[:, 0], AB.y[:, 1]), "mix")

            def c_k(u):
                r_ab.fill(channel_major(r_ab, u, "c_k", "c_k", c_hi, c_lo), "c_k")

            def c_v(u):
                bank = r_ab.claim(pe, u, "c_v")
                r_ab.fill(token_major(bank, "c_v", c_hi, c_lo), "c_v")

            def c_x_T(j):
                bank = r_cd.claim(pe, j, "x_T")
                S["c_xhat"].wait(pe, j)
                r_cd.fill(transposes(bank, CD.qk[:, 0, :]), "x_T")

            def c_q(j):
                r_cd.done(pe, j, "x_T")
                r_cd.fill(channel_major(r_cd, j, "q", "c_q", CD.x_hi, CD.x_lo), "q")

            def c_rough(j, p):
                bank = r_cd.claim(pe, j, f"rough{p}")
                if p == 0:
                    S["c_q_hi"].wait(pe, j)
                    S["c_kv"].wait(pe, j)
                    S["c_mask"].wait(pe, j)
                c, g = p // 4, p % 4
                r = slice(32 * g, 32 * g + 32)
                ins = None
                for s in range(GS):
                    dst = bank[:, s * 256:(s + 1) * 256]
                    kv = CD.y[r, :, :, :].rearrange("p v c (s k) -> p v c s k", s=GS)[:, :, c, s, :]
                    pe.matmul(dst, q_hi[r, c, s * P:(s + 1) * P], kv, start=True, stop=False)
                    ins = pe.matmul(dst, sel[:, PAIRS, :], mask_add[:, s * P:(s + 1) * P].rearrange("r (o k) -> r o k", o=1)
                                    .broadcast_to([P, 2, P]), start=False, stop=True)
                r_cd.fill(ins, f"rough{p}")

            def c_max_T(j):
                bank = r_cd.claim(pe, j, "max_T")
                S["c_part1"].wait(pe, j)
                bf = bank[:].bitcast(BF16)
                for s in range(GS):
                    for par in range(2):
                        o = (s * 2 + par) * P
                        ins = pe.transpose(bf[:, o:o + P],
                                           mx_parts[:, s, par, :, :].rearrange("q a b -> q (a b)"), ident_bf[:])
                r_cd.fill(ins, "max_T")

            def c_score(j, p):
                bank = r_cd.claim(pe, j, f"score{p}")
                if p == 0:
                    S["c_qv_hi"].wait(pe, j)
                    S["c_qv_lo"].wait(pe, j)
                    S["c_k_hi"].wait(pe, j)
                    S["c_k_lo"].wait(pe, j)
                    r_cd.done(pe, j, "max_T")
                r_cd.fill(scores(CD, bank, p, True), f"score{p}")

            def c_attend(j, p):
                r_cd.done(pe, j, f"score{p}")
                if p == 0:
                    r_ab.done(pe, j, "c_v")
                    S["d_x4"].wait_prev(pe, j)
                if p == PAIRS // 2:
                    S["c_osb"].wait_prev(pe, j, 2)
                attend(CD, p).then_inc(S["c_pv"].sem, 1)

            def c_o_T(j, s):
                bank = r_cd.claim(pe, j, f"o_T{s}")
                S["c_osb"].wait(pe, j)
                r_cd.fill(heads_to_tokens(CD, bank, s), f"o_T{s}")

            def c_y_T(j):
                bank = r_cd.claim(pe, j, "y_T")
                r_cd.done(pe, j, "o_T0")
                r_cd.done(pe, j, "o_T1")
                r_cd.fill(transposes(bank, CD.t1[:]), "y_T")

            def c_out(j):
                bank = r_cd.claim(pe, j, "out")
                r_cd.done(pe, j, "y_T")
                r_cd.fill(token_major(bank, "c_out", CD.y[:, 0], CD.y[:, 1]), "out")

            def x3_T(j):
                bank = r_cd.claim(pe, j, "x3_T")
                S["d_xhat"].wait(pe, j)
                r_cd.fill(transposes(bank, CD.t1[:]), "x3_T")

            def d_hidden(j, i):
                item = f"hidden{i}"
                bank = r_cd.claim(pe, j, item)
                if i == 0:
                    r_cd.done(pe, j, "x3_T")
                channel_major(r_cd, j, item, "d_gate", CD.x_hi, CD.x_lo, 1, i * P, bank[:, 0:256])
                r_cd.fill(channel_major(r_cd, j, item, "d_up", CD.x_hi, CD.x_lo, 1, i * P, bank[:, 256:512]), item)

            def d_down(j, i):
                S["d_h_hi"].wait(pe, j, i + 1)
                S["d_h_lo"].wait(pe, j, i + 1)
                acc = CD.o[:, 0:2, :, :].rearrange("p a b c -> p (a b c)")
                w_hi, w_lo = W["d_down"][0][:, i, :], W["d_down"][1][:, i, :]
                for s in range(GS):
                    h_hi = CD.qv_hi[:, i % 2, 0, :, :].rearrange("p a b -> p (a b)")[:, s * P:(s + 1) * P]
                    h_lo = CD.qv_lo[:, i % 2, 0, :, :].rearrange("p a b -> p (a b)")[:, s * P:(s + 1) * P]
                    for k, (h, w) in enumerate(((h_hi, w_hi), (h_lo, w_hi), (h_hi, w_lo))):
                        ins = pe.matmul(acc[:, s * D:(s + 1) * D], h, w,
                                        start=(i == 0 and s == 0 and k == 0), stop=(i == NHC - 1 and k == 2),
                                        skip_group_check=True)
                ins.then_inc(S["d_down"].sem, 1)

            def body(u, j, i):
                ab, c, d = u is not None, j is not None, i is not None
                if ab:
                    x_T(u)
                    ctx_T(u)
                    a_proj(u, "q", "a_q", AB.x_hi, AB.x_lo)
                    a_proj(u, "q_rot", "a_q_rot", AB.x_hi, AB.x_lo)
                    a_proj(u, "k", "a_k", c_hi, c_lo)
                    a_proj(u, "k_rot", "a_k_rot", c_hi, c_lo)
                if d:
                    x3_T(i)
                if ab:
                    a_v(u)
                if d:
                    d_hidden(i, 0)
                    d_hidden(i, 1)
                for p in range(PAIRS):
                    if ab:
                        a_score(u, p)
                    if ab and p > 0:
                        a_attend(u, p - 1)
                    if d and p < NHC:
                        d_down(i, p)
                    if d and p + 2 < NHC:
                        d_hidden(i, p + 2)
                    if c and p == 4:
                        c_x_T(j)
                    if ab and p == 5:
                        a_gate(u)
                    if c and p == 6:
                        c_q(j)
                if c:
                    c_rough(j, 0)
                if ab:
                    a_attend(u, PAIRS - 1)
                    c_k(u)
                if c:
                    c_rough(j, 1)
                    c_rough(j, 2)
                if ab:
                    a_o_T(u, 0)
                    a_o_T(u, 1)
                if c:
                    for p in range(3, PAIRS):
                        c_rough(j, p)
                if c:
                    c_max_T(j)
                if ab:
                    a_y_T(u)
                for p in range(PAIRS + 1):
                    if c and p < PAIRS:
                        c_score(j, p)
                    if ab and p == 1:
                        a_out(u)
                    if c and p > 0:
                        c_attend(j, p - 1)
                    if ab and p == 4:
                        x1_T(u)
                    if ab and p == PAIRS - 1:
                        b_recept(u)
                if ab:
                    b_key(u)
                if c:
                    c_o_T(j, 0)
                    c_o_T(j, 1)
                if ab:
                    c_v(u)
                if c:
                    c_y_T(j)
                if ab:
                    b_mix(u)
                if c:
                    c_out(j)

            pe.wait_ge(load, 16 * NLOAD)
            pe.wait_ge(mask_prep, 4)
            pe.transpose(AB.ring[0][:, 0:SEQ], CD.t2[0:SEQ, 0:P], ident[0:SEQ, 0:SEQ])
            pe.transpose(AB.ring[0][:, SEQ:2 * SEQ], CD.t2[0:SEQ, P:2 * P], ident[0:SEQ, 0:SEQ]).then_inc(mask_T, 1)
            pe.wait_ge(w_lo_done, len(parts))
            pe.wait_ge(dve_const, NDVE_CONST)
            pe.wait_ge(act_const, NACT_CONST)
            body(0, None, None)
            body(1, 0, None)
            with pe.Fori(2, NG - 1) as u:
                body(u, u - 1, u - 2)
            body(NG - 1, NG - 2, NG - 3)
            body(None, NG - 1, NG - 2)
            body(None, None, NG - 1)

        @block.scalar
        def _(act):
            def ctx_hi(u):
                bank = r_ab.wait(act, u, "ctx_T")
                act.activation(flat(c_hi), bank[:], ACT.Copy).then_inc(S["a_c_hi"].sem, 1)

            def x_hi(ring, it, item, ch, sig):
                bank = ring.wait(act, it, item)
                act.activation(flat(ch.x_hi), bank[:], ACT.Copy).then_inc(S[sig].sem, 1)

            def values(u):
                bank = r_ab.wait(act, u, "v")
                r_ab.drain(act.activation(AB.v[:, :, :, 0:HD].rearrange("p s h e -> p (s h) e"),
                                          bank[:].rearrange("p (a e) -> p a e", e=HD), ACT.Copy), "v")

            def by_parity(dst, src, par):
                return act.activation(dst[:].rearrange("p c s a t -> p (c s) a t")[:, :, par, :],
                                      src.rearrange("p (a t) -> p a t", t=P), ACT.Copy,
                                      scale=cols[:, COL["even"] + par:COL["even"] + par + 1])

            def qv_high(ch, it, n):
                if n == "a":
                    S["a_qk"].wait(act, it, 1)
                else:
                    r_cd.done(act, it, "q")
                    S["d_down"].wait_prev(act, it)
                for par in range(2):
                    by_parity(ch.qv_hi, ch.qk[:, 0, :], par).then_inc(S[n + "_qv_hi"].sem, 1)

            def c_qv_lo(j):
                S["c_q_lo"].wait(act, j)
                for par in range(2):
                    by_parity(CD.qv_lo, CD.t2[:], par).then_inc(S["c_qv_lo"].sem, 1)

            def a_th(u):
                r_ab.done(act, u, "gate")
                act.activation(AB.t2[:], AB.t1[:], ACT.Tanh, scale=0.5).then_inc(S["a_th"].sem, 1)

            def a_k_hi(u):
                S["a_qk"].wait(act, u, 2)
                act.activation(flat(AB.k_hi), AB.qk[:, 1, :], ACT.Copy).then_inc(S["a_k_hi"].sem, 1)

            def osb(ch, n, it, half_):
                S[n + "_pv"].wait(act, it, 4 * half_ + 4)
                act.activation(ch.o_sb[half_], ch.o[:, 2 * half_:2 * half_ + 2, :, :].rearrange("p a b c -> p (a b c)"),
                               ACT.Copy).then_inc(S[n + "_osb"].sem, 1)

            def a_sq(u, s):
                bank = r_ab.wait(act, u, f"o_T{s}")
                S["a_sg"].wait(act, u)
                act.activation(AB.t1[:, s * D:(s + 1) * D].rearrange("p (h e) -> p h e", e=HD),
                               bank[:].rearrange("p (h e) -> p h e", e=HP)[:, :, 0:HD],
                               ACT.Square).then_inc(S["a_sq"].sem, 1)

            def y_hi(ring, it, ch, n):
                bank = ring.wait(act, it, "y_T")
                act.activation(flat(ch.y[:, 0]), bank[:], ACT.Copy).then_inc(S[n + "_y_hi"].sem, 1)

            def b_xs(u):
                bank = r_ab.wait(act, u, "x1_T")
                r_ab.drain(act.activation(xs[:, :, :, 1:P + 1].rearrange("p c s t -> p (c s) t"),
                                          bank[:].rearrange("p (a t) -> p a t", t=P), ACT.Copy), "x1_T")

            def b_xr_hi(u):
                S["b_xr"].wait(act, u)
                act.activation(flat(AB.x_hi), AB.t2[:], ACT.Copy).then_inc(S["b_xr_hi"].sem, 1)

            def b_xk_hi(u):
                S["b_xk"].wait(act, u)
                act.activation(flat(AB.k_hi), AB.qk[:, 0, :], ACT.Copy).then_inc(S["b_xk_hi"].sem, 1)

            def b_th(u):
                bank = r_ab.wait(act, u, "recept")
                S["b_xr_lo"].wait(act, u)
                r_ab.drain(act.activation(AB.t2[:], bank[:], ACT.Tanh, scale=0.5), "recept")

            def b_relu(u):
                bank = r_ab.wait(act, u, "key")
                act.activation(AB.qk[:, 1, :], bank[:], ACT.Relu).then_inc(S["b_relu"].sem, 1)

            def b_k2_hi(u):
                r_ab.done(act, u, "key")
                act.activation(flat(AB.y[:, 0]), AB.t1[:], ACT.Copy).then_inc(S["b_k2_hi"].sem, 1)

            def plus_bias(ring, j, item, slot, col):
                bank = ring.wait(act, j, item)
                for m in range(NC):
                    ins = act.activation(CD.qk[:, slot, m * 256:(m + 1) * 256], bank[:, m * 256:(m + 1) * 256],
                                         ACT.Identity, bias=col[:, m:m + 1])
                ring.drain(ins, item)

            def c_k_hi(j):
                r_ab.done(act, j, "c_k")
                act.activation(flat(CD.k_hi), CD.qk[:, 1, :], ACT.Copy).then_inc(S["c_k_hi"].sem, 1)

            def c_q_hi(j):
                bank = r_cd.wait(act, j, "q")
                for m in range(NC):
                    act.activation(q_hi[:, m, :], bank[:, m * 256:(m + 1) * 256], ACT.Identity,
                                   bias=bq4[:, m:m + 1]).then_inc(S["c_q_hi"].sem, 1)

            def c_mT(j):
                bank = r_cd.wait(act, j, "max_T")
                r_cd.drain(act.activation(flat(m_T), bank[:].bitcast(BF16)[:, 0:GS * 2 * P], ACT.Copy), "max_T")

            def c_exp(j, p):
                bank = r_cd.wait(act, j, f"score{p}")
                if p == 0:
                    S["c_kcols"].wait(act, j)
                    S["out_done"].wait_prev(act, j)
                if p >= 2:
                    S["c_pv"].wait(act, j, p - 1)
                for s in range(GS):
                    ins = act.activation(flat(CD.p[:, p % 2, s]), bank[:, s * 256:(s + 1) * 256],
                                         ACT.Exp, bias=kcols[:, s, 1:2], scale=kcols[:, s, 0:1])
                r_cd.drain(ins, f"score{p}")

            def d_th(j, i):
                bank = r_cd.wait(act, j, f"hidden{i}")
                act.activation(CD.t1[:, (i % 2) * 256:(i % 2) * 256 + 256], bank[:, 0:256], ACT.Tanh,
                               scale=0.5 / 127.0).then_inc(S["d_th"].sem, 1)

            def d_h_hi(j, i):
                r_cd.done(act, j, f"hidden{i}")
                if i >= 2:
                    S["d_down"].wait(act, j, i - 1)
                act.activation(flat(CD.qv_hi[:, i % 2, 0]), CD.t2[:, (i % 2) * 256:(i % 2) * 256 + 256],
                               ACT.Copy).then_inc(S["d_h_hi"].sem, 1)

            def body(u, j, i):
                ab, c, d = u is not None, j is not None, i is not None
                if ab:
                    x_hi(r_ab, u, "x_T", AB, "a_x_hi")
                    ctx_hi(u)
                    qv_high(AB, u, "a")
                if d:
                    x_hi(r_cd, i, "x3_T", CD, "d_x_hi")
                if c:
                    c_k_hi(j)
                if ab:
                    a_k_hi(u)
                if d:
                    d_th(i, 0)
                    d_h_hi(i, 0)
                if ab:
                    values(u)
                if d:
                    for k in range(1, NHC):
                        d_th(i, k)
                        d_h_hi(i, k)
                if c:
                    x_hi(r_cd, j, "x_T", CD, "c_x_hi")
                if ab:
                    osb(AB, "a", u, 0)
                    a_th(u)
                if c:
                    c_q_hi(j)
                if ab:
                    osb(AB, "a", u, 1)
                if c:
                    plus_bias(r_cd, j, "q", 0, bq4)
                if ab:
                    plus_bias(r_ab, u, "c_k", 1, cols[:, COL["bk"]:COL["bk"] + 2])
                if ab:
                    a_sq(u, 0)
                    a_sq(u, 1)
                if c:
                    qv_high(CD, j, "c")
                if c:
                    c_qv_lo(j)
                    c_mT(j)
                if ab:
                    y_hi(r_ab, u, AB, "a")
                for p in range(PAIRS):
                    if c:
                        c_exp(j, p)
                    if ab and p == 4:
                        b_xs(u)
                    if c and p == 5:
                        osb(CD, "c", j, 0)
                    if ab and p == 6:
                        b_xr_hi(u)
                        b_xk_hi(u)
                if ab:
                    b_th(u)
                if c:
                    osb(CD, "c", j, 1)
                if ab:
                    b_relu(u)
                    b_k2_hi(u)
                if c:
                    y_hi(r_cd, j, CD, "c")

            act.wait_ge(load, 16 * NLOAD)
            for i, part in enumerate(parts):
                act.wait_ge(w_ready, i + 1)
                act.activation(part[1], wf[i % 2][:, 0:width(part)], ACT.Copy).then_inc(w_hi_done, 1)
            act.wait_ge(mask_T, 1)
            for i in range(2):
                act.activation(key_tab[:, :, i], AB.ring[0][:, i * SEQ:(i + 1) * SEQ], ACT.Copy).then_inc(act_const, 1)
            act.activation(bq4[:], cols[:, COL["bq"]:COL["bq"] + 2], ACT.Copy, scale=0.25).then_inc(act_const, 1)
            act.wait_ge(act_const, NACT_CONST)
            act.wait_ge(v_zero, 1)
            body(0, None, None)
            body(1, 0, None)
            with act.Fori(2, NG - 1) as u:
                body(u, u - 1, u - 2)
            body(NG - 1, NG - 2, NG - 3)
            body(None, NG - 1, NG - 2)
            body(None, None, NG - 1)

        @block.vector
        def _(dve):
            def stats(nm, it, n, x):
                for s in range(GS):
                    dve.bn_stats(nm.stats[:, s, :], x[:, s, :]).then_inc(S[n + "_stats"].sem, 1)
                for s in range(GS):
                    S[n + "_stats"].wait(dve, it, s + 1)
                    apart(dve)
                    dve.bn_aggr(nm.mv[:, s, :], nm.stats[:, s, :]).then_inc(S[n + "_aggr"].sem, 1)

            def low(ring, it, item, sig, lo, hi):
                bank = ring.wait(dve, it, item)
                S[sig].wait(dve, it)
                ring.drain(dve.tensor_tensor(lo, bank[:], raw(hi), ALU.subtract), item)

            def table(i):
                return rope[:, i:i + 1, :].broadcast_to([P, 2 * GS, P])

            def rows(x):
                return x.rearrange("p (a t) -> p a t", t=P)

            def a_gate(u):
                bank = r_ab.wait(dve, u, "gate")
                r_ab.drain(dve.tensor_tensor(AB.t1[:].rearrange("p (s n) -> p s n", s=GS), bank[:].rearrange("p (s n) -> p s n", s=GS),
                                             bias[:, 0:1, :].broadcast_to([P, GS, D]), ALU.add), "gate")

            def a_sg(u):
                S["a_th"].wait(dve, u)
                dve.scalar_tensor_tensor(flat(sg), AB.t2[:], 1.0, AB.t1[:], ALU.add, ALU.mult).then_inc(S["a_sg"].sem, 1)

            def a_rotate(u, i):
                item = ("q", "q_rot", "k", "k_rot")[i]
                bank = r_ab.wait(dve, u, item)
                if i == 2:
                    S["a_qk"].wait(dve, u, 1)
                dst = AB.t2 if i % 2 else AB.t1
                r_ab.drain(dve.tensor_tensor(rows(dst[:]), rows(bank[:]), table(i), ALU.mult), item)

            def a_qv_low(u):
                for par in range(2):
                    S["a_qv_hi"].wait(dve, u, par + 1)
                    dve.scalar_tensor_tensor(AB.qv_lo[:].rearrange("p c s a t -> p (c s) a t")[:, :, par, :],
                                             rows(AB.qk[:, 0, :]), cols[:, COL["even"] + par:COL["even"] + par + 1],
                                             raw(AB.qv_hi[:]).rearrange("p c s a t -> p (c s) a t")[:, :, par, :],
                                             ALU.mult, ALU.subtract).then_inc(S["a_qv_lo"].sem, 1)

            def c_values(u):
                bank = r_ab.wait(dve, u, "c_v")
                if not (isinstance(u, int) and u == 0):
                    r_cd.wait(dve, u - 1, "o_T1")
                r_ab.drain(dve.tensor_tensor(CD.v[:, :, :, 0:HD], bank[:].rearrange("p (s h e) -> p s h e", s=GS, e=HD),
                                             bias[:, 2:3, :].rearrange("p o (h e) -> p o h e", e=HD).broadcast_to([P, GS, H, HD]),
                                             ALU.add), "c_v")

            def k_low(ch, it, n):
                S[n + "_k_hi"].wait(dve, it)
                dve.tensor_tensor(flat(ch.k_lo), ch.qk[:, 1, :], raw(flat(ch.k_hi)), ALU.subtract).then_inc(S[n + "_k_lo"].sem, 1)

            def a_decay(u, p):
                bank = r_ab.wait(dve, u, f"score{p}")
                if p >= 2:
                    S["a_pv"].wait(dve, u, p - 1)
                r_ab.drain(dve.tensor_tensor(AB.p[:, p % 2].rearrange("k s a q -> k s (a q)"),
                                             bank[:].rearrange("k (s n) -> k s n", s=GS),
                                             decay[:, 2 * p:2 * p + 2, :].rearrange("k (o a) q -> k o (a q)", o=1).broadcast_to([P, GS, 2 * P]),
                                             ALU.mult), f"score{p}")

            def heads(bank):
                return bank[:].rearrange("p (h e) -> p h e", e=HP)[:, :, 0:HD]

            def a_ssq(u, s):
                S["a_sq"].wait(dve, u, s + 1)
                dve.tensor_reduce(ssq[:, s, :], AB.t1[:, s * D:(s + 1) * D].rearrange("p (h e) -> p h e", e=HD),
                                  AX_X, ALU.add).then_inc(S["a_ssq"].sem, 1)

            def a_y(u, s):
                bank = r_ab.wait(dve, u, f"o_T{s}")
                S["a_grstd"].wait(dve, u)
                r_ab.drain(dve.tensor_tensor(flat(AB.p[:, 0])[:, s * D:(s + 1) * D].rearrange("p (h e) -> p h e", e=HD), heads(bank),
                                             gn_rstd[:, s, :].rearrange("p (h o) -> p h o", o=1).broadcast_to([P, H, HD]), ALU.mult), f"o_T{s}")

            def residual(ring, it, ch, n):
                bank = ring.wait(dve, it, "out")
                S[n + "_xb"].wait(dve, it)
                ring.drain(dve.tensor_tensor(flat(ch.xb), bank[:], flat(ch.xb), ALU.add), "out")

            def b_shift(u):
                r_ab.done(dve, u, "x1_T")
                now = xs[:, :, :, 1:P + 1].rearrange("p c s t -> p (c s) t")
                before = xs[:, :, :, 0:P].rearrange("p c s t -> p (c s) t")
                dve.tensor_tensor(rows(AB.t1[:]), now, before, ALU.subtract).then_inc(S["b_d"].sem, 1)
                S["b_d"].wait(dve, u)
                for dst, mu, sig in ((AB.t2[:], "mu_r", "b_xr"), (AB.qk[:, 0, :], "mu_k", "b_xk")):
                    for c in range(NC):
                        dve.scalar_tensor_tensor(rows(dst)[:, GS * c:GS * c + GS, :], rows(AB.t1[:])[:, GS * c:GS * c + GS, :],
                                                 cols[:, COL[mu] + c:COL[mu] + c + 1], xs[:, c, :, 0:P],
                                                 ALU.mult, ALU.add).then_inc(S[sig].sem, 1)

            def b_lows(u):
                S["b_xr_hi"].wait(dve, u)
                dve.tensor_tensor(flat(AB.x_lo), AB.t2[:], raw(flat(AB.x_hi)), ALU.subtract).then_inc(S["b_xr_lo"].sem, 1)
                S["b_xk_hi"].wait(dve, u)
                dve.tensor_tensor(flat(AB.k_lo), AB.qk[:, 0, :], raw(flat(AB.k_hi)), ALU.subtract).then_inc(S["b_xk_lo"].sem, 1)

            def b_k2(u):
                bank = r_ab.wait(dve, u, "key")
                S["b_relu"].wait(dve, u)
                r_ab.drain(dve.tensor_tensor(AB.t1[:], bank[:], AB.qk[:, 1, :], ALU.mult), "key")

            def b_k2_lo(u):
                S["b_k2_hi"].wait(dve, u)
                dve.tensor_tensor(flat(AB.y[:, 1]), AB.t1[:], raw(flat(AB.y[:, 0])), ALU.subtract).then_inc(S["b_k2_lo"].sem, 1)

            def b_x2(u):
                bank = r_ab.wait(dve, u, "mix")
                r_ab.done(dve, u, "recept")
                r_ab.drain(dve.scalar_tensor_tensor(flat(AB.p[:, 0]), AB.t2[:], 1.0, bank[:], ALU.add, ALU.mult), "mix")
                r_ab.done(dve, u, "mix")
                if not (isinstance(u, int) and u == 0):
                    S["c_xb"].wait(dve, u - 1)
                    S["c_xhat"].wait(dve, u - 1)
                dve.tensor_tensor(flat(x2), flat(AB.xb), flat(AB.p[:, 0]), ALU.add).then_inc(S["b_x2"].sem, 1)

            def c_masks(j):
                S["mask_in"].wait(dve, j)
                dve.tensor_scalar(mask_add[:], mask_row[:], 0.0, NEG, ALU.is_equal, ALU.mult).then_inc(S["c_mask"].sem, 1)
                dve.tensor_copy(kcols[:], key_tab[:, seqs(j), :]).then_inc(S["c_kcols"].sem, 1)

            def c_kv(j):
                r_ab.done(dve, j, "c_k")
                for par in range(2):
                    dve.tensor_scalar(flat(CD.y[:, par]), CD.qk[:, 1, :], cols[:, COL["even"] + par:COL["even"] + par + 1],
                                      None, ALU.mult).then_inc(S["c_kv"].sem, 1)

            def c_max(j, p):
                bank = r_cd.wait(dve, j, f"rough{p}")
                r_cd.drain(dve.tensor_reduce(mx[:, p, :, :].rearrange("q s a -> q (s a)"),
                                             bank[:].rearrange("q (a k) -> q a k", k=P), AX_X, ALU.max), f"rough{p}")

            def c_parts(j):
                r_cd.done(dve, j, f"rough{PAIRS - 2}")
                r_cd.done(dve, j, f"rough{PAIRS - 1}")
                parts_ = mx_parts[:].rearrange("q s a g r -> q (s a) g r")
                for c in range(NC):
                    m = mx[:, 4 * c:4 * c + 4, :, :].rearrange("q g s a -> q (s a) g")
                    dve.tensor_copy(parts_[:, :, :, c], m).then_inc(S["c_part0"].sem, 1)
                for c in range(NC):
                    m = mx[:, 4 * c:4 * c + 4, :, :].rearrange("q g s a -> q (s a) g")
                    S["c_part0"].wait(dve, j, c + 1)
                    dve.tensor_tensor(parts_[:, :, :, NC + c], m, parts_[:, :, :, c], ALU.subtract).then_inc(S["c_part1"].sem, 1)

            def c_y(j, s):
                bank = r_cd.wait(dve, j, f"o_T{s}")
                dve.reciprocal(rz[:, s, :].rearrange("p (h o) -> p h o", o=1),
                               bank[:].rearrange("p (h e) -> p h e", e=HP)[:, :, HD:HD + 1]).then_inc(S["c_rz"].sem, 1)
                S["c_rz"].wait(dve, j, s + 1)
                r_cd.drain(dve.tensor_tensor(CD.t1[:, s * D:(s + 1) * D].rearrange("p (h e) -> p h e", e=HD), heads(bank),
                                             rz[:, s, :].rearrange("p (h o) -> p h o", o=1).broadcast_to([P, H, HD]), ALU.mult), f"o_T{s}")

            def d_h(j, i):
                bank = r_cd.wait(dve, j, f"hidden{i}")
                half_ = slice((i % 2) * 256, (i % 2) * 256 + 256)
                S["d_th"].wait(dve, j, i + 1)
                dve.scalar_tensor_tensor(CD.t1[:, half_], CD.t1[:, half_], 1.0, bank[:, 0:256], ALU.add, ALU.mult).then_inc(S["d_a"].sem, 1)
                S["d_a"].wait(dve, j, i + 1)
                if i >= 2:
                    S["d_h_lo"].wait(dve, j, i - 1)
                r_cd.drain(dve.tensor_tensor(CD.t2[:, half_], bank[:, 256:512], CD.t1[:, half_], ALU.mult), f"hidden{i}")

            def d_x4(j):
                S["d_down"].wait(dve, j)
                S["out_done"].wait_prev(dve, j)
                dve.scalar_tensor_tensor(xo.rearrange("p s n -> p (s n)"), CD.o[:, 0:2, :, :].rearrange("p a b c -> p (a b c)"), 0.5 / 127.0 ** 3,
                                         flat(CD.xb), ALU.mult, ALU.add).then_inc(S["d_x4"].sem, 1)

            def first_stats(u):
                S["x_in"].wait(dve, u)
                stats(A0, u, "a", xin)

            def body(u, j, i, n=None):
                ab, c, d = u is not None, j is not None, i is not None
                if d:
                    residual(r_cd, i, CD, "c")
                if ab:
                    low(r_ab, u, "x_T", "a_x_hi", flat(AB.x_lo), flat(AB.x_hi))
                if d:
                    r_cd.done(dve, i, "out")
                    stats(CD.norm, i, "d", CD.xb)
                if ab:
                    low(r_ab, u, "ctx_T", "a_c_hi", flat(c_lo), flat(c_hi))
                    for k in range(4):
                        a_rotate(u, k)
                if d:
                    low(r_cd, i, "x3_T", "d_x_hi", flat(CD.x_lo), flat(CD.x_hi))
                if ab:
                    a_qv_low(u)
                if d:
                    d_h(i, 0)
                if ab:
                    k_low(AB, u, "a")
                if d:
                    d_h(i, 1)
                for p in range(PAIRS):
                    if ab:
                        a_decay(u, p)
                    if d and p + 2 < NHC:
                        d_h(i, p + 2)
                    if c and p == 0:
                        S["b_x2"].wait(dve, j)
                        stats(CD.norm, j, "c", x2)
                        c_masks(j)
                    if c and p == 2:
                        k_low(CD, j, "c")
                    if c and p == 3:
                        c_kv(j)
                    if c and p == 4:
                        low(r_cd, j, "x_T", "c_x_hi", flat(CD.x_lo), flat(CD.x_hi))
                    if ab and p == 5:
                        a_gate(u)
                if ab:
                    a_sg(u)
                if c:
                    c_max(j, 0)
                    c_max(j, 1)
                if ab:
                    a_ssq(u, 0)
                    a_ssq(u, 1)
                if c:
                    for p in range(2, 6):
                        c_max(j, p)
                if ab:
                    a_y(u, 0)
                    a_y(u, 1)
                if c:
                    c_max(j, 6)
                    c_max(j, 7)
                    c_parts(j)
                if d:
                    d_x4(i)
                if ab:
                    low(r_ab, u, "y_T", "a_y_hi", flat(AB.y[:, 1]), flat(AB.y[:, 0]))
                    residual(r_ab, u, AB, "a")
                    r_ab.done(dve, u, "out")
                    stats(AB.norm, u, "b", AB.xb)
                if n is not None:
                    first_stats(n)
                if ab:
                    b_shift(u)
                    b_lows(u)
                    b_k2(u)
                if c:
                    c_y(j, 0)
                if ab:
                    b_k2_lo(u)
                if c:
                    c_y(j, 1)
                if ab:
                    c_values(u)
                if c:
                    low(r_cd, j, "y_T", "c_y_hi", flat(CD.y[:, 1]), flat(CD.y[:, 0]))
                if ab:
                    b_x2(u)

            dve.memset(half[:], -0.5).then_inc(dve_const, 1)
            dve.memset(one_half[:], 1.5).then_inc(dve_const, 1)
            dve.memset(CD.v[:], 0.0).then_inc(dve_const, 1)
            dve.wait_ge(dve_const, 3)
            dve.memset(CD.v[:, :, :, HD:HD + 1], 1.0).then_inc(dve_const, 1)
            dve.memset(xs[:, :, :, 0:1], 0.0).then_inc(dve_const, 1)
            dve.memset(mask_row[:], 1).then_inc(dve_const, 1)
            dve.memset(mx_parts[:], 0.0).then_inc(dve_const, 1)
            dve.wait_ge(load, 16 * NLOAD)
            dve.tensor_copy(ident_bf[:], ident[:]).then_inc(dve_const, 1)
            dve.tensor_copy(flat(sel)[:, 0:PAIRS * P], flat(AB.p)[:, 0:PAIRS * P]).then_inc(dve_const, 1)
            dve.tensor_copy(sel[:, PAIRS, :], CD.t2[:, 0:P]).then_inc(dve_const, 1)
            dve.wait_ge(dve_const, NDVE_CONST)
            m01, add = CD.t2[0:SEQ, 0:P], CD.t2[0:SEQ, P:2 * P]
            dve.tensor_scalar(m01, CD.t1[0:SEQ, 0:P].bitcast(I32), 0.0, None, ALU.not_equal).then_inc(mask_prep, 1)
            dve.wait_ge(mask_prep, 1)
            dve.tensor_reduce(any_key[:], m01, AX_X, ALU.max).then_inc(mask_prep, 1)
            dve.wait_ge(mask_prep, 2)
            dve.tensor_scalar(add, m01, -1.0, any_key[:, 0:1], ALU.add, ALU.mult).then_inc(mask_prep, 1)
            dve.wait_ge(mask_prep, 3)
            dve.tensor_scalar(add, add, -NEG, None, ALU.mult).then_inc(mask_prep, 1)
            for i, part in enumerate(parts):
                dve.wait_ge(staged[i % 2], 16 * (i // 2 + 1))
                if i >= 2:
                    dve.wait_ge(w_lo_done, i - 1)
                n, w = part[0], width(part)
                src, dst = stage[i % 2][:, 0:w], wf[i % 2][:, 0:w]
                if n == "a_v":
                    per_head = src.rearrange("p (h e) -> p h e", e=HD)
                    dve.tensor_reduce(head_mean[:, :], per_head, AX_X, ALU.add).then_inc(w_centred, 1)
                    dve.wait_ge(w_centred, 1)
                    dve.tensor_scalar(head_mean[:], head_mean[:], 1.0 / HD, None, ALU.mult).then_inc(w_centred, 1)
                    dve.wait_ge(w_centred, 2)
                    dve.tensor_tensor(dst.rearrange("p (h e) -> p h e", e=HD), per_head,
                                      head_mean[:].rearrange("p (h o) -> p h o", o=1).broadcast_to([P, w // HD, HD]),
                                      ALU.subtract).then_inc(w_ready, 1)
                elif n.startswith("d_"):
                    dve.tensor_copy(dst, src.bitcast(I32)).then_inc(w_ready, 1)
                else:
                    dve.tensor_scalar(dst, src, SCALES.get(n, 1.0), None, ALU.mult).then_inc(w_ready, 1)
            dve.wait_ge(w_lo_done, len(parts))
            dve.memset(AB.v[:], 0.0).then_inc(v_zero, 1)
            dve.wait_ge(act_const, NACT_CONST)
            first_stats(0)
            body(0, None, None, 1)
            body(1, 0, None, 2)
            with dve.Fori(2, NG - 1) as u:
                body(u, u - 1, u - 2, u + 1)
            body(NG - 1, NG - 2, NG - 3)
            body(None, NG - 1, NG - 2)
            body(None, None, NG - 1)

        @block.gpsimd
        def _(pool):
            def norm(nm, it, n, x, dst):
                S[n + "_aggr"].wait(pool, it)
                apart(pool)
                pool.tensor_scalar(nm.negmean[:], nm.mv[:, :, 0], -1.0, 1.0, ALU.mult, ALU.mult).then_inc(S[n + "_small"].sem, 1)
                pool.tensor_scalar(nm.vareps[:], nm.mv[:, :, 1], EPS, 1.0, ALU.add, ALU.mult).then_inc(S[n + "_small"].sem, 1)
                S[n + "_small"].wait(pool, it)
                pool.tensor_tensor(nm.rstd[:], nm.vareps[:], half[:, 0:GS], ALU.pow).then_inc(S[n + "_rstd"].sem, 1)
                S[n + "_rstd"].wait(pool, it)
                apart(pool)
                for s in range(GS):
                    pool.tensor_scalar(dst[:, s * D:(s + 1) * D], x[:, s, :], nm.negmean[:, s:s + 1], nm.rstd[:, s:s + 1],
                                       ALU.add, ALU.mult).then_inc(S[n + "_xhat"].sem, 1)

            def bias_rows(i):
                return bias[:, i:i + 1, :].broadcast_to([P, GS, D])

            def a_xb(u):
                pool.tensor_tensor(AB.xb[:], xin[:], bias_rows(1), ALU.add).then_inc(S["a_xb"].sem, 1)

            def c_xb(j):
                S["d_x4"].wait_prev(pool, j)
                pool.tensor_tensor(CD.xb[:], x2[:], bias_rows(3), ALU.add).then_inc(S["c_xb"].sem, 1)

            def a_rotated(u, i):
                r_ab.done(pool, u, ("q_rot", "k_rot")[i])
                r_ab.done(pool, u, ("q", "k")[i])
                pool.tensor_tensor(AB.qk[:, i, :], AB.t1[:], AB.t2[:], ALU.add).then_inc(S["a_qk"].sem, 1)

            def c_q_lo(j):
                S["c_q_hi"].wait(pool, j)
                r_cd.done(pool, j, "q")
                S["d_h_lo"].wait_prev(pool, j)
                pool.tensor_tensor(CD.t2[:], CD.qk[:, 0, :], raw(flat(q_hi)), ALU.subtract).then_inc(S["c_q_lo"].sem, 1)

            def a_gn(u):
                S["a_ssq"].wait(pool, u)
                apart(pool)
                pool.tensor_scalar(gn_var[:], ssq[:], 1.0 / HD, EPS, ALU.mult, ALU.add).then_inc(S["a_gvar"].sem, 1)
                pool.tensor_scalar(gn_neg_half[:], ssq[:], -0.5 / HD, -0.5 * EPS, ALU.mult, ALU.add).then_inc(S["a_ghalf"].sem, 1)
                S["a_gvar"].wait(pool, u)
                apart(pool)
                pool.tensor_scalar(gn_rstd[:].bitcast(I32), gn_var[:].bitcast(I32), -0.5, float(0x5F3759DF), ALU.mult, ALU.add).then_inc(S["a_grstd"].sem, 1)
                S["a_ghalf"].wait(pool, u)
                for k in range(NEWTON):
                    S["a_grstd"].wait(pool, u, k + 1)
                    pool.tensor_tensor(gn_sq[:], gn_rstd[:], gn_rstd[:], ALU.mult).then_inc(S["a_gsq"].sem, 1)
                    S["a_gsq"].wait(pool, u, k + 1)
                    pool.tensor_tensor(gn_var[:], gn_sq[:], gn_neg_half[:], ALU.mult).then_inc(S["a_gprod"].sem, 1)
                    S["a_gprod"].wait(pool, u, k + 1)
                    pool.tensor_tensor(gn_sq[:], gn_var[:], one_half[:], ALU.add).then_inc(S["a_gsum"].sem, 1)
                    S["a_gsum"].wait(pool, u, k + 1)
                    pool.tensor_tensor(gn_rstd[:], gn_sq[:], gn_rstd[:], ALU.mult).then_inc(S["a_grstd"].sem, 1)

            def a_yg(u, s):
                r_ab.done(pool, u, f"o_T{s}")
                pool.tensor_tensor(AB.t2[:, s * D:(s + 1) * D], flat(AB.p[:, 0])[:, s * D:(s + 1) * D], sg[:, s, :],
                                   ALU.mult).then_inc(S["a_yg"].sem, 1)

            def d_h_lo(j, i):
                S["d_h_hi"].wait(pool, j, i + 1)
                half_ = slice((i % 2) * 256, (i % 2) * 256 + 256)
                pool.tensor_tensor(flat(CD.qv_lo[:, i % 2, 0]), CD.t2[:, half_], raw(flat(CD.qv_hi[:, i % 2, 0])),
                                   ALU.subtract).then_inc(S["d_h_lo"].sem, 1)

            def body(u, j, i, n=None):
                ab, c, d = u is not None, j is not None, i is not None
                if d:
                    norm(CD.norm, i, "d", CD.xb, CD.t1[:])
                if ab:
                    a_rotated(u, 0)
                    a_rotated(u, 1)
                if d:
                    d_h_lo(i, 0)
                    d_h_lo(i, 1)
                    d_h_lo(i, 2)
                if c:
                    norm(CD.norm, j, "c", x2, CD.qk[:, 0, :])
                if ab:
                    a_xb(u)
                if d:
                    d_h_lo(i, 3)
                    d_h_lo(i, 4)
                    d_h_lo(i, 5)
                if c:
                    c_q_lo(j)
                if ab:
                    a_gn(u)
                    a_yg(u, 0)
                    a_yg(u, 1)
                if c:
                    c_xb(j)
                if ab:
                    norm(AB.norm, u, "b", AB.xb, AB.t1[:])
                if n is not None:
                    norm(A0, n, "a", xin, flat(sg))

            for i, part in enumerate(parts):
                pool.wait_ge(w_hi_done, i + 1)
                pool.tensor_tensor(part[2], wf[i % 2][:, 0:width(part)], raw(part[1]), ALU.subtract).then_inc(w_lo_done, 1)
            pool.wait_ge(dve_const, NDVE_CONST)
            pool.wait_ge(load, 16 * NLOAD)
            norm(A0, 0, "a", xin, flat(sg))
            body(0, None, None, 1)
            body(1, 0, None, 2)
            with pool.Fori(2, NG - 1) as u:
                body(u, u - 1, u - 2, u + 1)
            body(NG - 1, NG - 2, NG - 3)
            body(None, NG - 1, NG - 2)
            body(None, None, NG - 1)


def constants():
    import numpy as np
    f = np.float32
    half_ = HD // 2
    base = (np.arange(0, HD, 2, dtype=f) + f(0.4 * HD)) / f(1.4 * HD)
    power = (np.arange(-(P // 2), P - P // 2, dtype=f) / f(512.0))[:, None]
    scale = (base[None, :] ** power).astype(f)
    inv_freq = (f(1.0) / f(10000.0) ** (np.arange(half_, dtype=f) / f(half_))).astype(f)
    ang = (np.arange(P, dtype=f)[:, None] * inv_freq[None, :]).astype(f)
    sin, cos = np.sin(ang).astype(f), np.cos(ang).astype(f)
    sign = np.where(np.arange(HD) % 2 == 0, f(-1), f(1))
    rope = np.zeros((P, 4, P), f)
    for i, sc in enumerate((scale, (f(1.0) / scale).astype(f))):
        c = np.repeat(cos * sc, 2, axis=1)
        s = np.repeat(sin * sc, 2, axis=1) * sign
        rope[:, 2 * i, :] = np.tile(c.T, (P // HD, 1))
        rope[:, 2 * i + 1, :] = np.tile(s.T, (P // HD, 1))
    gamma = f(1.0) - np.exp(np.linspace(np.log(1.0 / 32.0), np.log(1.0 / 512.0), H).astype(f)).astype(f)
    dist = np.arange(P)[None, :] - np.arange(P)[:, None]
    decay = np.where(dist[:, None, :] >= 0, gamma[None, :, None] ** np.maximum(dist, 0)[:, None, :].astype(f), f(0)).astype(f)
    parity = np.zeros((P, 2), f)
    parity[np.arange(P) // HD % 2 == 0, 0] = 1
    parity[np.arange(P) // HD % 2 == 1, 1] = 1
    sel = np.zeros((P, PAIRS + 1, P), f)
    for p in range(PAIRS):
        row = 32 * (p % 4) + p // 4
        sel[row, p] = sel[row + NC, p] = -1
    sel[0, PAIRS] = 1
    return {"rope": rope, "decay": decay, "ident": np.eye(P, dtype=f), "parity": parity, "sel": sel.reshape(P, -1)}


def kernel(**inputs):
    import numpy as np
    import concourse.bacc as bacc
    from concourse.bass_utils import run_bass_kernel_spmd

    def heads_out(w):
        return np.ascontiguousarray(np.transpose(w, (1, 0, 2)).reshape(D, D))

    def swap_pairs(w):
        return np.ascontiguousarray(w.reshape(D, D // 2, 2)[:, :, ::-1].reshape(D, D))

    def turned(w):
        return np.ascontiguousarray(np.transpose(w))

    i = {k: np.asarray(v) for k, v in inputs.items()}
    arrays = {
        "x": i["x"], "ctx": i["ctx_1024"], "mask": i["mask_Bx1x1xS2_if1"],
        "a_q": heads_out(i["L0_xattn_W_Q"]), "a_q_rot": swap_pairs(heads_out(i["L0_xattn_W_Q"])),
        "a_k": heads_out(i["L0_xattn_W_K"]), "a_k_rot": swap_pairs(heads_out(i["L0_xattn_W_K"])),
        "a_v": heads_out(i["L0_xattn_W_V"]), "a_gate": turned(i["L0_xattn_g_w"]), "a_out": turned(i["L0_xattn_out_w"]),
        "gate_b": i["L0_xattn_g_b"], "out_b": i["L0_xattn_out_b"],
        "b_r": turned(i["L0_ffn_W_r"]), "b_k": turned(i["L0_ffn_W_k"]), "b_v": turned(i["L0_ffn_W_v"]),
        "mu_r": i["L0_ffn_mu_r"], "mu_k": i["L0_ffn_mu_k"],
        "c_q": turned(i["L1_xattn_Wq"]), "c_k": turned(i["L1_xattn_Wk"]), "c_v": turned(i["L1_xattn_Wv"]),
        "c_out": turned(i["L1_xattn_Wo"]), "bq": i["L1_xattn_bq"], "bk": i["L1_xattn_bk"],
        "bv": i["L1_xattn_bv"], "bo": i["L1_xattn_bo"],
        "d_gate": turned(i["L1_ffn_w_gate"]), "d_up": turned(i["L1_ffn_w_up"]), "d_down": turned(i["L1_ffn_w_down"]),
        **constants(),
    }
    nc = bacc.Bacc("TRN2", target_bir_lowering=False, num_devices=1)
    io = {n: nc.dram_tensor(f"in_{n}", a.shape, mybir.dt.from_np(a.dtype), kind="ExternalInput").ap() for n, a in arrays.items()}
    io["out"] = nc.dram_tensor("out_x", (SEQ, P, D), F32, kind="ExternalOutput").ap()
    build(nc, io)
    r = run_bass_kernel_spmd(nc, [{f"in_{n}": a for n, a in arrays.items()}], core_ids=[0])
    return r.results[0]["out_x"]
```

```python
from contextlib import ExitStack

import concourse.bass as bass
from concourse import mybir

P = 128
SEQ = 64
GS = 2
NG = SEQ // GS
D = 256
NC = D // P
H = 16
HD = D // H
HP = 2 * HD
PAIRS = H // 2
QUADS = H // 4
HID = 768
NHC = HID // P
EPS = 1e-5
NEWTON = 3
NEG = -1e9

F32 = mybir.dt.float32
F32R = mybir.dt.float32r
BF16 = mybir.dt.bfloat16
I32 = mybir.dt.int32
ALU = mybir.AluOpType
ACT = mybir.ActivationFunctionType
AX_X = mybir.AxisListType.X

AB_ITEMS = (["x_T", "ctx_T", "q", "q_rot", "k", "k_rot", "v"] + [f"score{p}" for p in range(PAIRS)]
            + ["o_T0", "o_T1", "gate", "c_k", "y_T", "out", "x1_T", "c_v", "key", "recept", "mix"])
CD_ITEMS = (["max_T"] + [f"score{p}" for p in range(PAIRS)] + ["o_T0", "o_T1", "y_T", "out", "x3_T"]
            + [f"hidden{i}" for i in range(NHC)])
EARLY_ITEMS = ["x_T", "q"] + [f"rough{p}" for p in range(PAIRS)]
if len(AB_ITEMS) % 2 or len(CD_ITEMS) % 2:
    raise ValueError("each ring bank has the same number of items in every iteration")


def later(it):
    return not (isinstance(it, int) and it == 0)


class Signal:

    def __init__(self, sem, per):
        self.sem, self.per = sem, per

    def after(self, it, count=None):
        return self.sem, it * self.per + (self.per if count is None else count)


class Ring:

    def __init__(self, banks, filled, drained, items):
        self.banks, self.filled_sems, self.drained_sems = banks, filled, drained
        n_banks = len(banks)
        self.where = {n: (i % n_banks, i // n_banks) for i, n in enumerate(items)}
        self.per = len(items) // n_banks

    def bank(self, name):
        return self.banks[self.where[name][0]]

    def reused(self, it, name):
        return later(it) or self.where[name][1] > 0

    def free(self, it, name):
        b, k = self.where[name]
        return self.drained_sems[b], it * self.per + k

    def full(self, it, name):
        b, k = self.where[name]
        return self.filled_sems[b], it * self.per + k + 1

    def read(self, it, name):
        b, k = self.where[name]
        return self.drained_sems[b], it * self.per + k + 1

    def filled(self, name):
        return self.filled_sems[self.where[name][0]]

    def drained(self, name):
        return self.drained_sems[self.where[name][0]]


def build(nc, io):
    ctx = ExitStack()
    with ctx:
        def sb(name, shape, dt=F32):
            return ctx.enter_context(nc.sbuf_tensor(name, shape, dt))

        def psum(name, shape, dt=F32):
            return ctx.enter_context(nc.psum_tensor(name, shape, dt))

        def sem(name):
            return ctx.enter_context(nc.semaphore(name))

        names = ["a_q", "a_q_rot", "a_k", "a_k_rot", "a_v", "a_gate", "a_out",
                 "b_r", "b_k", "b_v", "c_q", "c_k", "c_v", "c_out"]
        W = {n: (sb(f"{n}_hi", [P, NC, D], F32R), sb(f"{n}_lo", [P, NC, D], F32R)) for n in names}
        W["d_gate"] = (sb("d_gate_hi", [P, NC, HID], F32R), sb("d_gate_lo", [P, NC, HID], F32R))
        W["d_up"] = (sb("d_up_hi", [P, NC, HID], F32R), sb("d_up_lo", [P, NC, HID], F32R))
        W["d_down"] = (sb("d_down_hi", [P, NHC, D], F32R), sb("d_down_lo", [P, NHC, D], F32R))
        decay = sb("decay", [P, H, P])
        rope = sb("rope", [P, 4, P])
        ident = sb("ident", [P, P])
        ident_bf = sb("ident_bf", [P, P], BF16)
        sel = sb("sel", [P, PAIRS + 1, P], BF16)
        bias = sb("bias", [P, 4, D])
        cols = sb("cols", [P, 10])
        half = sb("half", [P, 2 * H])
        key_tab = sb("key_tab", [P, SEQ, 2])
        kcols = sb("kcols", [P, GS, 2])
        any_key = sb("any_key", [SEQ, 1])
        head_mean = sb("head_mean", [P, NC * H])
        bq4 = sb("bq4", [P, NC])
        mask_row = sb("mask_row", [P, GS * P], I32)
        mask_add = sb("mask_add", [P, GS * P], BF16)
        COL = {"mu_r": 0, "mu_k": 2, "bq": 4, "bk": 6, "even": 8, "odd": 9}

        xin = sb("xin", [P, GS, D])
        cin = sb("cin", [P, GS, D])
        c_hi = sb("c_hi", [P, NC, GS * P], F32R)
        c_lo = sb("c_lo", [P, NC, GS * P], F32R)

        class Norm:

            def __init__(self, n):
                self.stats = sb(f"{n}_stats", [P, GS, 6])
                self.mv = sb(f"{n}_mv", [P, GS, 2])
                self.negmean = sb(f"{n}_negmean", [P, GS])
                self.vareps = sb(f"{n}_vareps", [P, GS])
                self.rstd = sb(f"{n}_rstd", [P, GS])

        class Chain:
            def __init__(self, n):
                self.x_hi = sb(f"{n}_x_hi", [P, NC, GS * P], F32R)
                self.x_lo = sb(f"{n}_x_lo", [P, NC, GS * P], F32R)
                self.t1 = sb(f"{n}_t1", [P, 2 * D])
                self.t2 = sb(f"{n}_t2", [P, 2 * D])
                self.qk = sb(f"{n}_qk", [P, 2, 2 * D])
                self.qv_hi = sb(f"{n}_qv_hi", [P, NC, GS, 2, P], F32R)
                self.qv_lo = sb(f"{n}_qv_lo", [P, NC, GS, 2, P], F32R)
                self.k_hi = sb(f"{n}_k_hi", [P, NC, GS * P], F32R)
                self.k_lo = sb(f"{n}_k_lo", [P, NC, GS * P], F32R)
                self.o_sb = [self.qk[:, 0, :], self.qk[:, 1, :] if n == "ab" else self.t2[:]]
                self.v = sb(f"{n}_v", [P, GS, H, HP])
                self.p = sb(f"{n}_p", [P, 2, GS, 2, P])
                self.y = sb(f"{n}_y", [P, 2, NC, GS * P], F32R)
                self.xb = sb(f"{n}_xb", [P, GS, D])
                self.norm = Norm(n)
                self.ring = [psum(f"{n}_ring{i}", [P, 512]) for i in range(2)]
                self.o = psum(f"{n}_o", [P, QUADS, GS, P])

        AB, CD = Chain("ab"), Chain("cd")
        A0 = Norm("a0")
        products = [AB.t1[:], AB.t2[:]] + [AB.p[:, i].rearrange("p s a t -> p (s a t)") for i in range(2)]
        sg = sb("sg", [P, GS, D])
        x2 = sb("x2", [P, GS, D])
        xs = sb("xs", [P, NC, GS, P + 1])
        ssq = sb("ssq", [P, GS, H])
        gn_var = sb("gn_var", [P, GS, H])
        gn_rstd = sb("gn_rstd", [P, GS, H])
        gn_neg_half = sb("gn_neg_half", [P, GS, H])
        gn_sq = sb("gn_sq", [P, GS, H])
        one_half = sb("one_half", [P, GS, H])
        q_hi = sb("q_hi", [P, NC, GS * P], F32R)
        mx = sb("mx", [P, PAIRS, GS, 2])
        mx_parts = sb("mx_parts", [P, GS, 2, 4, 32], BF16)
        m_T = sb("m_T", [P, GS, 2, P], BF16)
        rz = sb("rz", [P, GS, H])
        xo = CD.p[:, 0].rearrange("p s a q -> p s (a q)")

        r_ab = Ring(AB.ring, [sem("ab_filled0"), sem("ab_filled1")], [sem("ab_drained0"), sem("ab_drained1")], AB_ITEMS)
        r_cd = Ring(CD.ring, [sem("cd_filled0"), sem("cd_filled1")], [sem("cd_drained0"), sem("cd_drained1")], CD_ITEMS)
        early_bank = CD.o[:, QUADS // 2:, :, :].rearrange("p a b c -> p (a b c)")
        r_early = Ring([early_bank], [sem("early_filled")], [sem("early_drained")], EARLY_ITEMS)

        def signals(**per):
            return {n: Signal(sem(n), k) for n, k in per.items()}

        S = signals(
            x_in=16, ctx_in=16, a_stats=2, a_aggr=2, a_small=2, a_rstd=1, a_xhat=2, a_x_hi=1, a_c_hi=1,
            a_th=1, a_sg=1, a_xb=1, a_qk=2, a_qv_hi=2, a_qv_lo=2, a_k_hi=1, a_k_lo=1,
            a_pv=PAIRS, a_osb=2, a_sq=2, a_ssq=2, a_y=2, a_gvar=1, a_ghalf=1,
            a_grstd=NEWTON + 1, a_gsq=NEWTON, a_gprod=NEWTON, a_gsum=NEWTON, a_yg=2, a_y_hi=1,
            b_stats=2, b_aggr=2, b_small=2, b_rstd=1, b_xhat=2, b_d=1, b_xr=2, b_xk=2,
            b_xr_hi=1, b_xr_lo=1, b_xk_hi=1, b_xk_lo=1, b_relu=1, b_k2_hi=1, b_k2_lo=1, b_x2=1,
            mask_in=16, c_mask=1, c_kcols=1, c_stats=2, c_aggr=2, c_small=2, c_rstd=1, c_xhat=2, c_x_hi=1,
            c_k_hi=1, c_k_lo=1, c_kv=2, c_q_hi=NC, c_q_lo=1, c_qv_hi=2, c_qv_lo=2, c_xb=1,
            c_part0=NC, c_part1=NC, c_pv=PAIRS, c_osb=2, c_rz=2, c_y_hi=1,
            d_stats=2, d_aggr=2, d_small=2, d_rstd=1, d_xhat=2, d_x_hi=1,
            d_th=NHC, d_a=NHC, d_h_hi=NHC, d_h_lo=NHC, d_down=NHC, d_x4=1, out_done=16,
        )
        load = sem("load")
        decay_in = sem("decay_in")
        w_staged = [sem(f"w_staged{i}") for i in range(4)]
        w_ready, w_centred, w_hi_done = sem("w_ready"), sem("w_centred"), sem("w_hi_done")
        w_lo_done = [sem("w_lo_even"), sem("w_lo_odd")]
        dw_staged = [sem("dw_staged_first"), sem("dw_staged_rest")]
        dw_ready, dw_hi_done, dw_lo_done = sem("dw_ready"), sem("dw_hi_done"), sem("dw_lo_done")
        mask_prep, mask_T, dve_const, act_const = sem("mask_prep"), sem("mask_T"), sem("dve_const"), sem("act_const")
        v_zero = sem("v_zero")
        NLOAD, NDVE_CONST, NACT_CONST = 7, 10, 3

        def flat(x):
            n = len(x.shape)
            names_ = "abcdef"[:n - 1]
            return x[:].rearrange("p " + " ".join(names_) + " -> p (" + " ".join(names_) + ")")

        def raw(x):
            return x.bitcast(F32)

        stepped = sem("stepped")

        def apart(eng):
            eng.sem_inc(stepped, 1)

        stage = [AB.qk[:, 0], AB.qk[:, 1], CD.qk[:, 0], CD.qk[:, 1]]
        wf = [flat(AB.v)[:, 0:512], flat(AB.v)[:, 512:1024], flat(CD.p)[:, 0:512], flat(CD.p)[:, 512:1024]]
        SLOTS = len(stage)
        SCALES = {"a_out": 0.5, "b_v": 0.5, "c_q": 0.25}
        NW = len(names)
        if NW % 2:
            raise ValueError("the even and the odd weights are as many")

        places = [flat(CD.p)[:, 0:512], flat(CD.p)[:, 512:1024], CD.qk[:, 0], flat(CD.xb), CD.t1[:], CD.t2[:]]
        NPLACES = len(places)
        d_parts = []
        for n in ("d_gate", "d_up", "d_down"):
            src = io[n].rearrange("(c p) n -> p c n", p=P)
            for k in range(3):
                cut = (slice(None), slice(2 * k, 2 * k + 2)) if n == "d_down" else \
                      (slice(None), slice(None), slice(256 * k, 256 * k + 256))
                place = places[len(d_parts) % NPLACES].rearrange("p (c n) -> p c n", c=2)
                d_parts.append((W[n][0][cut], W[n][1][cut], src[cut], place))
        ND = len(d_parts)
        if not NPLACES <= PAIRS < ND <= 2 * NPLACES:
            raise ValueError("the first parts are converted beside the first group's pairs of heads")

        block = ctx.enter_context(nc.Block())

        def seqs(u):
            return slice(GS * u, GS * u + GS) if isinstance(u, int) else bass.ds(GS * u, GS)

        @block.sync
        def _(sp):
            def weight(i):
                if i >= SLOTS:
                    sp.wait_ge(w_ready, i - SLOTS + 1)
                src = io[names[i]].rearrange("(c p) n -> p c n", p=P)
                sp.dma_start(stage[i % SLOTS].rearrange("p (c n) -> p c n", c=NC), src).then_inc(w_staged[i % SLOTS], 16)

            def loads(u):
                if later(u):
                    sp.wait_ge(*S["a_xb"].after(u - 1))
                if later(u):
                    sp.wait_ge(*S["a_xhat"].after(u - 1))
                sp.dma_start(xin[:], io["x"][seqs(u)].rearrange("s p c -> p s c")).then_inc(S["x_in"].sem, 16)
                if later(u):
                    sp.wait_ge(*r_ab.full(u - 1, "ctx_T"))
                sp.dma_start(cin[:], io["ctx"][seqs(u)].rearrange("s p c -> p s c")).then_inc(S["ctx_in"].sem, 16)

            def mask(j):
                if later(j):
                    sp.wait_ge(*S["c_mask"].after(j - 1))
                sp.dma_start(mask_row[0:1, :], io["mask"][seqs(j)].rearrange("(o s) i j k -> o (s i j k)", o=1)).then_inc(S["mask_in"].sem, 16)

            def store(j):
                sp.wait_ge(*S["d_x4"].after(j))
                sp.dma_start(io["out"][seqs(j)].rearrange("s p c -> p s c"), xo).then_inc(S["out_done"].sem, 16)

            for i in range(SLOTS):
                weight(i)
            loads(0)
            for i in range(SLOTS, NW):
                weight(i)
            for dst, src in ((rope[:], io["rope"]), (ident[:], io["ident"]),
                             (cols[:], io["cols"]), (bias[:], io["bias"].partition_broadcast(P)),
                             (CD.t1[0:SEQ, 0:P].bitcast(I32), io["mask"].rearrange("b i j k -> b (i j k)")),
                             (flat(AB.p)[:, 0:PAIRS * P], io["sel"][:, 0:PAIRS * P]),
                             (CD.t2[:, 0:P], io["sel"][:, PAIRS * P:(PAIRS + 1) * P])):
                sp.dma_start(dst, src).then_inc(load, 16)
            sp.dma_start(decay[:], io["decay"]).then_inc(decay_in, 16)
            sp.wait_ge(w_lo_done[0], NW // 2)
            sp.wait_ge(w_lo_done[1], NW // 2)
            for k, (_hi, _lo, src, place) in enumerate(d_parts):
                if k == NPLACES - 2:
                    sp.wait_ge(mask_T, 1)
                if k >= NPLACES:
                    sp.wait_ge(dw_lo_done, k - NPLACES + 1)
                sp.dma_start(place.bitcast(I32), src).then_inc(dw_staged[k // NPLACES], 16)
            loads(1)
            sp.wait_ge(dve_const, NDVE_CONST)
            mask(0)
            with sp.Fori(1, NG - 1) as u:
                loads(u + 1)
                mask(u)
                store(u - 1)
            mask(NG - 1)
            store(NG - 2)
            store(NG - 1)
            sp.wait_ge(*S["out_done"].after(NG - 1))

        @block.tensor
        def _(pe):

            def channel_major(bank, outs, x_hi):
                for o, (n, col) in enumerate(outs):
                    for c in range(NC):
                        for w in W[n]:
                            pe.matmul(bank[:, o * 256:(o + 1) * 256], w[:, c, col:col + P], x_hi[:, c, :],
                                      start=(o == 0 and c == 0 and w is W[n][0]), stop=False, skip_group_check=True)

            def channel_major_lo(bank, outs, x_lo):
                for o, (n, col) in enumerate(outs):
                    for c in range(NC):
                        ins = pe.matmul(bank[:, o * 256:(o + 1) * 256], W[n][0][:, c, col:col + P], x_lo[:, c, :],
                                        start=False, stop=(c == NC - 1), skip_group_check=True)
                return ins

            def token_major(bank, n, x_hi):
                for s in range(GS):
                    for c in range(NC):
                        for w in W[n]:
                            pe.matmul(bank[:, s * D:(s + 1) * D], x_hi[:, c, s * P:(s + 1) * P], w[:, c, :],
                                      start=(s == 0 and c == 0 and w is W[n][0]), stop=False, skip_group_check=True)

            def token_major_lo(bank, n, x_lo):
                for s in range(GS):
                    for c in range(NC):
                        ins = pe.matmul(bank[:, s * D:(s + 1) * D], x_lo[:, c, s * P:(s + 1) * P], W[n][0][:, c, :],
                                        start=False, stop=(c == NC - 1), skip_group_check=True)
                return ins

            def transposes(bank, src):
                ins = None
                for c in range(NC):
                    for s in range(GS):
                        o = (c * GS + s) * P
                        ins = pe.transpose(bank[:, o:o + P], src[:, s * D + c * P:s * D + (c + 1) * P], ident[:])
                return ins

            def rows_of(x, p, s):
                return x[32 * (p % 4):32 * (p % 4) + 32, p // 4, s * P:(s + 1) * P]

            def queries_of(x, p, s):
                return x[32 * (p % 4):32 * (p % 4) + 32, p // 4, s, :, :].rearrange("p a q -> p (a q)")

            def scores(ch, bank, p):
                for s in range(GS):
                    pe.matmul(bank[:, s * 256:(s + 1) * 256], rows_of(ch.k_hi, p, s), queries_of(ch.qv_hi, p, s),
                              start=(s == 0), stop=False, skip_group_check=True)

            def scores_lo(ch, bank, p, last):
                for s in range(GS):
                    pe.matmul(bank[:, s * 256:(s + 1) * 256], rows_of(ch.k_lo, p, s), queries_of(ch.qv_hi, p, s),
                              start=False, stop=False, skip_group_check=True)
                    ins = pe.matmul(bank[:, s * 256:(s + 1) * 256], rows_of(ch.k_hi, p, s), queries_of(ch.qv_lo, p, s),
                                    start=False, stop=last, skip_group_check=True)
                return ins

            def attend(ch, p):
                ins = None
                for s in range(GS):
                    for par in range(2):
                        h = 2 * p + par
                        j, quad = h % 4, h // 4
                        ins = pe.matmul(ch.o[32 * j:32 * j + 32, quad, s, :], ch.v[:, s, h, :],
                                        ch.p[:, p % 2, s, par, :], start=True, stop=True, skip_group_check=True,
                                        tile_position=(0, 32 * j))
                return ins

            def heads_to_tokens(ch, bank, s):
                ins = None
                for quad in range(QUADS):
                    src = ch.o_sb[quad // 2][:, (quad % 2 * GS + s) * P:(quad % 2 * GS + s + 1) * P]
                    ins = pe.transpose(bank[:, quad * P:(quad + 1) * P], src, ident[:])
                return ins

            def ctx_T(u):
                bank = r_ab.bank("ctx_T")
                if r_ab.reused(u, "ctx_T"):
                    pe.wait_ge(*r_ab.free(u, "ctx_T"))
                pe.wait_ge(*S["ctx_in"].after(u))
                transposes(bank, cin[:].rearrange("p s c -> p (s c)")).then_inc(r_ab.filled("ctx_T"), 1)

            def x_T(u):
                bank = r_ab.bank("x_T")
                if r_ab.reused(u, "x_T"):
                    pe.wait_ge(*r_ab.free(u, "x_T"))
                pe.wait_ge(*S["a_xhat"].after(u))
                transposes(bank, sg[:].rearrange("p s c -> p (s c)")).then_inc(r_ab.filled("x_T"), 1)

            def a_v(u):
                bank = r_ab.bank("v")
                if r_ab.reused(u, "v"):
                    pe.wait_ge(*r_ab.free(u, "v"))
                token_major(bank, "a_v", c_hi)
                ins = token_major_lo(bank, "a_v", c_lo)
                ins.then_inc(r_ab.filled("v"), 1)

            def a_gate(u):
                bank = r_ab.bank("gate")
                if r_ab.reused(u, "gate"):
                    pe.wait_ge(*r_ab.free(u, "gate"))
                token_major(bank, "a_gate", AB.x_hi)
                ins = token_major_lo(bank, "a_gate", AB.x_lo)
                ins.then_inc(r_ab.filled("gate"), 1)

            def a_q(u):
                bank = r_ab.bank("q")
                if r_ab.reused(u, "q"):
                    pe.wait_ge(*r_ab.free(u, "q"))
                pe.wait_ge(*S["a_x_hi"].after(u))
                channel_major(bank, (("a_q", 0), ("a_q", P)), AB.x_hi)
                pe.wait_ge(*r_ab.read(u, "x_T"))
                ins = channel_major_lo(bank, (("a_q", 0), ("a_q", P)), AB.x_lo)
                ins.then_inc(r_ab.filled("q"), 1)

            def a_q_rot(u):
                bank = r_ab.bank("q_rot")
                if r_ab.reused(u, "q_rot"):
                    pe.wait_ge(*r_ab.free(u, "q_rot"))
                channel_major(bank, (("a_q_rot", 0), ("a_q_rot", P)), AB.x_hi)
                ins = channel_major_lo(bank, (("a_q_rot", 0), ("a_q_rot", P)), AB.x_lo)
                ins.then_inc(r_ab.filled("q_rot"), 1)

            def a_k(u):
                bank = r_ab.bank("k")
                if r_ab.reused(u, "k"):
                    pe.wait_ge(*r_ab.free(u, "k"))
                pe.wait_ge(*S["a_c_hi"].after(u))
                channel_major(bank, (("a_k", 0), ("a_k", P)), c_hi)
                pe.wait_ge(*r_ab.read(u, "ctx_T"))
                ins = channel_major_lo(bank, (("a_k", 0), ("a_k", P)), c_lo)
                ins.then_inc(r_ab.filled("k"), 1)

            def a_k_rot(u):
                bank = r_ab.bank("k_rot")
                if r_ab.reused(u, "k_rot"):
                    pe.wait_ge(*r_ab.free(u, "k_rot"))
                channel_major(bank, (("a_k_rot", 0), ("a_k_rot", P)), c_hi)
                ins = channel_major_lo(bank, (("a_k_rot", 0), ("a_k_rot", P)), c_lo)
                ins.then_inc(r_ab.filled("k_rot"), 1)

            def a_score(u, p):
                bank = r_ab.bank(f"score{p}")
                if r_ab.reused(u, f"score{p}"):
                    pe.wait_ge(*r_ab.free(u, f"score{p}"))
                if p == 0:
                    pe.wait_ge(*S["a_qv_hi"].after(u))
                    pe.wait_ge(*S["a_k_hi"].after(u))
                scores(AB, bank, p)
                if p == 0:
                    pe.wait_ge(*S["a_qv_lo"].after(u))
                    pe.wait_ge(*S["a_k_lo"].after(u))
                ins = scores_lo(AB, bank, p, True)
                ins.then_inc(r_ab.filled(f"score{p}"), 1)

            def a_attend(u, p):
                pe.wait_ge(*r_ab.read(u, f"score{p}"))
                if p == 0:
                    pe.wait_ge(*r_ab.read(u, "v"))
                    if later(u):
                        pe.wait_ge(*S["a_osb"].after(u - 1, 1))
                if p == PAIRS // 2:
                    if later(u):
                        pe.wait_ge(*S["a_osb"].after(u - 1, 2))
                attend(AB, p).then_inc(S["a_pv"].sem, 1)

            def a_o_T(u, s):
                bank = r_ab.bank(f"o_T{s}")
                if r_ab.reused(u, f"o_T{s}"):
                    pe.wait_ge(*r_ab.free(u, f"o_T{s}"))
                pe.wait_ge(*S["a_osb"].after(u))
                heads_to_tokens(AB, bank, s).then_inc(r_ab.filled(f"o_T{s}"), 1)

            def a_y_T(u):
                bank = r_ab.bank("y_T")
                if r_ab.reused(u, "y_T"):
                    pe.wait_ge(*r_ab.free(u, "y_T"))
                pe.wait_ge(*S["a_yg"].after(u))
                transposes(bank, AB.t2[:]).then_inc(r_ab.filled("y_T"), 1)

            def a_out(u):
                bank = r_ab.bank("out")
                if r_ab.reused(u, "out"):
                    pe.wait_ge(*r_ab.free(u, "out"))
                pe.wait_ge(*S["a_y_hi"].after(u))
                token_major(bank, "a_out", AB.y[:, 0])
                pe.wait_ge(*r_ab.read(u, "y_T"))
                ins = token_major_lo(bank, "a_out", AB.y[:, 1])
                ins.then_inc(r_ab.filled("out"), 1)

            def x1_T(u):
                bank = r_ab.bank("x1_T")
                if r_ab.reused(u, "x1_T"):
                    pe.wait_ge(*r_ab.free(u, "x1_T"))
                pe.wait_ge(*S["b_xhat"].after(u))
                transposes(bank, AB.t1[:]).then_inc(r_ab.filled("x1_T"), 1)

            def b_recept(u):
                bank = r_ab.bank("recept")
                if r_ab.reused(u, "recept"):
                    pe.wait_ge(*r_ab.free(u, "recept"))
                pe.wait_ge(*S["b_xr_hi"].after(u))
                token_major(bank, "b_r", AB.x_hi)
                pe.wait_ge(*S["b_xr_lo"].after(u))
                ins = token_major_lo(bank, "b_r", AB.x_lo)
                ins.then_inc(r_ab.filled("recept"), 1)

            def b_key(u):
                bank = r_ab.bank("key")
                if r_ab.reused(u, "key"):
                    pe.wait_ge(*r_ab.free(u, "key"))
                pe.wait_ge(*S["b_xk_hi"].after(u))
                channel_major(bank, (("b_k", 0), ("b_k", P)), AB.k_hi)
                pe.wait_ge(*S["b_xk_lo"].after(u))
                ins = channel_major_lo(bank, (("b_k", 0), ("b_k", P)), AB.k_lo)
                ins.then_inc(r_ab.filled("key"), 1)

            def b_mix(u):
                bank = r_ab.bank("mix")
                if r_ab.reused(u, "mix"):
                    pe.wait_ge(*r_ab.free(u, "mix"))
                pe.wait_ge(*S["b_k2_hi"].after(u))
                token_major(bank, "b_v", AB.y[:, 0])
                pe.wait_ge(*S["b_k2_lo"].after(u))
                ins = token_major_lo(bank, "b_v", AB.y[:, 1])
                ins.then_inc(r_ab.filled("mix"), 1)

            def c_k(u):
                bank = r_ab.bank("c_k")
                if r_ab.reused(u, "c_k"):
                    pe.wait_ge(*r_ab.free(u, "c_k"))
                channel_major(bank, (("c_k", 0), ("c_k", P)), c_hi)
                ins = channel_major_lo(bank, (("c_k", 0), ("c_k", P)), c_lo)
                ins.then_inc(r_ab.filled("c_k"), 1)

            def c_v(u):
                bank = r_ab.bank("c_v")
                if r_ab.reused(u, "c_v"):
                    pe.wait_ge(*r_ab.free(u, "c_v"))
                token_major(bank, "c_v", c_hi)
                ins = token_major_lo(bank, "c_v", c_lo)
                ins.then_inc(r_ab.filled("c_v"), 1)

            def c_x_T(j):
                bank = r_early.bank("x_T")
                if r_early.reused(j, "x_T"):
                    pe.wait_ge(*r_early.free(j, "x_T"))
                if later(j):
                    pe.wait_ge(*S["c_osb"].after(j - 1))
                pe.wait_ge(*S["c_xhat"].after(j))
                transposes(bank, CD.qk[:, 0, :]).then_inc(r_early.filled("x_T"), 1)

            def c_q(j):
                bank = r_early.bank("q")
                if r_early.reused(j, "q"):
                    pe.wait_ge(*r_early.free(j, "q"))
                pe.wait_ge(*S["c_x_hi"].after(j))
                channel_major(bank, (("c_q", 0), ("c_q", P)), AB.y[:, 0])
                pe.wait_ge(*r_early.read(j, "x_T"))
                ins = channel_major_lo(bank, (("c_q", 0), ("c_q", P)), AB.y[:, 1])
                ins.then_inc(r_early.filled("q"), 1)

            def c_rough(j, p):
                bank = r_early.bank(f"rough{p}")
                if r_early.reused(j, f"rough{p}"):
                    pe.wait_ge(*r_early.free(j, f"rough{p}"))
                if p == 0:
                    pe.wait_ge(*S["c_q_hi"].after(j))
                    pe.wait_ge(*S["c_kv"].after(j))
                    pe.wait_ge(*S["c_mask"].after(j))
                c, g = p // 4, p % 4
                r = slice(32 * g, 32 * g + 32)
                ins = None
                for s in range(GS):
                    dst = bank[:, s * 256:(s + 1) * 256]
                    kv = CD.y[r, :, :, :].rearrange("p v c (s k) -> p v c s k", s=GS)[:, :, c, s, :]
                    pe.matmul(dst, q_hi[r, c, s * P:(s + 1) * P], kv, start=True, stop=False)
                    ins = pe.matmul(dst, sel[:, PAIRS, :], mask_add[:, s * P:(s + 1) * P].rearrange("r (o k) -> r o k", o=1)
                                    .broadcast_to([P, 2, P]), start=False, stop=True)
                ins.then_inc(r_early.filled(f"rough{p}"), 1)

            def c_max_T(j):
                bank = r_cd.bank("max_T")
                if r_cd.reused(j, "max_T"):
                    pe.wait_ge(*r_cd.free(j, "max_T"))
                pe.wait_ge(*S["c_part1"].after(j))
                bf = bank[:].bitcast(BF16)
                for s in range(GS):
                    for par in range(2):
                        o = (s * 2 + par) * P
                        ins = pe.transpose(bf[:, o:o + P],
                                           mx_parts[:, s, par, :, :].rearrange("q a b -> q (a b)"), ident_bf[:])
                ins.then_inc(r_cd.filled("max_T"), 1)

            def c_score(j, p):
                bank = r_cd.bank(f"score{p}")
                if r_cd.reused(j, f"score{p}"):
                    pe.wait_ge(*r_cd.free(j, f"score{p}"))
                if p == 0:
                    pe.wait_ge(*S["c_qv_hi"].after(j))
                    pe.wait_ge(*S["c_k_hi"].after(j))
                scores(CD, bank, p)
                if p == 0:
                    pe.wait_ge(*S["c_qv_lo"].after(j))
                    pe.wait_ge(*S["c_k_lo"].after(j))
                scores_lo(CD, bank, p, False)
                if p == 0:
                    pe.wait_ge(*r_cd.read(j, "max_T"))
                for s in range(GS):
                    ins = pe.matmul(bank[:, s * 256:(s + 1) * 256], sel[:, p, :], m_T[:, s, :, :].rearrange("r a q -> r (a q)"),
                                    start=False, stop=True, skip_group_check=True)
                ins.then_inc(r_cd.filled(f"score{p}"), 1)

            def c_attend(j, p):
                pe.wait_ge(*r_cd.read(j, f"score{p}"))
                if p == 0:
                    pe.wait_ge(*r_ab.read(j, "c_v"))
                    if later(j):
                        pe.wait_ge(*S["d_x4"].after(j - 1))
                if p == PAIRS // 2:
                    if later(j):
                        pe.wait_ge(*S["c_osb"].after(j - 1, 2))
                attend(CD, p).then_inc(S["c_pv"].sem, 1)

            def c_o_T(j, s):
                bank = r_cd.bank(f"o_T{s}")
                if r_cd.reused(j, f"o_T{s}"):
                    pe.wait_ge(*r_cd.free(j, f"o_T{s}"))
                pe.wait_ge(*S["c_osb"].after(j))
                heads_to_tokens(CD, bank, s).then_inc(r_cd.filled(f"o_T{s}"), 1)

            def c_y_T(j):
                bank = r_cd.bank("y_T")
                if r_cd.reused(j, "y_T"):
                    pe.wait_ge(*r_cd.free(j, "y_T"))
                pe.wait_ge(*r_cd.read(j, "o_T0"))
                pe.wait_ge(*r_cd.read(j, "o_T1"))
                transposes(bank, CD.t1[:]).then_inc(r_cd.filled("y_T"), 1)

            def c_out(j):
                bank = r_cd.bank("out")
                if r_cd.reused(j, "out"):
                    pe.wait_ge(*r_cd.free(j, "out"))
                pe.wait_ge(*S["c_y_hi"].after(j))
                token_major(bank, "c_out", CD.y[:, 0])
                pe.wait_ge(*r_cd.read(j, "y_T"))
                ins = token_major_lo(bank, "c_out", CD.y[:, 1])
                ins.then_inc(r_cd.filled("out"), 1)

            def x3_T(j):
                bank = r_cd.bank("x3_T")
                if r_cd.reused(j, "x3_T"):
                    pe.wait_ge(*r_cd.free(j, "x3_T"))
                pe.wait_ge(*S["d_xhat"].after(j))
                transposes(bank, CD.t1[:]).then_inc(r_cd.filled("x3_T"), 1)

            def d_hidden(j, i):
                bank = r_cd.bank(f"hidden{i}")
                if r_cd.reused(j, f"hidden{i}"):
                    pe.wait_ge(*r_cd.free(j, f"hidden{i}"))
                if i == 0:
                    pe.wait_ge(*S["d_x_hi"].after(j))
                channel_major(bank, (("d_gate", i * P), ("d_up", i * P)), CD.x_hi)
                if i == 0:
                    pe.wait_ge(*r_cd.read(j, "x3_T"))
                ins = channel_major_lo(bank, (("d_gate", i * P), ("d_up", i * P)), CD.x_lo)
                ins.then_inc(r_cd.filled(f"hidden{i}"), 1)

            def d_down(j, i):
                acc = CD.o[:, 0:2, :, :].rearrange("p a b c -> p (a b c)")
                w_hi, w_lo = W["d_down"][0][:, i, :], W["d_down"][1][:, i, :]
                h_hi = CD.qv_hi[:, i % 2, 0, :, :].rearrange("p a b -> p (a b)")
                h_lo = CD.qv_lo[:, i % 2, 0, :, :].rearrange("p a b -> p (a b)")
                pe.wait_ge(*S["d_h_hi"].after(j, i + 1))
                for s in range(GS):
                    for w in (w_hi, w_lo):
                        pe.matmul(acc[:, s * D:(s + 1) * D], h_hi[:, s * P:(s + 1) * P], w,
                                  start=(i == 0 and s == 0 and w is w_hi), stop=False, skip_group_check=True)
                pe.wait_ge(*S["d_h_lo"].after(j, i + 1))
                for s in range(GS):
                    ins = pe.matmul(acc[:, s * D:(s + 1) * D], h_lo[:, s * P:(s + 1) * P], w_hi,
                                    start=False, stop=(i == NHC - 1), skip_group_check=True)
                ins.then_inc(S["d_down"].sem, 1)

            def body(u, j, i, n=None):
                ab, c, d = u is not None, j is not None, i is not None
                if ab:
                    a_q(u)
                    a_q_rot(u)
                    a_k(u)
                    a_k_rot(u)
                if d:
                    x3_T(i)
                if ab:
                    a_v(u)
                if d:
                    d_hidden(i, 0)
                    d_hidden(i, 1)
                for p in range(PAIRS):
                    if ab:
                        a_score(u, p)
                    if ab and p > 0:
                        a_attend(u, p - 1)
                    if d and p == 0:
                        d_hidden(i, 2)
                        d_down(i, 0)
                    if c and p == 1:
                        c_x_T(j)
                    if d and p == 1:
                        d_down(i, 1)
                    if d and p == 2:
                        d_hidden(i, 3)
                    if d and p == 3:
                        d_down(i, 2)
                    if c and p == 3:
                        c_q(j)
                    if d and p == 4:
                        d_hidden(i, 4)
                    if d and p == 5:
                        d_down(i, 3)
                    if c and p >= 4:
                        c_rough(j, p - 4)
                if ab:
                    a_attend(u, PAIRS - 1)
                if d:
                    d_hidden(i, 5)
                if c:
                    c_rough(j, 4)
                if ab:
                    a_o_T(u, 0)
                    a_o_T(u, 1)
                if d:
                    d_down(i, 4)
                if c:
                    c_rough(j, 5)
                if d:
                    d_down(i, 5)
                if c:
                    c_rough(j, 6)
                if ab:
                    a_gate(u)
                if c:
                    c_rough(j, 7)
                if ab:
                    c_k(u)
                if c:
                    c_max_T(j)
                for p in range(PAIRS + 1):
                    if c and p < PAIRS:
                        c_score(j, p)
                    if ab and p == 1:
                        a_y_T(u)
                    if ab and p == 2:
                        a_out(u)
                    if ab and p == 7:
                        c_v(u)
                    if c and p > 0:
                        c_attend(j, p - 1)
                    if ab and p == 5:
                        x1_T(u)
                if ab:
                    b_key(u)
                    b_recept(u)
                if c:
                    c_o_T(j, 0)
                    c_o_T(j, 1)
                if ab:
                    b_mix(u)
                if c:
                    c_y_T(j)
                if n is not None:
                    x_T(n)
                    ctx_T(n)
                if c:
                    c_out(j)

            pe.wait_ge(load, 16 * NLOAD)
            pe.wait_ge(mask_prep, 4)
            pe.transpose(AB.ring[0][:, 0:SEQ], CD.t2[0:SEQ, 0:P], ident[0:SEQ, 0:SEQ])
            pe.transpose(AB.ring[0][:, SEQ:2 * SEQ], CD.t2[0:SEQ, P:2 * P], ident[0:SEQ, 0:SEQ]).then_inc(mask_T, 1)
            pe.wait_ge(w_lo_done[0], NW // 2)
            pe.wait_ge(w_lo_done[1], NW // 2)
            pe.wait_ge(dve_const, NDVE_CONST)
            pe.wait_ge(act_const, NACT_CONST)
            x_T(0)
            ctx_T(0)
            body(0, None, None, 1)
            pe.wait_ge(dw_lo_done, ND)
            body(1, 0, None, 2)
            with pe.Fori(2, NG - 1) as u:
                body(u, u - 1, u - 2, u + 1)
            body(NG - 1, NG - 2, NG - 3)
            body(None, NG - 1, NG - 2)
            body(None, None, NG - 1)

        @block.scalar
        def _(act):
            def ctx_hi(u):
                bank = r_ab.bank("ctx_T")
                act.wait_ge(*r_ab.full(u, "ctx_T"))
                act.activation(flat(c_hi), bank[:], ACT.Copy).then_inc(S["a_c_hi"].sem, 1)

            def x_hi(ring, it, item, dst, sig):
                bank = ring.bank(item)
                act.wait_ge(*ring.full(it, item))
                act.activation(flat(dst), bank[:], ACT.Copy).then_inc(S[sig].sem, 1)

            def values(u):
                bank = r_ab.bank("v")
                act.wait_ge(*r_ab.full(u, "v"))
                act.activation(AB.v[:, :, :, 0:HD].rearrange("p s h e -> p (s h) e"),
                                          bank[:].rearrange("p (a e) -> p a e", e=HD), ACT.Copy).then_inc(r_ab.drained("v"), 1)

            def by_parity(dst, src, par):
                return act.activation(dst[:].rearrange("p c s a t -> p (c s) a t")[:, :, par, :],
                                      src.rearrange("p (a t) -> p a t", t=P), ACT.Copy,
                                      scale=cols[:, COL["even"] + par:COL["even"] + par + 1])

            def a_qv_high(u):
                act.wait_ge(*S["a_qk"].after(u, 1))
                for par in range(2):
                    by_parity(AB.qv_hi, AB.qk[:, 0, :], par).then_inc(S["a_qv_hi"].sem, 1)

            def qv_high(j):
                act.wait_ge(*S["c_q_hi"].after(j))
                if later(j):
                    act.wait_ge(*S["d_down"].after(j - 1))
                for par in range(2):
                    by_parity(CD.qv_hi, raw(flat(q_hi)), par).then_inc(S["c_qv_hi"].sem, 1)

            def qv_low(j):
                act.wait_ge(*S["c_q_lo"].after(j))
                for par in range(2):
                    by_parity(CD.qv_lo, CD.qk[:, 0, :], par).then_inc(S["c_qv_lo"].sem, 1)

            def a_th(u):
                act.wait_ge(*r_ab.read(u, "gate"))
                act.wait_ge(*S["a_ssq"].after(u))
                act.activation(flat(AB.p[:, 1]), AB.t2[:], ACT.Tanh, scale=0.5).then_inc(S["a_th"].sem, 1)

            def a_k_hi(u):
                act.wait_ge(*S["a_qk"].after(u, 2))
                act.activation(flat(AB.k_hi), AB.qk[:, 1, :], ACT.Copy).then_inc(S["a_k_hi"].sem, 1)

            def osb(ch, n, it, half_):
                act.wait_ge(*S[n + "_pv"].after(it, 4 * half_ + 4))
                act.activation(ch.o_sb[half_], ch.o[:, 2 * half_:2 * half_ + 2, :, :].rearrange("p a b c -> p (a b c)"),
                               ACT.Copy).then_inc(S[n + "_osb"].sem, 1)

            def a_o(u, s):
                bank = r_ab.bank(f"o_T{s}")
                act.wait_ge(*r_ab.full(u, f"o_T{s}"))
                act.activation(AB.t1[:, s * D:(s + 1) * D].rearrange("p (h e) -> p h e", e=HD),
                                          bank[:].rearrange("p (h e) -> p h e", e=HP)[:, :, 0:HD], ACT.Copy).then_inc(r_ab.drained(f"o_T{s}"), 1)

            def a_sq(u, s):
                act.wait_ge(*r_ab.read(u, f"o_T{s}"))
                act.activation(flat(AB.p[:, 1])[:, s * D:(s + 1) * D], AB.t1[:, s * D:(s + 1) * D],
                               ACT.Square).then_inc(S["a_sq"].sem, 1)

            def y_hi(ring, it, ch, n):
                bank = ring.bank("y_T")
                act.wait_ge(*ring.full(it, "y_T"))
                act.activation(flat(ch.y[:, 0]), bank[:], ACT.Copy).then_inc(S[n + "_y_hi"].sem, 1)

            def b_xs(u):
                bank = r_ab.bank("x1_T")
                act.wait_ge(*r_ab.full(u, "x1_T"))
                act.activation(xs[:, :, :, 1:P + 1].rearrange("p c s t -> p (c s) t"),
                                          bank[:].rearrange("p (a t) -> p a t", t=P), ACT.Copy).then_inc(r_ab.drained("x1_T"), 1)

            def b_xr_hi(u):
                act.wait_ge(*S["b_xr"].after(u))
                act.activation(flat(AB.x_hi), AB.t2[:], ACT.Copy).then_inc(S["b_xr_hi"].sem, 1)

            def b_xk_hi(u):
                act.wait_ge(*S["b_xk"].after(u))
                act.activation(flat(AB.k_hi), AB.qk[:, 0, :], ACT.Copy).then_inc(S["b_xk_hi"].sem, 1)

            def b_th(u):
                bank = r_ab.bank("recept")
                act.wait_ge(*r_ab.full(u, "recept"))
                act.wait_ge(*S["b_xr_lo"].after(u))
                act.activation(AB.t2[:], bank[:], ACT.Tanh, scale=0.5).then_inc(r_ab.drained("recept"), 1)

            def b_relu(u):
                bank = r_ab.bank("key")
                act.wait_ge(*r_ab.full(u, "key"))
                act.activation(AB.qk[:, 1, :], bank[:], ACT.Relu).then_inc(S["b_relu"].sem, 1)

            def b_k2_hi(u):
                act.wait_ge(*r_ab.read(u, "key"))
                act.activation(flat(AB.y[:, 0]), AB.t1[:], ACT.Copy).then_inc(S["b_k2_hi"].sem, 1)

            def plus_bias(ring, j, item, slot, col):
                bank = ring.bank(item)
                act.wait_ge(*ring.full(j, item))
                for m in range(NC):
                    ins = act.activation(CD.qk[:, slot, m * 256:(m + 1) * 256], bank[:, m * 256:(m + 1) * 256],
                                         ACT.Identity, bias=col[:, m:m + 1])
                ins.then_inc(ring.drained(item), 1)

            def c_k_hi(j):
                act.wait_ge(*r_ab.read(j, "c_k"))
                act.activation(flat(CD.k_hi), CD.qk[:, 1, :], ACT.Copy).then_inc(S["c_k_hi"].sem, 1)

            def c_q_hi(j):
                bank = r_early.bank("q")
                act.wait_ge(*r_early.full(j, "q"))
                for m in range(NC):
                    act.activation(q_hi[:, m, :], bank[:, m * 256:(m + 1) * 256], ACT.Identity,
                                   bias=bq4[:, m:m + 1]).then_inc(S["c_q_hi"].sem, 1)

            def c_mT(j):
                bank = r_cd.bank("max_T")
                act.wait_ge(*r_cd.full(j, "max_T"))
                act.activation(flat(m_T), bank[:].bitcast(BF16)[:, 0:GS * 2 * P], ACT.Copy).then_inc(r_cd.drained("max_T"), 1)

            def c_exp(j, p):
                bank = r_cd.bank(f"score{p}")
                act.wait_ge(*r_cd.full(j, f"score{p}"))
                if p == 0:
                    act.wait_ge(*S["c_kcols"].after(j))
                    if later(j):
                        act.wait_ge(*S["out_done"].after(j - 1))
                if p >= 2:
                    act.wait_ge(*S["c_pv"].after(j, p - 1))
                for s in range(GS):
                    ins = act.activation(flat(CD.p[:, p % 2, s]), bank[:, s * 256:(s + 1) * 256],
                                         ACT.Exp, bias=kcols[:, s, 1:2], scale=kcols[:, s, 0:1])
                ins.then_inc(r_cd.drained(f"score{p}"), 1)

            def d_th(j, i):
                bank = r_cd.bank(f"hidden{i}")
                act.wait_ge(*r_cd.full(j, f"hidden{i}"))
                act.activation(CD.t1[:, (i % 2) * 256:(i % 2) * 256 + 256], bank[:, 0:256], ACT.Tanh,
                               scale=0.5 / 127.0).then_inc(S["d_th"].sem, 1)

            def d_h_hi(j, i):
                act.wait_ge(*r_cd.read(j, f"hidden{i}"))
                if i >= 2:
                    act.wait_ge(*S["d_down"].after(j, i - 1))
                act.activation(flat(CD.qv_hi[:, i % 2, 0]), CD.t2[:, (i % 2) * 256:(i % 2) * 256 + 256],
                               ACT.Copy).then_inc(S["d_h_hi"].sem, 1)

            def d_weight_hi(k):
                hi, _lo, _src, place = d_parts[k]
                act.wait_ge(dw_ready, k + 1)
                act.activation(hi, place, ACT.Copy).then_inc(dw_hi_done, 1)

            def first_his(u):
                x_hi(r_ab, u, "x_T", AB.x_hi, "a_x_hi")
                ctx_hi(u)

            def body(u, j, i, n=None):
                ab, c, d = u is not None, j is not None, i is not None
                if d:
                    x_hi(r_cd, i, "x3_T", CD.x_hi, "d_x_hi")
                if ab:
                    a_qv_high(u)
                if ab:
                    a_k_hi(u)
                if d:
                    d_th(i, 0)
                    d_h_hi(i, 0)
                if ab:
                    values(u)
                if ab and not later(u):
                    for k in range(4):
                        d_weight_hi(k)
                if d:
                    for k in range(1, 3):
                        d_th(i, k)
                        d_h_hi(i, k)
                if c:
                    c_k_hi(j)
                    x_hi(r_early, j, "x_T", AB.y[:, 0], "c_x_hi")
                if d:
                    d_th(i, 3)
                    d_h_hi(i, 3)
                if c:
                    c_q_hi(j)
                if ab:
                    osb(AB, "a", u, 0)
                if ab and not later(u):
                    for k in range(4, ND):
                        d_weight_hi(k)
                if c:
                    plus_bias(r_early, j, "q", 0, bq4)
                if d:
                    d_th(i, 4)
                    d_h_hi(i, 4)
                if ab:
                    osb(AB, "a", u, 1)
                if d:
                    d_th(i, 5)
                    d_h_hi(i, 5)
                if ab:
                    a_o(u, 0)
                    a_o(u, 1)
                    a_sq(u, 0)
                    a_sq(u, 1)
                if c:
                    qv_high(j)
                    qv_low(j)
                if ab:
                    a_th(u)
                    plus_bias(r_ab, u, "c_k", 1, cols[:, COL["bk"]:COL["bk"] + 2])
                if c:
                    c_mT(j)
                for p in range(PAIRS):
                    if c:
                        c_exp(j, p)
                    if ab and p == 1:
                        y_hi(r_ab, u, AB, "a")
                    if ab and p == 5:
                        b_xs(u)
                    if c and p == 5:
                        osb(CD, "c", j, 0)
                if ab:
                    b_xk_hi(u)
                    b_xr_hi(u)
                if c:
                    osb(CD, "c", j, 1)
                if ab:
                    b_relu(u)
                    b_k2_hi(u)
                    b_th(u)
                if c:
                    y_hi(r_cd, j, CD, "c")
                if n is not None:
                    first_his(n)

            for i, n in enumerate(names):
                act.wait_ge(w_ready, i + 1)
                act.activation(flat(W[n][0]), wf[i % SLOTS], ACT.Copy).then_inc(w_hi_done, 1)
            act.wait_ge(load, 16 * NLOAD)
            act.wait_ge(mask_T, 1)
            for i in range(2):
                act.activation(key_tab[:, :, i], AB.ring[0][:, i * SEQ:(i + 1) * SEQ], ACT.Copy).then_inc(act_const, 1)
            act.activation(bq4[:], cols[:, COL["bq"]:COL["bq"] + 2], ACT.Copy, scale=0.25).then_inc(act_const, 1)
            act.wait_ge(act_const, NACT_CONST)
            first_his(0)
            act.wait_ge(v_zero, 1)
            body(0, None, None, 1)
            act.wait_ge(dw_lo_done, ND)
            body(1, 0, None, 2)
            with act.Fori(2, NG - 1) as u:
                body(u, u - 1, u - 2, u + 1)
            body(NG - 1, NG - 2, NG - 3)
            body(None, NG - 1, NG - 2)
            body(None, None, NG - 1)

        @block.vector
        def _(dve):
            def stats(nm, it, n, x):
                for s in range(GS):
                    dve.bn_stats(nm.stats[:, s, :], x[:, s, :]).then_inc(S[n + "_stats"].sem, 1)
                for s in range(GS):
                    dve.wait_ge(*S[n + "_stats"].after(it, s + 1))
                    apart(dve)
                    dve.bn_aggr(nm.mv[:, s, :], nm.stats[:, s, :]).then_inc(S[n + "_aggr"].sem, 1)

            def low(ring, it, item, sig, lo, hi):
                bank = ring.bank(item)
                dve.wait_ge(*ring.full(it, item))
                dve.wait_ge(*S[sig].after(it))
                dve.tensor_tensor(lo, bank[:], raw(hi), ALU.subtract).then_inc(ring.drained(item), 1)

            def table(i):
                return rope[:, i:i + 1, :].broadcast_to([P, 2 * GS, P])

            def rows(x):
                return x.rearrange("p (a t) -> p a t", t=P)

            def a_gate(u):
                bank = r_ab.bank("gate")
                dve.wait_ge(*r_ab.full(u, "gate"))
                dve.tensor_tensor(AB.t2[:].rearrange("p (s n) -> p s n", s=GS), bank[:].rearrange("p (s n) -> p s n", s=GS),
                                             bias[:, 0:1, :].broadcast_to([P, GS, D]), ALU.add).then_inc(r_ab.drained("gate"), 1)

            def a_sg(u):
                dve.wait_ge(*S["a_th"].after(u))
                dve.scalar_tensor_tensor(flat(sg), flat(AB.p[:, 1]), 1.0, AB.t2[:], ALU.add, ALU.mult).then_inc(S["a_sg"].sem, 1)

            def a_rotate(u, i):
                item = ("q", "q_rot", "k", "k_rot")[i]
                bank = r_ab.bank(item)
                dve.wait_ge(*r_ab.full(u, item))
                dve.tensor_tensor(rows(products[i]), rows(bank[:]), table(i), ALU.mult).then_inc(r_ab.drained(item), 1)

            def a_qv_low(u):
                for par in range(2):
                    dve.wait_ge(*S["a_qv_hi"].after(u, par + 1))
                    dve.scalar_tensor_tensor(AB.qv_lo[:].rearrange("p c s a t -> p (c s) a t")[:, :, par, :],
                                             rows(AB.qk[:, 0, :]), cols[:, COL["even"] + par:COL["even"] + par + 1],
                                             raw(AB.qv_hi[:]).rearrange("p c s a t -> p (c s) a t")[:, :, par, :],
                                             ALU.mult, ALU.subtract).then_inc(S["a_qv_lo"].sem, 1)

            def c_values(u):
                bank = r_ab.bank("c_v")
                dve.wait_ge(*r_ab.full(u, "c_v"))
                if later(u):
                    dve.wait_ge(*S["c_pv"].after(u - 1))
                dve.tensor_tensor(CD.v[:, :, :, 0:HD], bank[:].rearrange("p (s h e) -> p s h e", s=GS, e=HD),
                                             bias[:, 2:3, :].rearrange("p o (h e) -> p o h e", e=HD).broadcast_to([P, GS, H, HD]),
                                             ALU.add).then_inc(r_ab.drained("c_v"), 1)

            def k_low(ch, it, n):
                dve.wait_ge(*S[n + "_k_hi"].after(it))
                dve.tensor_tensor(flat(ch.k_lo), ch.qk[:, 1, :], raw(flat(ch.k_hi)), ALU.subtract).then_inc(S[n + "_k_lo"].sem, 1)

            def a_decay(u, p):
                bank = r_ab.bank(f"score{p}")
                dve.wait_ge(*r_ab.full(u, f"score{p}"))
                if p >= 2:
                    dve.wait_ge(*S["a_pv"].after(u, p - 1))
                dve.tensor_tensor(AB.p[:, p % 2].rearrange("k s a q -> k s (a q)"),
                                             bank[:].rearrange("k (s n) -> k s n", s=GS),
                                             decay[:, 2 * p:2 * p + 2, :].rearrange("k (o a) q -> k o (a q)", o=1).broadcast_to([P, GS, 2 * P]),
                                             ALU.mult).then_inc(r_ab.drained(f"score{p}"), 1)

            def heads(bank):
                return bank[:].rearrange("p (h e) -> p h e", e=HP)[:, :, 0:HD]

            def a_ssq(u, s):
                dve.wait_ge(*S["a_sq"].after(u, s + 1))
                dve.tensor_reduce(ssq[:, s, :], flat(AB.p[:, 1])[:, s * D:(s + 1) * D].rearrange("p (h e) -> p h e", e=HD),
                                  AX_X, ALU.add).then_inc(S["a_ssq"].sem, 1)

            def a_y(u, s):
                dve.wait_ge(*r_ab.read(u, f"o_T{s}"))
                dve.wait_ge(*S["a_grstd"].after(u))
                dve.tensor_tensor(flat(AB.p[:, 0])[:, s * D:(s + 1) * D].rearrange("p (h e) -> p h e", e=HD),
                                  AB.t1[:, s * D:(s + 1) * D].rearrange("p (h e) -> p h e", e=HD),
                                  gn_rstd[:, s, :].rearrange("p (h o) -> p h o", o=1).broadcast_to([P, H, HD]),
                                  ALU.mult).then_inc(S["a_y"].sem, 1)

            def a_yg(u, s):
                dve.wait_ge(*S["a_y"].after(u, s + 1))
                dve.wait_ge(*S["a_sg"].after(u))
                dve.tensor_tensor(AB.t2[:, s * D:(s + 1) * D], flat(AB.p[:, 0])[:, s * D:(s + 1) * D], sg[:, s, :],
                                  ALU.mult).then_inc(S["a_yg"].sem, 1)

            def residual(ring, it, ch, n):
                bank = ring.bank("out")
                dve.wait_ge(*ring.full(it, "out"))
                dve.wait_ge(*S[n + "_xb"].after(it))
                dve.tensor_tensor(flat(ch.xb), bank[:], flat(ch.xb), ALU.add).then_inc(ring.drained("out"), 1)

            def b_shift(u):
                dve.wait_ge(*r_ab.read(u, "x1_T"))
                now = xs[:, :, :, 1:P + 1].rearrange("p c s t -> p (c s) t")
                before = xs[:, :, :, 0:P].rearrange("p c s t -> p (c s) t")
                dve.tensor_tensor(rows(AB.t1[:]), now, before, ALU.subtract).then_inc(S["b_d"].sem, 1)
                dve.wait_ge(*S["b_d"].after(u))
                for dst, mu, sig in ((AB.qk[:, 0, :], "mu_k", "b_xk"), (AB.t2[:], "mu_r", "b_xr")):
                    for c in range(NC):
                        dve.scalar_tensor_tensor(rows(dst)[:, GS * c:GS * c + GS, :], rows(AB.t1[:])[:, GS * c:GS * c + GS, :],
                                                 cols[:, COL[mu] + c:COL[mu] + c + 1], xs[:, c, :, 0:P],
                                                 ALU.mult, ALU.add).then_inc(S[sig].sem, 1)

            def b_xk_lo(u):
                dve.wait_ge(*S["b_xk_hi"].after(u))
                dve.tensor_tensor(flat(AB.k_lo), AB.qk[:, 0, :], raw(flat(AB.k_hi)), ALU.subtract).then_inc(S["b_xk_lo"].sem, 1)

            def b_xr_lo(u):
                dve.wait_ge(*S["b_xr_hi"].after(u))
                dve.tensor_tensor(flat(AB.x_lo), AB.t2[:], raw(flat(AB.x_hi)), ALU.subtract).then_inc(S["b_xr_lo"].sem, 1)

            def b_k2(u):
                bank = r_ab.bank("key")
                dve.wait_ge(*r_ab.full(u, "key"))
                dve.wait_ge(*S["b_relu"].after(u))
                dve.tensor_tensor(AB.t1[:], bank[:], AB.qk[:, 1, :], ALU.mult).then_inc(r_ab.drained("key"), 1)

            def b_k2_lo(u):
                dve.wait_ge(*S["b_k2_hi"].after(u))
                dve.tensor_tensor(flat(AB.y[:, 1]), AB.t1[:], raw(flat(AB.y[:, 0])), ALU.subtract).then_inc(S["b_k2_lo"].sem, 1)

            def b_mixed(u):
                bank = r_ab.bank("mix")
                dve.wait_ge(*r_ab.full(u, "mix"))
                dve.wait_ge(*r_ab.read(u, "recept"))
                dve.scalar_tensor_tensor(flat(AB.p[:, 0]), AB.t2[:], 1.0, bank[:], ALU.add, ALU.mult).then_inc(r_ab.drained("mix"), 1)

            def b_x2(u):
                dve.wait_ge(*r_ab.read(u, "mix"))
                if later(u):
                    dve.wait_ge(*S["c_xb"].after(u - 1))
                    dve.wait_ge(*S["c_xhat"].after(u - 1))
                dve.tensor_tensor(flat(x2), flat(AB.xb), flat(AB.p[:, 0]), ALU.add).then_inc(S["b_x2"].sem, 1)

            def c_masks(j):
                dve.wait_ge(*S["mask_in"].after(j))
                dve.tensor_scalar(mask_add[:], mask_row[:], 0.0, NEG, ALU.is_equal, ALU.mult).then_inc(S["c_mask"].sem, 1)
                dve.tensor_copy(kcols[:], key_tab[:, seqs(j), :]).then_inc(S["c_kcols"].sem, 1)

            def c_kv(j):
                dve.wait_ge(*r_ab.read(j, "c_k"))
                for par in range(2):
                    dve.tensor_scalar(flat(CD.y[:, par]), CD.qk[:, 1, :], cols[:, COL["even"] + par:COL["even"] + par + 1],
                                      None, ALU.mult).then_inc(S["c_kv"].sem, 1)

            def c_max(j, p):
                bank = r_early.bank(f"rough{p}")
                dve.wait_ge(*r_early.full(j, f"rough{p}"))
                dve.tensor_reduce(mx[:, p, :, :].rearrange("q s a -> q (s a)"),
                                             bank[:].rearrange("q (a k) -> q a k", k=P), AX_X, ALU.max).then_inc(r_early.drained(f"rough{p}"), 1)

            def c_parts(j):
                dve.wait_ge(*r_early.read(j, f"rough{PAIRS - 1}"))
                parts_ = mx_parts[:].rearrange("q s a g r -> q (s a) g r")
                for c in range(NC):
                    m = mx[:, 4 * c:4 * c + 4, :, :].rearrange("q g s a -> q (s a) g")
                    dve.tensor_copy(parts_[:, :, :, c], m).then_inc(S["c_part0"].sem, 1)
                for c in range(NC):
                    m = mx[:, 4 * c:4 * c + 4, :, :].rearrange("q g s a -> q (s a) g")
                    dve.wait_ge(*S["c_part0"].after(j, c + 1))
                    dve.tensor_tensor(parts_[:, :, :, NC + c], m, parts_[:, :, :, c], ALU.subtract).then_inc(S["c_part1"].sem, 1)

            def c_y(j, s):
                bank = r_cd.bank(f"o_T{s}")
                dve.wait_ge(*r_cd.full(j, f"o_T{s}"))
                dve.reciprocal(rz[:, s, :].rearrange("p (h o) -> p h o", o=1),
                               bank[:].rearrange("p (h e) -> p h e", e=HP)[:, :, HD:HD + 1]).then_inc(S["c_rz"].sem, 1)
                dve.wait_ge(*S["c_rz"].after(j, s + 1))
                dve.tensor_tensor(CD.t1[:, s * D:(s + 1) * D].rearrange("p (h e) -> p h e", e=HD), heads(bank),
                                             rz[:, s, :].rearrange("p (h o) -> p h o", o=1).broadcast_to([P, H, HD]), ALU.mult).then_inc(r_cd.drained(f"o_T{s}"), 1)

            def d_h(j, i):
                bank = r_cd.bank(f"hidden{i}")
                dve.wait_ge(*r_cd.full(j, f"hidden{i}"))
                half_ = slice((i % 2) * 256, (i % 2) * 256 + 256)
                dve.wait_ge(*S["d_th"].after(j, i + 1))
                dve.scalar_tensor_tensor(CD.t1[:, half_], CD.t1[:, half_], 1.0, bank[:, 0:256], ALU.add, ALU.mult).then_inc(S["d_a"].sem, 1)
                dve.wait_ge(*S["d_a"].after(j, i + 1))
                if i >= 2:
                    dve.wait_ge(*S["d_h_lo"].after(j, i - 1))
                dve.tensor_tensor(CD.t2[:, half_], bank[:, 256:512], CD.t1[:, half_], ALU.mult).then_inc(r_cd.drained(f"hidden{i}"), 1)

            def d_x4(j):
                dve.wait_ge(*S["d_down"].after(j))
                if later(j):
                    dve.wait_ge(*S["out_done"].after(j - 1))
                dve.scalar_tensor_tensor(xo.rearrange("p s n -> p (s n)"), CD.o[:, 0:2, :, :].rearrange("p a b c -> p (a b c)"), 0.5 / 127.0 ** 3,
                                         flat(CD.xb), ALU.mult, ALU.add).then_inc(S["d_x4"].sem, 1)

            def d_weight(k):
                place = d_parts[k][3]
                dve.tensor_copy(place, place.bitcast(I32)).then_inc(dw_ready, 1)

            def first_stats(u):
                dve.wait_ge(*S["x_in"].after(u))
                stats(A0, u, "a", xin)

            def body(u, j, i, n=None):
                ab, c, d = u is not None, j is not None, i is not None
                if d:
                    residual(r_cd, i, CD, "c")
                if ab:
                    a_rotate(u, 0)
                if d:
                    dve.wait_ge(*r_cd.read(i, "out"))
                    stats(CD.norm, i, "d", CD.xb)
                if ab:
                    for k in range(1, 4):
                        a_rotate(u, k)
                if d:
                    low(r_cd, i, "x3_T", "d_x_hi", flat(CD.x_lo), flat(CD.x_hi))
                if ab:
                    a_qv_low(u)
                    k_low(AB, u, "a")
                if d:
                    d_h(i, 0)
                if c:
                    dve.wait_ge(*S["b_x2"].after(j))
                    stats(CD.norm, j, "c", x2)
                if d:
                    d_h(i, 1)
                for p in range(PAIRS):
                    if ab and not later(u):
                        if p == 0:
                            dve.wait_ge(dw_staged[0], 16 * NPLACES)
                        if p < NPLACES:
                            d_weight(p)
                    if ab:
                        a_decay(u, p)
                    if d and p == 0:
                        d_h(i, 2)
                    if c and p == 1:
                        c_masks(j)
                        low(r_early, j, "x_T", "c_x_hi", flat(AB.y[:, 1]), flat(AB.y[:, 0]))
                    if d and p == 2:
                        d_h(i, 3)
                    if c and p == 2:
                        c_kv(j)
                    if c and p == 3:
                        k_low(CD, j, "c")
                    if d and p == 4:
                        d_h(i, 4)
                    if c and p >= 4:
                        c_max(j, p - 4)
                if ab and not later(u):
                    dve.wait_ge(dw_staged[1], 16 * (ND - NPLACES))
                    for k in range(NPLACES, ND):
                        d_weight(k)
                if d:
                    d_h(i, 5)
                if c:
                    c_max(j, 4)
                    c_max(j, 5)
                if ab:
                    a_ssq(u, 0)
                    a_ssq(u, 1)
                if c:
                    c_max(j, 6)
                if d:
                    d_x4(i)
                if ab:
                    a_gate(u)
                if c:
                    c_max(j, 7)
                    c_parts(j)
                if ab:
                    a_sg(u)
                    a_y(u, 0)
                    a_y(u, 1)
                    a_yg(u, 0)
                    a_yg(u, 1)
                if ab:
                    low(r_ab, u, "y_T", "a_y_hi", flat(AB.y[:, 1]), flat(AB.y[:, 0]))
                    residual(r_ab, u, AB, "a")
                    dve.wait_ge(*r_ab.read(u, "out"))
                    stats(AB.norm, u, "b", AB.xb)
                if n is not None:
                    first_stats(n)
                if ab:
                    b_shift(u)
                    b_xk_lo(u)
                    c_values(u)
                    b_xr_lo(u)
                if ab:
                    b_k2(u)
                if c:
                    c_y(j, 0)
                if ab:
                    b_k2_lo(u)
                if c:
                    c_y(j, 1)
                if ab:
                    b_mixed(u)
                if c:
                    low(r_cd, j, "y_T", "c_y_hi", flat(CD.y[:, 1]), flat(CD.y[:, 0]))
                if n is not None:
                    low(r_ab, n, "x_T", "a_x_hi", flat(AB.x_lo), flat(AB.x_hi))
                if ab:
                    b_x2(u)
                if n is not None:
                    low(r_ab, n, "ctx_T", "a_c_hi", flat(c_lo), flat(c_hi))

            dve.memset(half[:], -0.5).then_inc(dve_const, 1)
            dve.memset(one_half[:], 1.5).then_inc(dve_const, 1)
            dve.memset(CD.v[:], 0.0).then_inc(dve_const, 1)
            dve.wait_ge(dve_const, 3)
            dve.memset(CD.v[:, :, :, HD:HD + 1], 1.0).then_inc(dve_const, 1)
            dve.memset(xs[:, :, :, 0:1], 0.0).then_inc(dve_const, 1)
            dve.memset(mask_row[:], 1).then_inc(dve_const, 1)
            dve.memset(mx_parts[:], 0.0).then_inc(dve_const, 1)

            def weight(i):
                dve.wait_ge(w_staged[i % SLOTS], 16 * (i // SLOTS + 1))
                if i >= SLOTS:
                    dve.wait_ge(w_lo_done[i % 2], (i - SLOTS) // 2 + 1)
                n, src, dst = names[i], stage[i % SLOTS], wf[i % SLOTS]
                if n == "a_v":
                    per_head = src.rearrange("p (h e) -> p h e", e=HD)
                    dve.tensor_reduce(head_mean[:, :], per_head, AX_X, ALU.add).then_inc(w_centred, 1)
                    dve.wait_ge(w_centred, 1)
                    dve.tensor_scalar(head_mean[:], head_mean[:], 1.0 / HD, None, ALU.mult).then_inc(w_centred, 1)
                    dve.wait_ge(w_centred, 2)
                    dve.tensor_tensor(dst.rearrange("p (h e) -> p h e", e=HD), per_head,
                                      head_mean[:].rearrange("p (h o) -> p h o", o=1).broadcast_to([P, NC * H, HD]),
                                      ALU.subtract).then_inc(w_ready, 1)
                else:
                    dve.tensor_scalar(dst, src, SCALES.get(n, 1.0), None, ALU.mult).then_inc(w_ready, 1)

            def weight_lo(i):
                hi, lo = W[names[i]]
                dve.wait_ge(w_hi_done, i + 1)
                dve.tensor_tensor(flat(lo), wf[i % SLOTS], raw(flat(hi)), ALU.subtract).then_inc(w_lo_done[1], 1)

            for i in range(SLOTS):
                weight(i)
            weight_lo(1)
            for i in range(SLOTS, NW):
                weight(i)
                if i % 2:
                    weight_lo(i - 2)
                if i == 2 * SLOTS - 1:
                    first_stats(0)
            weight_lo(NW - 1)
            dve.wait_ge(w_lo_done[0], NW // 2)
            dve.wait_ge(w_lo_done[1], NW // 2)
            dve.memset(AB.v[:], 0.0).then_inc(v_zero, 1)
            dve.wait_ge(load, 16 * NLOAD)
            dve.tensor_copy(ident_bf[:], ident[:]).then_inc(dve_const, 1)
            dve.tensor_copy(flat(sel)[:, 0:PAIRS * P], flat(AB.p)[:, 0:PAIRS * P]).then_inc(dve_const, 1)
            dve.tensor_copy(sel[:, PAIRS, :], CD.t2[:, 0:P]).then_inc(dve_const, 1)
            dve.wait_ge(dve_const, NDVE_CONST)
            m01, add = CD.t2[0:SEQ, 0:P], CD.t2[0:SEQ, P:2 * P]
            dve.tensor_scalar(m01, CD.t1[0:SEQ, 0:P].bitcast(I32), 0.0, None, ALU.not_equal).then_inc(mask_prep, 1)
            dve.wait_ge(mask_prep, 1)
            dve.tensor_reduce(any_key[:], m01, AX_X, ALU.max).then_inc(mask_prep, 1)
            dve.wait_ge(mask_prep, 2)
            dve.tensor_scalar(add, m01, -1.0, any_key[:, 0:1], ALU.add, ALU.mult).then_inc(mask_prep, 1)
            dve.wait_ge(mask_prep, 3)
            dve.tensor_scalar(add, add, -NEG, None, ALU.mult).then_inc(mask_prep, 1)
            dve.wait_ge(act_const, NACT_CONST)
            low(r_ab, 0, "x_T", "a_x_hi", flat(AB.x_lo), flat(AB.x_hi))
            low(r_ab, 0, "ctx_T", "a_c_hi", flat(c_lo), flat(c_hi))
            dve.wait_ge(decay_in, 16)
            body(0, None, None, 1)
            dve.wait_ge(dw_lo_done, ND)
            body(1, 0, None, 2)
            with dve.Fori(2, NG - 1) as u:
                body(u, u - 1, u - 2, u + 1)
            body(NG - 1, NG - 2, NG - 3)
            body(None, NG - 1, NG - 2)
            body(None, None, NG - 1)

        @block.gpsimd
        def _(pool):
            def norm(nm, it, n, x, dst):
                pool.wait_ge(*S[n + "_aggr"].after(it))
                apart(pool)
                pool.tensor_scalar(nm.negmean[:], nm.mv[:, :, 0], -1.0, 1.0, ALU.mult, ALU.mult).then_inc(S[n + "_small"].sem, 1)
                pool.tensor_scalar(nm.vareps[:], nm.mv[:, :, 1], EPS, 1.0, ALU.add, ALU.mult).then_inc(S[n + "_small"].sem, 1)
                pool.wait_ge(*S[n + "_small"].after(it))
                pool.tensor_tensor(nm.rstd[:], nm.vareps[:], half[:, 0:GS], ALU.pow).then_inc(S[n + "_rstd"].sem, 1)
                pool.wait_ge(*S[n + "_rstd"].after(it))
                apart(pool)
                for s in range(GS):
                    pool.tensor_scalar(dst[:, s * D:(s + 1) * D], x[:, s, :], nm.negmean[:, s:s + 1], nm.rstd[:, s:s + 1],
                                       ALU.add, ALU.mult).then_inc(S[n + "_xhat"].sem, 1)

            def bias_rows(i):
                return bias[:, i:i + 1, :].broadcast_to([P, GS, D])

            def a_xb(u):
                pool.tensor_tensor(AB.xb[:], xin[:], bias_rows(1), ALU.add).then_inc(S["a_xb"].sem, 1)

            def c_xb(j):
                if later(j):
                    pool.wait_ge(*S["d_x4"].after(j - 1))
                pool.tensor_tensor(CD.xb[:], x2[:], bias_rows(3), ALU.add).then_inc(S["c_xb"].sem, 1)

            def a_rotated(u, i):
                pool.wait_ge(*r_ab.read(u, ("q_rot", "k_rot")[i]))
                pool.wait_ge(*r_ab.read(u, ("q", "k")[i]))
                pool.tensor_tensor(AB.qk[:, i, :], products[2 * i], products[2 * i + 1], ALU.add).then_inc(S["a_qk"].sem, 1)

            def c_q_lo(j):
                pool.wait_ge(*S["c_q_hi"].after(j))
                pool.wait_ge(*r_early.read(j, "q"))
                pool.tensor_tensor(CD.qk[:, 0, :], CD.qk[:, 0, :], raw(flat(q_hi)), ALU.subtract).then_inc(S["c_q_lo"].sem, 1)

            def a_gn(u):
                pool.wait_ge(*S["a_ssq"].after(u))
                apart(pool)
                pool.tensor_scalar(gn_var[:], ssq[:], 1.0 / HD, EPS, ALU.mult, ALU.add).then_inc(S["a_gvar"].sem, 1)
                pool.tensor_scalar(gn_neg_half[:], ssq[:], -0.5 / HD, -0.5 * EPS, ALU.mult, ALU.add).then_inc(S["a_ghalf"].sem, 1)
                pool.wait_ge(*S["a_gvar"].after(u))
                apart(pool)
                pool.tensor_scalar(gn_rstd[:].bitcast(I32), gn_var[:].bitcast(I32), -0.5, float(0x5F3759DF), ALU.mult, ALU.add).then_inc(S["a_grstd"].sem, 1)
                pool.wait_ge(*S["a_ghalf"].after(u))
                for k in range(NEWTON):
                    pool.wait_ge(*S["a_grstd"].after(u, k + 1))
                    pool.tensor_tensor(gn_sq[:], gn_rstd[:], gn_rstd[:], ALU.mult).then_inc(S["a_gsq"].sem, 1)
                    pool.wait_ge(*S["a_gsq"].after(u, k + 1))
                    pool.tensor_tensor(gn_var[:], gn_sq[:], gn_neg_half[:], ALU.mult).then_inc(S["a_gprod"].sem, 1)
                    pool.wait_ge(*S["a_gprod"].after(u, k + 1))
                    pool.tensor_tensor(gn_sq[:], gn_var[:], one_half[:], ALU.add).then_inc(S["a_gsum"].sem, 1)
                    pool.wait_ge(*S["a_gsum"].after(u, k + 1))
                    pool.tensor_tensor(gn_rstd[:], gn_sq[:], gn_rstd[:], ALU.mult).then_inc(S["a_grstd"].sem, 1)

            def d_h_lo(j, i):
                pool.wait_ge(*S["d_h_hi"].after(j, i + 1))
                half_ = slice((i % 2) * 256, (i % 2) * 256 + 256)
                pool.tensor_tensor(flat(CD.qv_lo[:, i % 2, 0]), CD.t2[:, half_], raw(flat(CD.qv_hi[:, i % 2, 0])),
                                   ALU.subtract).then_inc(S["d_h_lo"].sem, 1)

            def d_weight_lo(k):
                hi, lo, _src, place = d_parts[k]
                pool.wait_ge(dw_hi_done, k + 1)
                pool.tensor_tensor(lo, place, raw(hi), ALU.subtract).then_inc(dw_lo_done, 1)

            def body(u, j, i, n=None):
                ab, c, d = u is not None, j is not None, i is not None
                if d:
                    norm(CD.norm, i, "d", CD.xb, CD.t1[:])
                if ab:
                    a_rotated(u, 0)
                    a_rotated(u, 1)
                if ab and not later(u):
                    for k in range(ND):
                        d_weight_lo(k)
                if d:
                    d_h_lo(i, 0)
                if c:
                    norm(CD.norm, j, "c", x2, CD.qk[:, 0, :])
                if d:
                    d_h_lo(i, 1)
                    d_h_lo(i, 2)
                if ab:
                    a_xb(u)
                if d:
                    d_h_lo(i, 3)
                if c:
                    c_q_lo(j)
                if d:
                    d_h_lo(i, 4)
                    d_h_lo(i, 5)
                if ab:
                    a_gn(u)
                if c:
                    c_xb(j)
                if ab:
                    norm(AB.norm, u, "b", AB.xb, AB.t1[:])
                if n is not None:
                    norm(A0, n, "a", xin, flat(sg))

            for i in range(0, NW, 2):
                hi, lo = W[names[i]]
                pool.wait_ge(w_hi_done, i + 1)
                pool.tensor_tensor(flat(lo), wf[i % SLOTS], raw(flat(hi)), ALU.subtract).then_inc(w_lo_done[0], 1)
                if i + 2 == 2 * SLOTS:
                    pool.wait_ge(dve_const, 3)
                    norm(A0, 0, "a", xin, flat(sg))
            pool.wait_ge(dve_const, NDVE_CONST)
            pool.wait_ge(load, 16 * NLOAD)
            body(0, None, None, 1)
            body(1, 0, None, 2)
            with pool.Fori(2, NG - 1) as u:
                body(u, u - 1, u - 2, u + 1)
            body(NG - 1, NG - 2, NG - 3)
            body(None, NG - 1, NG - 2)
            body(None, None, NG - 1)


def constants():
    import numpy as np
    f = np.float32
    half_ = HD // 2
    base = (np.arange(0, HD, 2, dtype=f) + f(0.4 * HD)) / f(1.4 * HD)
    power = (np.arange(-(P // 2), P - P // 2, dtype=f) / f(512.0))[:, None]
    scale = (base[None, :] ** power).astype(f)
    inv_freq = (f(1.0) / f(10000.0) ** (np.arange(half_, dtype=f) / f(half_))).astype(f)
    ang = (np.arange(P, dtype=f)[:, None] * inv_freq[None, :]).astype(f)
    sin, cos = np.sin(ang).astype(f), np.cos(ang).astype(f)
    sign = np.where(np.arange(HD) % 2 == 0, f(-1), f(1))
    rope = np.zeros((P, 4, P), f)
    for i, sc in enumerate((scale, (f(1.0) / scale).astype(f))):
        c = np.repeat(cos * sc, 2, axis=1)
        s = np.repeat(sin * sc, 2, axis=1) * sign
        rope[:, 2 * i, :] = np.tile(c.T, (P // HD, 1))
        rope[:, 2 * i + 1, :] = np.tile(s.T, (P // HD, 1))
    gamma = f(1.0) - np.exp(np.linspace(np.log(1.0 / 32.0), np.log(1.0 / 512.0), H).astype(f)).astype(f)
    dist = np.arange(P)[None, :] - np.arange(P)[:, None]
    decay = np.where(dist[:, None, :] >= 0, gamma[None, :, None] ** np.maximum(dist, 0)[:, None, :].astype(f), f(0)).astype(f)
    parity = np.zeros((P, 2), f)
    parity[np.arange(P) // HD % 2 == 0, 0] = 1
    parity[np.arange(P) // HD % 2 == 1, 1] = 1
    sel = np.zeros((P, PAIRS + 1, P), f)
    for p in range(PAIRS):
        row = 32 * (p % 4) + p // 4
        sel[row, p] = sel[row + NC, p] = -1
    sel[0, PAIRS] = 1
    return {"rope": rope, "decay": decay, "ident": np.eye(P, dtype=f), "parity": parity, "sel": sel.reshape(P, -1)}


def kernel(**inputs):
    import numpy as np
    import concourse.bacc as bacc
    from concourse.bass_utils import run_bass_kernel_spmd

    def heads_out(w):
        return np.ascontiguousarray(np.transpose(w, (1, 0, 2)).reshape(D, D))

    def swap_pairs(w):
        return np.ascontiguousarray(w.reshape(D, D // 2, 2)[:, :, ::-1].reshape(D, D))

    def turned(w):
        return np.ascontiguousarray(np.transpose(w))

    i = {k: np.asarray(v) for k, v in inputs.items()}
    tables = constants()
    arrays = {
        "x": i["x"], "ctx": i["ctx_1024"], "mask": i["mask_Bx1x1xS2_if1"],
        "a_q": heads_out(i["L0_xattn_W_Q"]), "a_q_rot": swap_pairs(heads_out(i["L0_xattn_W_Q"])),
        "a_k": heads_out(i["L0_xattn_W_K"]), "a_k_rot": swap_pairs(heads_out(i["L0_xattn_W_K"])),
        "a_v": heads_out(i["L0_xattn_W_V"]), "a_gate": turned(i["L0_xattn_g_w"]), "a_out": turned(i["L0_xattn_out_w"]),
        "bias": np.stack([i["L0_xattn_g_b"], i["L0_xattn_out_b"], i["L1_xattn_bv"], i["L1_xattn_bo"]]),
        "b_r": turned(i["L0_ffn_W_r"]), "b_k": turned(i["L0_ffn_W_k"]), "b_v": turned(i["L0_ffn_W_v"]),
        "c_q": turned(i["L1_xattn_Wq"]), "c_k": turned(i["L1_xattn_Wk"]), "c_v": turned(i["L1_xattn_Wv"]),
        "c_out": turned(i["L1_xattn_Wo"]),
        "cols": np.concatenate([turned(np.reshape(i[n], (NC, P))) for n in ("L0_ffn_mu_r", "L0_ffn_mu_k", "L1_xattn_bq", "L1_xattn_bk")]
                               + [tables.pop("parity")], axis=1),
        "d_gate": turned(i["L1_ffn_w_gate"]), "d_up": turned(i["L1_ffn_w_up"]), "d_down": turned(i["L1_ffn_w_down"]),
        **tables,
    }
    nc = bacc.Bacc("TRN2", target_bir_lowering=False, num_devices=1)
    io = {n: nc.dram_tensor(f"in_{n}", a.shape, mybir.dt.from_np(a.dtype), kind="ExternalInput").ap() for n, a in arrays.items()}
    io["out"] = nc.dram_tensor("out_x", (SEQ, P, D), F32, kind="ExternalOutput").ap()
    build(nc, io)
    r = run_bass_kernel_spmd(nc, [{f"in_{n}": a for n, a in arrays.items()}], core_ids=[0])
    return r.results[0]["out_x"]
```
